# Optimizing a Trainium2 kernel written in Bass

```python
import numpy as np
import jax
import jax.numpy as jnp

def _softmax(x, axis=-1):
    return jax.nn.softmax(x, axis=axis)

def _gelu(x):
    return jax.nn.gelu(x, approximate=True)

def _silu(x):
    return jax.nn.silu(x)

def _sigmoid(x):
    return jax.nn.sigmoid(x)

def _layernorm(x, axis=-1, eps=1e-05):
    m = jnp.mean(x, axis=axis, keepdims=True)
    v = jnp.var(x, axis=axis, keepdims=True)
    return (x - m) / jnp.sqrt(v + eps)

def _scatter_add(tgt, idx, src, axis=0):
    return tgt.at[idx].add(src)

def _segment_sum(src, seg, n):
    return jax.ops.segment_sum(src, seg, n)
kernel_name = 'mk_decoder_postln_d1_seqx_r8_cb9560'

def setup_inputs(seed: int=0):
    np.random.seed(seed)
    _w = jnp.asarray

    def _rec_inputs():
        import jax
        import jax.numpy as jnp
        _rk = jax.random.key(seed)
        x = -0.0003929 + 0.9999 * jax.random.normal(jax.random.fold_in(_rk, 1), (32, 56, 256), jnp.float32)
        _lenS = 56 - jax.random.randint(jax.random.fold_in(_rk, 7), (32,), 0, max(1, 56 // 4) + 1, jnp.int32)
        _lenS2 = 1500 - jax.random.randint(jax.random.fold_in(_rk, 8), (32,), 0, max(1, 1500 // 4) + 1, jnp.int32)
        _ctx_1024P = jax.random.normal(jax.random.fold_in(_rk, 11), (32, 16, 128), jnp.float32)
        _ctx_1024c = jax.random.dirichlet(jax.random.fold_in(_rk, 511), 0.3 * jnp.ones((16,), jnp.float32), (32, 1500))
        _ctx_1024t = jnp.einsum('bsk,bkd->bsd', _ctx_1024c, _ctx_1024P)
        _ctx_1024t = _ctx_1024t * jax.lax.rsqrt(jnp.mean(jnp.square(_ctx_1024t)) + 1e-12) * 0.953939
        ctx_1024 = -0.000494167 + 1.00018 * (_ctx_1024t + 0.3 * jax.random.normal(jax.random.fold_in(_rk, 611), (32, 1500, 128), jnp.float32))
        _validS = jnp.arange(56)[None, :] < _lenS[:, None]
        _validS2 = jnp.arange(1500)[None, :] < _lenS2[:, None]
        _causal = jnp.tril(jnp.ones((56, 56), dtype=bool))
        mask_BxS2_bf1 = jnp.ones((32, 1500), dtype=bool)
        return (x, ctx_1024, mask_BxS2_bf1)
    x, ctx_1024, mask_BxS2_bf1 = _rec_inputs()

    def _L0_attn_setup():
        import jax, jax.numpy as jnp
        import numpy as np
        IN_FEATURES = 256
        HEAD_NUM = 64
        D = IN_FEATURES // HEAD_NUM
        SCALE = float(np.sqrt(D))
        key = jax.random.key(seed)
        ks = jax.random.split(key, 9)
        F = IN_FEATURES
        x = jax.random.normal(ks[0], (4, 128, F), dtype=jnp.float32)
        w = lambda k: jax.random.normal(k, (F, F), dtype=jnp.float32) * 0.02
        b = lambda k: jax.random.normal(k, (F,), dtype=jnp.float32) * 0.01
        return {'x': x, 'Wq': w(ks[1]), 'bq': b(ks[2]), 'Wk': w(ks[3]), 'bk': b(ks[4]), 'Wv': w(ks[5]), 'bv': b(ks[6]), 'Wo': w(ks[7]), 'bo': b(ks[8])}
    _L0_attn_all = _L0_attn_setup()
    _L0_attn_in = {k: v for k, v in _L0_attn_all.items() if k in ('Wq', 'bq', 'Wk', 'bk', 'Wv', 'bv', 'Wo', 'bo')}
    del _L0_attn_all

    def _L0_xattn_setup():
        import jax, jax.numpy as jnp
        import numpy as np
        N_HEADS = 16
        N_KV_HEADS = 8
        HEAD_DIM = 128
        D_TEXT = 256
        D_VISION = 128
        GROUPS = N_HEADS // N_KV_HEADS
        key = jax.random.key(seed)
        ks = jax.random.split(key, 6)
        B, T_text, T_vis = (4, 256, 72)
        text_hidden = jax.random.normal(ks[0], (B, T_text, D_TEXT), dtype=jnp.float32)
        vision_tokens = jax.random.normal(ks[1], (B, T_vis, D_VISION), dtype=jnp.float32)
        vision_mask = jnp.ones((B, T_vis), dtype=bool)
        s = 0.02
        Wq = jax.random.normal(ks[2], (D_TEXT, N_HEADS * HEAD_DIM), dtype=jnp.float32) * s
        Wk = jax.random.normal(ks[3], (D_VISION, N_KV_HEADS * HEAD_DIM), dtype=jnp.float32) * s
        Wv = jax.random.normal(ks[4], (D_VISION, N_KV_HEADS * HEAD_DIM), dtype=jnp.float32) * s
        Wo = jax.random.normal(ks[5], (N_HEADS * HEAD_DIM, D_TEXT), dtype=jnp.float32) * s
        return {'text_hidden': text_hidden, 'vision_tokens': vision_tokens, 'vision_mask': vision_mask, 'Wq': Wq, 'Wk': Wk, 'Wv': Wv, 'Wo': Wo}
    _L0_xattn_all = _L0_xattn_setup()
    _L0_xattn_in = {k: v for k, v in _L0_xattn_all.items() if k in ('Wq', 'Wk', 'Wv', 'Wo')}
    del _L0_xattn_all

    def _L0_ffn_setup():
        import jax, jax.numpy as jnp
        import numpy as np
        E = 8
        TOP_K = 2
        H = 256
        I_MOE = 176
        I_SH = 704
        B, S = (2, 256)

        def _moe_forward(hidden_states, router_weight, gate_up_proj, down_proj, sh_gate_w, sh_up_w, sh_down_w, shared_gate_w):
            b, s, h = hidden_states.shape
            x = hidden_states.reshape(-1, h)
            shared = jnp.einsum('ti,hi->th', jax.nn.silu(x @ sh_gate_w.T) * (x @ sh_up_w.T), sh_down_w)
            logits = x @ router_weight.T
            probs = jax.nn.softmax(logits.astype(jnp.float32), axis=-1)
            top_v, top_i = jax.lax.top_k(probs, TOP_K)
            top_v = top_v / top_v.sum(axis=-1, keepdims=True)
            combine = (jax.nn.one_hot(top_i, E, dtype=top_v.dtype) * top_v[..., None]).sum(axis=1)
            out = jnp.zeros_like(x)
            for e in range(E):
                gu = x @ gate_up_proj[e].T
                gate, up = (gu[:, :I_MOE], gu[:, I_MOE:])
                cur = jax.nn.silu(gate) * up @ down_proj[e].T
                out = out + cur * combine[:, e:e + 1]
            out = out + jax.nn.sigmoid(x @ shared_gate_w.T) * shared
            return out.reshape(b, s, h)
        key = jax.random.key(seed)
        ks = jax.random.split(key, 8)
        scale = 0.02
        return {'hidden_states': jax.random.normal(ks[0], (B, S, H), dtype=jnp.float32), 'router_weight': jax.random.normal(ks[1], (E, H), dtype=jnp.float32) * scale, 'gate_up_proj': jax.random.normal(ks[2], (E, 2 * I_MOE, H), dtype=jnp.float32) * scale, 'down_proj': jax.random.normal(ks[3], (E, H, I_MOE), dtype=jnp.float32) * scale, 'sh_gate_w': jax.random.normal(ks[4], (I_SH, H), dtype=jnp.float32) * scale, 'sh_up_w': jax.random.normal(ks[5], (I_SH, H), dtype=jnp.float32) * scale, 'sh_down_w': jax.random.normal(ks[6], (H, I_SH), dtype=jnp.float32) * scale, 'shared_gate_w': jax.random.normal(ks[7], (1, H), dtype=jnp.float32) * scale}
    _L0_ffn_all = _L0_ffn_setup()
    _L0_ffn_in = {k: v for k, v in _L0_ffn_all.items() if k in ('router_weight', 'gate_up_proj', 'down_proj', 'sh_gate_w', 'sh_up_w', 'sh_down_w', 'shared_gate_w')}
    del _L0_ffn_all
    return {'x': x, 'ctx_1024': ctx_1024, 'mask_BxS2_bf1': mask_BxS2_bf1, 'L0_attn_Wq': _L0_attn_in['Wq'], 'L0_attn_bq': _L0_attn_in['bq'], 'L0_attn_Wk': _L0_attn_in['Wk'], 'L0_attn_bk': _L0_attn_in['bk'], 'L0_attn_Wv': _L0_attn_in['Wv'], 'L0_attn_bv': _L0_attn_in['bv'], 'L0_attn_Wo': _L0_attn_in['Wo'], 'L0_attn_bo': _L0_attn_in['bo'], 'L0_xattn_Wq': _L0_xattn_in['Wq'], 'L0_xattn_Wk': _L0_xattn_in['Wk'], 'L0_xattn_Wv': _L0_xattn_in['Wv'], 'L0_xattn_Wo': _L0_xattn_in['Wo'], 'L0_ffn_router_weight': _L0_ffn_in['router_weight'], 'L0_ffn_gate_up_proj': _L0_ffn_in['gate_up_proj'], 'L0_ffn_down_proj': _L0_ffn_in['down_proj'], 'L0_ffn_sh_gate_w': _L0_ffn_in['sh_gate_w'], 'L0_ffn_sh_up_w': _L0_ffn_in['sh_up_w'], 'L0_ffn_sh_down_w': _L0_ffn_in['sh_down_w'], 'L0_ffn_shared_gate_w': _L0_ffn_in['shared_gate_w']}

def reference(x, ctx_1024, mask_BxS2_bf1, L0_attn_Wq, L0_attn_bq, L0_attn_Wk, L0_attn_bk, L0_attn_Wv, L0_attn_bv, L0_attn_Wo, L0_attn_bo, L0_xattn_Wq, L0_xattn_Wk, L0_xattn_Wv, L0_xattn_Wo, L0_ffn_router_weight, L0_ffn_gate_up_proj, L0_ffn_down_proj, L0_ffn_sh_gate_w, L0_ffn_sh_up_w, L0_ffn_sh_down_w, L0_ffn_shared_gate_w):
    import jax
    import jax.numpy as jnp

    def _L0_attn_ref(x, Wq, bq, Wk, bk, Wv, bv, Wo, bo):
        import jax, jax.numpy as jnp
        import numpy as np
        IN_FEATURES = 256
        HEAD_NUM = 64
        D = IN_FEATURES // HEAD_NUM
        SCALE = float(np.sqrt(D))
        B, S, F = x.shape
        d = D
        h = F // d
        q = x @ Wq + bq
        k = x @ Wk + bk
        v = x @ Wv + bv

        def to_heads(t):
            return t.reshape(B, S, d, h).transpose(0, 2, 1, 3)
        q, k, v = (to_heads(q), to_heads(k), to_heads(v))
        scores = jnp.einsum('bdsh,bdth->bdst', q, k) / SCALE
        weights = jax.nn.softmax(scores, axis=-1)
        feats = jnp.einsum('bdst,bdth->bdsh', weights, v)
        feats = feats.transpose(0, 2, 1, 3).reshape(B, S, F)
        return feats @ Wo + bo

    def _L0_xattn_ref(text_hidden, vision_tokens, vision_mask, Wq, Wk, Wv, Wo):
        import jax, jax.numpy as jnp
        import numpy as np
        N_HEADS = 16
        N_KV_HEADS = 8
        HEAD_DIM = 128
        D_TEXT = 256
        D_VISION = 128
        GROUPS = N_HEADS // N_KV_HEADS
        B, T_text, _ = text_hidden.shape
        T_vis = vision_tokens.shape[1]
        scale = jnp.float32(np.sqrt(HEAD_DIM))
        q = (text_hidden @ Wq).reshape(B, T_text, N_HEADS, HEAD_DIM).transpose(0, 2, 1, 3)
        k = (vision_tokens @ Wk).reshape(B, T_vis, N_KV_HEADS, HEAD_DIM).transpose(0, 2, 1, 3)
        v = (vision_tokens @ Wv).reshape(B, T_vis, N_KV_HEADS, HEAD_DIM).transpose(0, 2, 1, 3)
        k = jnp.repeat(k, GROUPS, axis=1)
        v = jnp.repeat(v, GROUPS, axis=1)
        scores = jnp.einsum('bhtd,bhsd->bhts', q, k) / scale
        mask = vision_mask[:, None, None, :]
        scores = jnp.where(mask, scores, -jnp.inf)
        attn = jax.nn.softmax(scores, axis=-1)
        attn = jnp.nan_to_num(attn, nan=0.0)
        out = jnp.einsum('bhts,bhsd->bhtd', attn, v)
        out = out.transpose(0, 2, 1, 3).reshape(B, T_text, N_HEADS * HEAD_DIM)
        return out @ Wo

    def _L0_ffn_ref(hidden_states, router_weight, gate_up_proj, down_proj, sh_gate_w, sh_up_w, sh_down_w, shared_gate_w):
        import jax, jax.numpy as jnp
        import numpy as np
        E = 8
        TOP_K = 2
        H = 256
        I_MOE = 176
        I_SH = 704
        B, S = (2, 256)

        def _moe_forward(hidden_states, router_weight, gate_up_proj, down_proj, sh_gate_w, sh_up_w, sh_down_w, shared_gate_w):
            b, s, h = hidden_states.shape
            x = hidden_states.reshape(-1, h)
            shared = jnp.einsum('ti,hi->th', jax.nn.silu(x @ sh_gate_w.T) * (x @ sh_up_w.T), sh_down_w)
            logits = x @ router_weight.T
            probs = jax.nn.softmax(logits.astype(jnp.float32), axis=-1)
            top_v, top_i = jax.lax.top_k(probs, TOP_K)
            top_v = top_v / top_v.sum(axis=-1, keepdims=True)
            combine = (jax.nn.one_hot(top_i, E, dtype=top_v.dtype) * top_v[..., None]).sum(axis=1)
            out = jnp.zeros_like(x)
            for e in range(E):
                gu = x @ gate_up_proj[e].T
                gate, up = (gu[:, :I_MOE], gu[:, I_MOE:])
                cur = jax.nn.silu(gate) * up @ down_proj[e].T
                out = out + cur * combine[:, e:e + 1]
            out = out + jax.nn.sigmoid(x @ shared_gate_w.T) * shared
            return out.reshape(b, s, h)
        return _moe_forward(hidden_states, router_weight, gate_up_proj, down_proj, sh_gate_w, sh_up_w, sh_down_w, shared_gate_w)
    x = _layernorm(x + _L0_attn_ref(x, L0_attn_Wq, L0_attn_bq, L0_attn_Wk, L0_attn_bk, L0_attn_Wv, L0_attn_bv, L0_attn_Wo, L0_attn_bo), axis=-1)
    x = _layernorm(x + _L0_xattn_ref(x, ctx_1024, mask_BxS2_bf1, L0_xattn_Wq, L0_xattn_Wk, L0_xattn_Wv, L0_xattn_Wo), axis=-1)
    x = _layernorm(x + _L0_ffn_ref(x, L0_ffn_router_weight, L0_ffn_gate_up_proj, L0_ffn_down_proj, L0_ffn_sh_gate_w, L0_ffn_sh_up_w, L0_ffn_sh_down_w, L0_ffn_shared_gate_w), axis=-1)
    return x

_drawn_inputs = setup_inputs


def setup_inputs(seed=0):
    import zlib

    import numpy as np

    out = dict(_drawn_inputs(seed))
    spreads = {}
    factors = {'L0_attn_Wq': 8.0,
     'L0_attn_bq': 8.0,
     'L0_attn_Wk': 8.0,
     'L0_attn_bk': 8.0,
     'L0_attn_Wv': 3.806,
     'L0_attn_bv': 8.0,
     'L0_attn_Wo': 3.662,
     'L0_attn_bo': 5.883,
     'L0_xattn_Wq': 8.0,
     'L0_xattn_Wk': 8.0,
     'L0_ffn_router_weight': 6.49,
     'L0_ffn_gate_up_proj': 5.668,
     'L0_ffn_down_proj': 5.681,
     'L0_ffn_sh_gate_w': 4.05,
     'L0_ffn_sh_up_w': 3.994,
     'L0_ffn_sh_down_w': 4.012,
     'L0_ffn_shared_gate_w': 8.0}
    for name, (base, spread) in spreads.items():
        noise = np.random.default_rng([zlib.crc32(name.encode()), seed]).standard_normal(out[name].shape)
        drawn = base * np.exp(spread * noise) if base else spread * noise
        out[name] = jnp.asarray(drawn.astype(out[name].dtype))
    for name, factor in factors.items():
        out[name] = (out[name] * factor).astype(out[name].dtype)
    return out
```

```python
from contextlib import ExitStack

import numpy as np

import concourse.bass as bass
from concourse import mybir

ALU = mybir.AluOpType
ACT = mybir.ActivationFunctionType
AX = mybir.AxisListType
F32 = mybir.dt.float32
F32R = mybir.dt.float32r
BF16 = mybir.dt.bfloat16
U8 = mybir.dt.uint8

B, S, F = 32, 56, 256
KC = F // 128
PAIR = 2 * S
NPAIR = B // 2
TILES = 4
BLK = TILES * PAIR
NBLK = NPAIR // TILES
SA_HEADS, SA_D = 4, 64
SA_SCALE = 1.0 / np.sqrt(F // 64)
CTX, CD = 1500, 128
XH, XKV = 16, 8
X_SCALE = 1.0 / np.sqrt(128.0)
CH = 12
CK = CTX // CH
FILLS = 3
FW = CTX // FILLS
UNITS = 4
SLOTS = 4
SW = UNITS * PAIR
EXPERTS, I_MOE, I_SH = 8, 176, 704
NR = EXPERTS + 1
IW = EXPERTS * I_MOE + I_SH
IC = -(-IW // 128)
EPS = 1e-5
BIG = 1e30


def wait_apart(engine, held, *waits):
    for semaphore, count in waits[:-1]:
        engine.wait_ge(semaphore, count)
    semaphore, count = waits[-1]
    if not isinstance(count, int):
        with engine.register() as own:
            engine.reg_add(own, count - 1, 1)
            engine.wait_ge(*held)
            engine.wait_ge(semaphore, own)
    else:
        engine.wait_ge(semaphore, count)


def norm_stats(dve, z, stats, mv, chain, count, done):
    dve.bn_stats(out=stats, in_=z).then_inc(chain, 1)
    wait_apart(dve, done, (chain, count + 1))
    dve.bn_aggr(out=mv, in_=stats).then_inc(chain, 1)
    dve.wait_ge(chain, count + 2)
    return dve.tensor_scalar(mv[:, 1:2], mv[:, 1:2], EPS, None, ALU.add)


def phase_a(nc, D, A_fold, M_fold):
    with ExitStack() as ctx:
        def sb(name, shape, dt=F32):
            return ctx.enter_context(nc.sbuf_tensor(name, shape, dt))

        def sem(name):
            return ctx.enter_context(nc.semaphore("a_" + name))

        bank = [ctx.enter_context(nc.psum_tensor(f"a_bank{j}", [128, 512], F32)) for j in range(8)]

        wqT = sb("a_wqT", [128, XH, F])
        wkT = sb("a_wkT", [128, XKV, CD])
        wvT = sb("a_wvT", [128, XKV, CD])
        wo = sb("a_wo", [128, XH, F])
        saw = sb("a_saw", [128, 4, KC, F])
        bqk = sb("a_bqk", [128, 2, KC])
        bv = sb("a_bv", [PAIR, F])
        bo = sb("a_bo", [PAIR, F])
        ident = sb("a_ident", [128, 128])
        own_q = sb("a_own_q", [2, PAIR])
        other_k = sb("a_other_k", [2, SA_HEADS * PAIR])
        xT = sb("a_xT", [128, KC, BLK])
        x = sb("a_x", [PAIR, TILES, F])
        xb = sb("a_xb", [PAIR, TILES, F])
        qT = sb("a_qT", [128, KC, BLK])
        kT = sb("a_kT", [128, 2, KC, BLK])
        v = sb("a_v", [PAIR, TILES, F])
        e = sb("a_e", [PAIR, TILES, SA_HEADS, PAIR])
        eT = sb("a_eT", [PAIR, TILES, SA_HEADS * PAIR])
        oT = sb("a_oT", [128, TILES, KC, PAIR])
        mx = sb("a_mx", [PAIR, TILES, SA_HEADS])
        shift = sb("a_shift", [PAIR, TILES, SA_HEADS])
        den = sb("a_den", [PAIR, TILES, SA_HEADS])
        rden = sb("a_rden", [PAIR, TILES, SA_HEADS])
        z = sb("a_z", [PAIR, TILES, F])
        y = sb("a_y", [PAIR, TILES, F])
        stats = sb("a_stats", [PAIR, TILES, 6])
        mv = sb("a_mv", [PAIR, TILES, 2])
        half = sb("a_half", [PAIR, 1])

        fold_loaded, loaded, x_loaded = sem("fold_loaded"), sem("loaded"), sem("x_loaded")
        folded, fold_taken = sem("folded"), sem("fold_taken")
        half_set = sem("half_set")
        qk_done, qk_taken = sem("qk_done"), sem("qk_taken")
        v_done, v_taken = sem("v_done"), sem("v_taken")
        xb_done, s_done = sem("xb_done"), sem("s_done")
        max_done, shift_done, e_done = sem("max_done"), sem("shift_done"), sem("e_done")
        rden_done, e_normed = sem("rden_done"), sem("e_normed")
        eT_done, eT_taken = sem("eT_done"), sem("eT_taken")
        o_done, o_taken = sem("o_done"), sem("o_taken")
        p_done, z_done = sem("p_done"), sem("z_done")
        stat_chain, var_done, rstd_done = sem("stat_chain"), sem("var_done"), sem("rstd_done")
        y_done, y_stored = sem("y_done"), sem("y_stored")

        FOLDS = XH

        block = ctx.enter_context(nc.Block())

        @block.sync
        def _(sp):
            for dst, src in ((wqT, D["xwqT"]), (wkT, D["xwkT"]), (wvT, D["xwvT"]), (wo, D["xwo"])):
                sp.dma_start(dst[:], src).then_inc(fold_loaded, 16)
            for n, name in enumerate(("wq", "wk", "wv", "wo")):
                sp.dma_start(saw[:, n], D[name]).then_inc(loaded, 16)
            sp.dma_start(bqk[:, 0], D["bq"]).then_inc(loaded, 16)
            sp.dma_start(bqk[:, 1], D["bk"]).then_inc(loaded, 16)
            sp.dma_start(bv[:], D["bv"].partition_broadcast(PAIR)).then_inc(loaded, 16)
            sp.dma_start(bo[:], D["bo"].partition_broadcast(PAIR)).then_inc(loaded, 16)
            sp.dma_start(ident[:], D["ident"]).then_inc(loaded, 16)
            sp.dma_start(own_q[:], D["own_q"]).then_inc(loaded, 16)
            sp.dma_start(other_k[:], D["other_k"]).then_inc(loaded, 16)

            def block_io(i, first=False):
                if not first:
                    sp.wait_ge(v_done, 2 * i)
                    sp.wait_ge(xb_done, i)
                sp.dma_start(xT[:], D["xT"][:, :, bass.ts(i, BLK)]).then_inc(x_loaded, 16)
                sp.dma_start(x[:], D["x"][:, bass.ts(i, TILES), :]).then_inc(x_loaded, 16)
                for t in range(TILES):
                    sp.wait_ge(y_done, TILES * i + t + 1)
                    sp.dma_start(D["y1"][:, bass.ds(i * TILES + t, 1), :], y[:, t:t + 1]).then_inc(y_stored, 16)

            block_io(0, first=True)
            with sp.Fori(1, NBLK) as i:
                block_io(i)
            sp.wait_ge(y_stored, 16 * NPAIR)

        @block.tensor
        def _(pe):
            pe.wait_ge(fold_loaded, 64)
            for n in range(FOLDS):
                if n >= 8:
                    pe.wait_ge(fold_taken, n - 7)
                for k in range(2):
                    h = 2 * (n % 8) + k
                    out = bank[n % 8][:, k * F:(k + 1) * F]
                    if n < 8:
                        for kc in range(KC):
                            mm = pe.matmul(out[:, kc * 128:(kc + 1) * 128], wqT[:, h, kc * 128:(kc + 1) * 128],
                                           wkT[:, h // 2, :], start=True, stop=True)
                    else:
                        mm = pe.matmul(out, wvT[:, h // 2, :], wo[:, h, :], start=True, stop=True)
                mm.then_inc(folded, 1)
            pe.wait_ge(loaded, 16 * 11)
            pe.wait_ge(fold_taken, FOLDS)
            pe.wait_ge(half_set, 3)

            def block_pe(i, first=False):
                pe.wait_ge(x_loaded, 32 * (i + 1))
                if not first:
                    pe.wait_ge(o_taken, 2 * TILES * i)
                for n in range(4):
                    for kc in range(KC):
                        mm = pe.matmul(bank[n][:, 0:BLK], saw[:, n // 2, kc, (n % 2) * 128:(n % 2 + 1) * 128],
                                       xT[:, kc, :], start=(kc == 0), stop=(kc == KC - 1))
                    mm.then_inc(qk_done, 1)
                if not first:
                    pe.wait_ge(z_done, TILES * i)
                for t in range(TILES):
                    for kc in range(KC):
                        mm = pe.matmul(bank[4 + t // 2][0:PAIR, (t % 2) * F:(t % 2 + 1) * F],
                                       xT[:, kc, t * PAIR:(t + 1) * PAIR], saw[:, 2, kc, :],
                                       start=(kc == 0), stop=(kc == KC - 1))
                    if t % 2:
                        mm.then_inc(v_done, 1)
                pe.wait_ge(qk_taken, 6 * (i + 1))
                for t in range(TILES):
                    sc = bank[t][0:PAIR, 0:SA_HEADS * PAIR]
                    for h in range(SA_HEADS):
                        mm = pe.matmul(sc[:, h * PAIR:(h + 1) * PAIR],
                                       qT[:, h // 2, t * PAIR:(t + 1) * PAIR],
                                       kT[:, h % 2, h // 2, t * PAIR:(t + 1) * PAIR],
                                       start=(h == 0), stop=False, skip_group_check=True)
                    pe.matmul(sc, own_q[:], other_k[:], start=False, stop=True, skip_group_check=True).then_inc(s_done, 1)
                pe.wait_ge(v_taken, 2 * (i + 1))
                for t in range(TILES):
                    pe.wait_ge(e_normed, TILES * i + t + 1)
                    for h in range(SA_HEADS):
                        mm = pe.transpose(bank[4 + t][0:PAIR, h * PAIR:(h + 1) * PAIR], e[:, t, h, :],
                                          ident[0:PAIR, 0:PAIR])
                    mm.then_inc(eT_done, 1)
                for t in range(TILES):
                    pe.wait_ge(eT_taken, TILES * i + t + 1)
                    for m in range(KC):
                        mm = pe.matmul(bank[t][:, m * 2 * PAIR:(m + 1) * 2 * PAIR], v[:, t, m * 128:(m + 1) * 128],
                                       eT[:, t, m * 2 * PAIR:(m + 1) * 2 * PAIR], start=True, stop=True)
                    mm.then_inc(o_done, 1)
                for t in range(TILES):
                    pe.wait_ge(o_taken, 2 * (TILES * i + t + 1))
                    for m in range(KC):
                        mm = pe.matmul(bank[4 + t][0:PAIR, 0:F], oT[:, t, m, :], saw[:, 3, m, :],
                                       start=(m == 0), stop=(m == KC - 1))
                    mm.then_inc(p_done, 1)

            block_pe(0, first=True)
            with pe.Fori(1, NBLK) as i:
                block_pe(i)

        @block.scalar
        def _(act):
            for n in range(FOLDS):
                act.wait_ge(folded, n + 1)
                dst = (A_fold if n < 8 else M_fold)[:, 2 * (n % 8):2 * (n % 8) + 2, :]
                act.copy(dst, bank[n % 8][:].rearrange("p (a n) -> p a n", a=2)).then_inc(fold_taken, 1)
            act.wait_ge(loaded, 16 * 11)

            def block_act(i):
                for m in range(KC):
                    act.wait_ge(qk_done, 4 * i + m + 1)
                    act.activation(qT[:, m, :], bank[m][:, 0:BLK], ACT.Identity,
                                   bias=bqk[:, 0, m:m + 1]).then_inc(qk_taken, 1)
                for m in range(KC):
                    act.wait_ge(qk_done, 4 * i + KC + m + 1)
                    for k in range(2):
                        own = slice(SA_D * k, SA_D * (k + 1))
                        act.activation(kT[own, k, m, :], bank[KC + m][own, 0:BLK], ACT.Identity,
                                       bias=bqk[own, 1, m:m + 1]).then_inc(qk_taken, 1)
                for t in range(TILES):
                    act.wait_ge(shift_done, TILES * i + t + 1)
                    for h in range(SA_HEADS):
                        act.activation(e[:, t, h, :], bank[t][0:PAIR, h * PAIR:(h + 1) * PAIR], ACT.Exp,
                                       bias=shift[:, t, h:h + 1], scale=float(SA_SCALE),
                                       accum_out=den[:, t, h:h + 1]).then_inc(e_done, 1)
                for t in range(TILES):
                    act.wait_ge(eT_done, TILES * i + t + 1)
                    act.copy(eT[:, t, :], bank[4 + t][0:PAIR, 0:SA_HEADS * PAIR]).then_inc(eT_taken, 1)

            block_act(0)
            with act.Fori(1, NBLK) as i:
                block_act(i)

        @block.vector
        def _(dve):
            dve.memset(half[:], -0.5).then_inc(half_set, 1)
            dve.memset(kT[SA_D:, 0], 0.0).then_inc(half_set, 1)
            dve.memset(kT[:SA_D, 1], 0.0).then_inc(half_set, 1)
            dve.wait_ge(loaded, 16 * 11)

            def block_dve(i, first=False):
                for n in range(2):
                    dve.wait_ge(v_done, 2 * i + n + 1)
                    dve.tensor_tensor(v[:, 2 * n:2 * n + 2, :],
                                      bank[4 + n][0:PAIR, :].rearrange("p (t f) -> p t f", t=2),
                                      bv[:].unsqueeze(1).to_broadcast([PAIR, 2, F]), ALU.add).then_inc(v_taken, 1)
                for t in range(TILES):
                    dve.wait_ge(s_done, TILES * i + t + 1)
                    dve.tensor_reduce(mx[:, t, :], bank[t][0:PAIR, 0:SA_HEADS * PAIR].rearrange(
                        "p (h k) -> p h k", h=SA_HEADS), AX.X, ALU.max).then_inc(max_done, 1)
                    dve.wait_ge(max_done, TILES * i + t + 1)
                    dve.tensor_scalar(shift[:, t, :], mx[:, t, :], -float(SA_SCALE), None,
                                      ALU.mult).then_inc(shift_done, 1)
                for t in range(TILES):
                    dve.wait_ge(e_done, SA_HEADS * (TILES * i + t + 1))
                    dve.reciprocal(rden[:, t, :], den[:, t, :]).then_inc(rden_done, 1)
                    dve.wait_ge(rden_done, TILES * i + t + 1)
                    dve.tensor_tensor(e[:, t], e[:, t], rden[:, t, :].unsqueeze(2).to_broadcast(
                        [PAIR, SA_HEADS, PAIR]), ALU.mult).then_inc(e_normed, 1)
                for t in range(TILES):
                    dve.wait_ge(o_done, TILES * i + t + 1)
                    for k in range(2):
                        p0 = SA_D * k
                        dve.tensor_copy(oT[p0:p0 + SA_D, t], bank[t][p0:p0 + SA_D, 0:4 * PAIR].rearrange(
                            "p (m k q) -> p m k q", m=KC, k=2)[:, :, k, :]).then_inc(o_taken, 1)
                dve.wait_ge(xb_done, i + 1)
                for t in range(TILES):
                    n = TILES * i + t
                    dve.wait_ge(p_done, n + 1)
                    dve.tensor_tensor(z[:, t, :], bank[4 + t][0:PAIR, 0:F], xb[:, t, :], ALU.add).then_inc(z_done, 1)
                    dve.wait_ge(z_done, n + 1)
                    norm_stats(dve, z[:, t, :], stats[:, t, :], mv[:, t, :], stat_chain, 2 * n, (loaded, 16)).then_inc(var_done, 1)
                for t in range(TILES):
                    n = TILES * i + t
                    dve.wait_ge(rstd_done, n + 1)
                    if not first:
                        dve.wait_ge(y_stored, 16 * (n - TILES + 1))
                    dve.tensor_scalar(y[:, t, :], z[:, t, :], mv[:, t, 0:1], mv[:, t, 1:2],
                                      ALU.subtract, ALU.mult).then_inc(y_done, 1)

            block_dve(0, first=True)
            with dve.Fori(1, NBLK) as i:
                block_dve(i)

        @block.gpsimd
        def _(pool):
            pool.wait_ge(loaded, 16 * 11)
            pool.wait_ge(half_set, 1)

            def block_pool(i, first=False):
                pool.wait_ge(x_loaded, 32 * (i + 1))
                if not first:
                    pool.wait_ge(z_done, TILES * i)
                pool.tensor_tensor(xb[:], x[:], bo[:].unsqueeze(1).to_broadcast([PAIR, TILES, F]),
                                   ALU.add).then_inc(xb_done, 1)
                for t in range(TILES):
                    pool.wait_ge(var_done, TILES * i + t + 1)
                    pool.tensor_tensor(mv[:, t, 1:2], mv[:, t, 1:2], half[:], ALU.pow).then_inc(rstd_done, 1)

            block_pool(0, first=True)
            with pool.Fori(1, NBLK) as i:
                block_pool(i)


def phase_b(nc, D, A_fold, M_fold):
    with ExitStack() as ctx:
        def sb(name, shape, dt=F32):
            return ctx.enter_context(nc.sbuf_tensor("b_" + name, shape, dt))

        def sem(name):
            return ctx.enter_context(nc.semaphore("b_" + name))

        def ps(name):
            return ctx.enter_context(nc.psum_tensor("b_" + name, [128, 512], F32))

        score_bank = [ps(f"score{j}") for j in range(FILLS)]
        turn_bank = [ps(f"turn{j}") for j in range(3)]
        out_bank = ps("out")
        misc_bank = ps("misc")

        ident = sb("ident", [128, 128])
        ones_r = sb("ones_r", [2 * UNITS, 128], F32R)
        own_unit = sb("own_unit", [2 * UNITS, UNITS, PAIR])
        half = sb("half", [PAIR, 1])
        y1 = sb("y1", [PAIR, F])
        y1T = sb("y1T", [128, KC, PAIR])
        q_hi = sb("q_hi", [128, 2, XH, S], F32R)
        q_lo = sb("q_lo", [128, 2, XH, S], F32R)
        cT_in = sb("cT_in", [128, CTX])
        cT_hi = sb("cT_hi", [128, 2, CTX], F32R)
        cT_lo = sb("cT_lo", [128, 2, CTX], F32R)
        c_in = sb("c_in", [CK, CH * CD])
        c_hi = sb("c_hi", [CK, 2, CH * CD], F32R)
        c_lo = sb("c_lo", [CK, 2, CH * CD], F32R)
        mask_in = sb("mask_in", [PAIR, CTX], U8)
        mask_add = sb("mask_add", [PAIR, 2, CTX], BF16)
        p = sb("p", [PAIR, 2, UNITS, CTX])
        top = sb("top", [PAIR, 2, UNITS, FILLS])
        top3 = sb("top3", [PAIR, FILLS])
        shift = sb("shift", [PAIR, 2, UNITS])
        den = sb("den", [PAIR, 2, UNITS])
        keep = sb("keep", [PAIR, UNITS])
        rden = sb("rden", [PAIR, UNITS])
        rden_parts = sb("rden_parts", [PAIR, 2 * UNITS])
        rden_r = sb("rden_r", [PAIR, UNITS], F32R)
        rden_rows = sb("rden_rows", [2 * UNITS, UNITS, PAIR], F32R)
        pT_hi = sb("pT_hi", [CK, 3, SW], F32R)
        pT_lo = sb("pT_lo", [CK, 3, SW], F32R)
        out_sb = sb("out_sb", [128, SW])
        oT = sb("oT", [128, XH, PAIR])
        y1_res = sb("y1_res", [PAIR, F])
        z = sb("z", [PAIR, F])
        y2 = sb("y2", [PAIR, F])
        stats = sb("stats", [PAIR, 6])
        mv = sb("mv", [PAIR, 2])

        const_loaded, const_set = sem("const_loaded"), sem("const_set")
        y1_loaded, cT_loaded, c_loaded, mask_loaded = sem("y1_loaded"), sem("cT_loaded"), sem("c_loaded"), sem("mask_loaded")
        res_loaded, y2_stored = sem("res_loaded"), sem("y2_stored")
        y1_turned, y1T_done = sem("y1_turned"), sem("y1T_done")
        q_done, q_hi_done, q_lo_done = sem("q_done"), sem("q_hi_done"), sem("q_lo_done")
        cT_split, c_split, mask_ready = sem("cT_split"), sem("c_split"), sem("mask_ready")
        fill_done, fill_taken = sem("fill_done"), sem("fill_taken")
        shift_done, exp_done = sem("shift_done"), sem("exp_done")
        turned, hi_done, lo_done, pv_done = sem("turned"), sem("hi_done"), sem("lo_done"), sem("pv_done")
        out_copied = sem("out_copied")
        rden_chain, rden_turned, rows_done, spread_done = sem("rden_chain"), sem("rden_turned"), sem("rows_done"), sem("spread_done")
        oT_done, proj_done = sem("oT_done"), sem("proj_done")
        z_done, stat_chain, var_done, rstd_done, y2_done = sem("z_done"), sem("stat_chain"), sem("var_done"), sem("rstd_done"), sem("y2_done")

        STEPS = SLOTS * CH
        TURN_LAG = CH + 3
        PV_LAG = TURN_LAG + 2
        TAIL = 2 * CH + 8
        RDEN = 6

        def four_heads(q, g):
            return q[:, :, 4 * g:4 * g + 4, :].rearrange("p b h q -> p h b q")

        def four_heads_bank(g):
            return score_bank[g % FILLS][:, 0:4 * PAIR].rearrange("p (h b q) -> p h b q", h=4, b=2)

        def pair_of(i, n):
            return i + n // STEPS, n % STEPS

        block = ctx.enter_context(nc.Block())

        @block.sync
        def _(sp):
            sp.dma_start(ident[:], D["ident"]).then_inc(const_loaded, 16)
            sp.dma_start(own_unit[:], D["own_unit"]).then_inc(const_loaded, 16)

            def load_y1(i, first=False):
                if not first:
                    sp.wait_ge(y1_turned, i)
                sp.dma_start(y1[:], D["y1"][:, bass.ds(i, 1), :].rearrange("p a f -> p (a f)")).then_inc(y1_loaded, 16)

            def load_batch(i, b, first=False):
                n = 2 * i + b
                if not (first and b == 0):
                    sp.wait_ge(cT_split, 2 * n)
                sp.dma_start(cT_in[:], D["ctxT"][bass.ds(n, 1)].rearrange("a d s -> (a d) s")).then_inc(cT_loaded, 16)
                if not (first and b == 0):
                    wait_apart(sp, (y1_loaded, 16), (mask_ready, n))
                sp.dma_start(mask_in[:], D["mask"][bass.ds(n, 1)].rearrange("a s -> (a s)").partition_broadcast(
                    PAIR)).then_inc(mask_loaded, 16)
                if not (first and b == 0):
                    sp.wait_ge(c_split, 2 * n)
                sp.dma_start(c_in[:], D["ctx"][bass.ds(n, 1)].rearrange("a p n -> (a p) n")).then_inc(c_loaded, 16)

            def residual(i):
                sp.dma_start(y1_res[:], D["y1"][:, bass.ds(i, 1), :].rearrange("p a f -> p (a f)")).then_inc(res_loaded, 16)

            def store(i):
                sp.wait_ge(y2_done, i + 1)
                sp.dma_start(D["y2"][:, bass.ds(i, 1), :].rearrange("p a f -> p (a f)"), y2[:]).then_inc(y2_stored, 16)

            load_y1(0, first=True)
            load_batch(0, 0, first=True)
            load_batch(0, 1, first=True)
            residual(0)
            with sp.Fori(1, NPAIR) as i:
                load_y1(i)
                load_batch(i, 0)
                load_batch(i, 1)
                store(i - 1)
                residual(i)
            store(NPAIR - 1)
            sp.wait_ge(y2_stored, 16 * NPAIR)

        @block.tensor
        def _(pe):
            pe.wait_ge(const_loaded, 32)
            pe.wait_ge(const_set, 3)

            def queries(i, first=False):
                pe.wait_ge(y1_loaded, 16 * (i + 1))
                if not first:
                    pe.wait_ge(rows_done, SLOTS * i - 1)
                for kc in range(KC):
                    mm = pe.transpose(misc_bank[:, kc * PAIR:(kc + 1) * PAIR], y1[:, kc * 128:(kc + 1) * 128],
                                      ident[0:PAIR, 0:PAIR])
                mm.then_inc(y1_turned, 1)
                pe.wait_ge(y1T_done, i + 1)
                if not first:
                    pe.wait_ge(fill_taken, STEPS * i)
                for g in range(XH // 4):
                    if g == FILLS:
                        pe.wait_ge(q_lo_done, 4 * i + 1)
                    for k in range(4):
                        h = 4 * g + k
                        for kc in range(KC):
                            mm = pe.matmul(score_bank[g % FILLS][:, k * PAIR:(k + 1) * PAIR],
                                           A_fold[:, h, kc * 128:(kc + 1) * 128], y1T[:, kc, :],
                                           start=(kc == 0), stop=(kc == KC - 1))
                    mm.then_inc(q_done, 1)
                pe.wait_ge(q_lo_done, 4 * (i + 1))

            def fill(i, n):
                slot, u, j = n // CH, n % CH // FILLS, n % FILLS
                b, h = slot // 2, (slot % 2) * 2 * UNITS + 2 * u
                if n % (2 * CH) == 0:
                    pe.wait_ge(cT_split, 2 * (2 * i + b + 1))
                if n >= FILLS:
                    pe.wait_ge(fill_taken, STEPS * i + n - FILLS + 1)
                out = score_bank[j][0:PAIR, 0:FW]
                keys = slice(j * FW, (j + 1) * FW)
                hi = q_hi[:, b, h:h + 2, :].rearrange("p h q -> p (h q)")
                lo = q_lo[:, b, h:h + 2, :].rearrange("p h q -> p (h q)")
                pe.matmul(out, hi, cT_hi[:, b, keys], start=True, stop=False)
                pe.matmul(out, hi, cT_lo[:, b, keys], start=False, stop=False)
                pe.matmul(out, lo, cT_hi[:, b, keys], start=False, stop=True).then_inc(fill_done, 1)

            def turn(i, n, first):
                slot, c = n // CH, n % CH
                if c == 0:
                    pe.wait_ge(exp_done, UNITS * (SLOTS * i + slot + 1))
                if not (first and n < 3):
                    pe.wait_ge(lo_done, STEPS * i + n - 2)
                for u in range(UNITS):
                    mm = pe.transpose(turn_bank[n % 3][0:CK, u * PAIR:(u + 1) * PAIR],
                                      p[:, slot % 2, u, c * CK:(c + 1) * CK], ident[0:PAIR, 0:PAIR])
                mm.then_inc(turned, 1)

            def weigh(i, n, first):
                slot, c = n // CH, n % CH
                b = slot // 2
                if c == 0:
                    if not (first and slot == 0):
                        pe.wait_ge(out_copied, SLOTS * i + slot)
                    pe.wait_ge(c_split, 2 * (2 * i + b + 1))
                pe.wait_ge(lo_done, STEPS * i + n + 1)
                out = out_bank[:, 0:SW]
                hi, lo = c_hi[:, b, c * CD:(c + 1) * CD], c_lo[:, b, c * CD:(c + 1) * CD]
                pe.matmul(out, hi, pT_hi[:, n % 3, :], start=(c == 0), stop=False)
                pe.matmul(out, hi, pT_lo[:, n % 3, :], start=False, stop=False)
                pe.matmul(out, lo, pT_hi[:, n % 3, :], start=False, stop=(c == CH - 1)).then_inc(pv_done, 1)

            def turn_rden(i, slot, first):
                s = SLOTS * i + slot
                if not (first and slot == 0):
                    pe.wait_ge(oT_done, s)
                if slot == 0 and not first:
                    pe.wait_ge(z_done, i)
                pe.wait_ge(rden_chain, RDEN * (s + 1))
                pe.transpose(misc_bank[0:2 * UNITS, 0:PAIR], rden_parts[:], ident[0:PAIR, 0:PAIR]).then_inc(rden_turned, 1)

            def spread_rden(i, slot):
                pe.wait_ge(rows_done, SLOTS * i + slot + 1)
                pe.matmul(misc_bank[:, 0:SW], ones_r[:], rden_rows[:].rearrange("r u q -> r (u q)"),
                          start=True, stop=True).then_inc(spread_done, 1)

            def project(i):
                pe.wait_ge(oT_done, SLOTS * (i + 1))
                for h in range(XH):
                    mm = pe.matmul(misc_bank[0:PAIR, 0:F], oT[:, h, :], M_fold[:, h, :],
                                   start=(h == 0), stop=(h == XH - 1))
                mm.then_inc(proj_done, 1)

            def step(i, n, first, fills=True):
                if fills:
                    fill(i, n)
                j, m = pair_of(i, n - TURN_LAG)
                if not (first and n < TURN_LAG) and (fills or n - TURN_LAG < STEPS * 1):
                    turn(j, m, first and n - TURN_LAG < STEPS)
                j, m = pair_of(i, n - PV_LAG)
                if not (first and n < PV_LAG) and (fills or n - PV_LAG < STEPS * 1):
                    weigh(j, m, first and n - PV_LAG < STEPS)
                side(i, n, first, fills)

            def side(i, n, first, fills):
                slot = n // CH
                if n % CH == 7:
                    j, m = i + (slot - 1) // SLOTS, (slot - 1) % SLOTS
                    if not (first and slot < 1) and (fills or slot - 1 < SLOTS):
                        turn_rden(j, m, first)
                if n % CH == 4:
                    j, m = i + (slot - 2) // SLOTS, (slot - 2) % SLOTS
                    if not (first and slot < 2) and (fills or slot - 2 < SLOTS):
                        spread_rden(j, m)
                if n == CH + 6 and not first:
                    project(i - 1)

            def pair_pe(i, first=False):
                queries(i, first)
                for n in range(STEPS):
                    step(i, n, first)

            pair_pe(0, first=True)
            with pe.Fori(1, NPAIR) as i:
                pair_pe(i)
            for n in range(STEPS, STEPS + CH + 5):
                step(NPAIR - 1, n, False, fills=False)
            project(NPAIR - 1)

        @block.scalar
        def _(act):
            def y1T_copy(i):
                act.wait_ge(y1_turned, i + 1)
                act.copy(y1T[:].rearrange("p k q -> p (k q)"), misc_bank[:, 0:KC * PAIR]).then_inc(y1T_done, 1)

            def q_round(i):
                for g in range(XH // 4):
                    act.wait_ge(q_done, 4 * i + g + 1)
                    act.copy(four_heads(q_hi, g), four_heads_bank(g)).then_inc(q_hi_done, 1)

            def p_round(i, n, first):
                g = STEPS * i + n
                act.wait_ge(turned, g + 1)
                if not (first and n < 3):
                    act.wait_ge(pv_done, g - 2)
                act.copy(pT_hi[:, n % 3, :], turn_bank[n % 3][0:CK, 0:SW]).then_inc(hi_done, 1)

            def exps(i, slot, u):
                act.wait_ge(shift_done, UNITS * (SLOTS * i + slot) + u + 1)
                act.activation(p[:, slot % 2, u, :], p[:, slot % 2, u, :], ACT.Exp,
                               bias=shift[:, slot % 2, u:u + 1], scale=float(X_SCALE),
                               accum_out=den[:, slot % 2, u:u + 1]).then_inc(exp_done, 1)

            def out_copy(i, slot, first):
                if not (first and slot == 0):
                    act.wait_ge(oT_done, SLOTS * i + slot)
                act.wait_ge(pv_done, CH * (SLOTS * i + slot + 1))
                act.copy(out_sb[:], out_bank[:, 0:SW]).then_inc(out_copied, 1)

            def step(i, n, first, fills=True):
                j, m = pair_of(i, n - TURN_LAG)
                if not (first and n < TURN_LAG) and (fills or n - TURN_LAG < STEPS):
                    p_round(j, m, first)
                if n % FILLS == FILLS - 1 and fills:
                    exps(i, n // CH, n % CH // FILLS)
                slot = n // CH
                if n % CH == 4:
                    j, m = i + (slot - 2) // SLOTS, (slot - 2) % SLOTS
                    if not (first and slot < 2) and (fills or slot - 2 < SLOTS):
                        out_copy(j, m, first)

            def pair_act(i, first=False):
                y1T_copy(i)
                q_round(i)
                for n in range(STEPS):
                    step(i, n, first)

            pair_act(0, first=True)
            with act.Fori(1, NPAIR) as i:
                pair_act(i)
            for n in range(STEPS, STEPS + CH + 5):
                step(NPAIR - 1, n, False, fills=False)

        @block.vector
        def _(dve):
            dve.memset(half[:], -0.5).then_inc(const_set, 1)
            dve.memset(out_sb[0:2 * UNITS, 0:128], 1.0).then_inc(const_set, 1)
            dve.wait_ge(const_set, 2)
            dve.tensor_copy(ones_r[:], out_sb[0:2 * UNITS, 0:128]).then_inc(const_set, 1)
            dve.wait_ge(const_loaded, 32)

            def q_rest(i):
                for g in range(XH // 4):
                    dve.wait_ge(q_hi_done, 4 * i + g + 1)
                    dve.tensor_tensor(four_heads(q_lo, g), four_heads_bank(g), four_heads(q_hi, g).bitcast(F32),
                                      ALU.subtract).then_inc(q_lo_done, 1)

            def scores(i, n, first):
                slot, u, j = n // CH, n % CH // FILLS, n % FILLS
                par, b = slot % 2, slot // 2
                waits = [(fill_done, STEPS * i + n + 1)]
                if n % (2 * CH) == 0:
                    waits.append((mask_ready, 2 * i + b + 1))
                if u == 0 and not (first and slot < 2):
                    waits.append((turned, CH * (SLOTS * i + slot - 2) + (j + 1) * (CH // FILLS)))
                wait_apart(dve, (const_loaded, 32), *waits)
                keys = slice(j * FW, (j + 1) * FW)
                dve.tensor_tensor_reduce(out=p[:, par, u, keys], in0=score_bank[j][0:PAIR, 0:FW],
                                         in1=mask_add[:, b, keys], scale=1.0, scalar=-3.0e38,
                                         op0=ALU.add, op1=ALU.max,
                                         accum_out=top[:, par, u, j:j + 1]).then_inc(fill_taken, 1)

            def shifts(i, slot, u):
                par = slot % 2
                dve.wait_ge(fill_taken, STEPS * i + CH * slot + FILLS * (u + 1))
                dve.tensor_scalar(top3[:], top[:, par, u, :], -float(X_SCALE), None, ALU.mult, ALU.min,
                                  accum_out=shift[:, par, u:u + 1]).then_inc(shift_done, 1)

            def p_rest(i, n, first):
                g = STEPS * i + n
                dve.wait_ge(hi_done, g + 1)
                dve.tensor_tensor(pT_lo[:, n % 3, :], turn_bank[n % 3][0:CK, 0:SW],
                                  pT_hi[:, n % 3, :].bitcast(F32), ALU.subtract).then_inc(lo_done, 1)

            def reciprocals(i, slot):
                s = SLOTS * i + slot
                par = slot % 2
                dve.wait_ge(exp_done, UNITS * (s + 1))
                dve.tensor_scalar(keep[:], shift[:, par, :], float(X_SCALE * BIG / 2), None,
                                  ALU.is_lt).then_inc(rden_chain, 1)
                dve.reciprocal(rden[:], den[:, par, :]).then_inc(rden_chain, 1)
                dve.wait_ge(rden_chain, RDEN * s + 2)
                dve.tensor_tensor(rden[:], rden[:], keep[:], ALU.mult).then_inc(rden_chain, 1)
                dve.wait_ge(rden_chain, RDEN * s + 3)
                dve.tensor_copy(rden_r[:], rden[:]).then_inc(rden_chain, 1)
                dve.wait_ge(rden_chain, RDEN * s + 4)
                dve.tensor_copy(rden_parts[:, 0:UNITS], rden_r[:].bitcast(F32)).then_inc(rden_chain, 1)
                dve.tensor_tensor(rden_parts[:, UNITS:2 * UNITS], rden[:], rden_r[:].bitcast(F32),
                                  ALU.subtract).then_inc(rden_chain, 1)

            def rows(i, slot):
                dve.wait_ge(rden_turned, SLOTS * i + slot + 1)
                dve.tensor_tensor(rden_rows[:], own_unit[:],
                                  misc_bank[0:2 * UNITS, 0:PAIR].unsqueeze(1).to_broadcast([2 * UNITS, UNITS, PAIR]),
                                  ALU.mult).then_inc(rows_done, 1)

            def scale_out(i, slot, first):
                s = SLOTS * i + slot
                b, h0 = slot // 2, (slot % 2) * 2 * UNITS
                dve.wait_ge(out_copied, s + 1)
                dve.wait_ge(spread_done, s + 1)
                if slot == 0 and not first:
                    dve.wait_ge(proj_done, i)
                dve.tensor_tensor(oT[:, h0:h0 + 2 * UNITS, b * S:(b + 1) * S],
                                  out_sb[:].rearrange("p (h q) -> p h q", q=S),
                                  misc_bank[:, 0:SW].rearrange("p (h q) -> p h q", q=S), ALU.mult).then_inc(oT_done, 1)

            def norm(i, first=False):
                dve.wait_ge(proj_done, i + 1)
                dve.wait_ge(res_loaded, 16 * (i + 1))
                dve.tensor_tensor(z[:], misc_bank[0:PAIR, 0:F], y1_res[:], ALU.add).then_inc(z_done, 1)
                dve.wait_ge(z_done, i + 1)
                norm_stats(dve, z[:], stats[:], mv[:], stat_chain, 2 * i, (const_loaded, 32)).then_inc(var_done, 1)

            def norm_out(i, first=False):
                dve.wait_ge(rstd_done, i + 1)
                if not first:
                    dve.wait_ge(y2_stored, 16 * i)
                dve.tensor_scalar(y2[:], z[:], mv[:, 0:1], mv[:, 1:2], ALU.subtract, ALU.mult).then_inc(y2_done, 1)

            def step(i, n, first, fills=True):
                if fills:
                    scores(i, n, first)
                j, m = pair_of(i, n - TURN_LAG)
                if not (first and n < TURN_LAG) and (fills or n - TURN_LAG < STEPS):
                    p_rest(j, m, first)
                if n % FILLS == FILLS - 1 and fills:
                    shifts(i, n // CH, n % CH // FILLS)
                slot = n // CH
                if n % CH == 5:
                    j, m = i + (slot - 2) // SLOTS, (slot - 2) % SLOTS
                    if not (first and slot < 2) and (fills or slot - 2 < SLOTS):
                        scale_out(j, m, first)
                    j, m = i + (slot - 1) // SLOTS, (slot - 1) % SLOTS
                    if not (first and slot < 1) and (fills or slot - 1 < SLOTS):
                        reciprocals(j, m)
                if n % CH == 8:
                    j, m = i + (slot - 1) // SLOTS, (slot - 1) % SLOTS
                    if not (first and slot < 1) and (fills or slot - 1 < SLOTS):
                        rows(j, m)
                if n == CH + 6 and not first:
                    norm(i - 1)
                if n == CH + 9 and not first:
                    norm_out(i - 1)

            def pair_dve(i, first=False):
                q_rest(i)
                for n in range(STEPS):
                    step(i, n, first)

            pair_dve(0, first=True)
            with dve.Fori(1, NPAIR) as i:
                pair_dve(i)
            for n in range(STEPS, STEPS + CH + 6):
                step(NPAIR - 1, n, False, fills=False)
            norm(NPAIR - 1)
            norm_out(NPAIR - 1)

        @block.gpsimd
        def _(pool):
            pool.wait_ge(const_set, 1)

            def split_cT(i, b, first):
                n = 2 * i + b
                waits = [(cT_loaded, 16 * (n + 1))]
                if not first:
                    waits.append((fill_done, 2 * CH * (n - 1)))
                wait_apart(pool, (const_set, 1), *waits)
                pool.tensor_copy(cT_hi[:, b, :], cT_in[:]).then_inc(cT_split, 1)
                pool.wait_ge(cT_split, 2 * n + 1)
                pool.tensor_tensor(cT_lo[:, b, :], cT_in[:], cT_hi[:, b, :].bitcast(F32),
                                   ALU.subtract).then_inc(cT_split, 1)

            def mask_bias(i, b, first):
                n = 2 * i + b
                waits = [(mask_loaded, 16 * (n + 1))]
                if not first:
                    waits.append((fill_taken, 2 * CH * (n - 1)))
                wait_apart(pool, (const_set, 1), *waits)
                pool.tensor_scalar(mask_add[:, b, :], mask_in[:], BIG, -BIG, ALU.mult, ALU.add).then_inc(mask_ready, 1)

            def split_c(i, b, first):
                n = 2 * i + b
                waits = [(c_loaded, 16 * (n + 1))]
                if not first:
                    waits.append((pv_done, 2 * CH * (n - 1)))
                wait_apart(pool, (const_set, 1), *waits)
                pool.tensor_copy(c_hi[:, b, :], c_in[:]).then_inc(c_split, 1)
                pool.wait_ge(c_split, 2 * n + 1)
                pool.tensor_tensor(c_lo[:, b, :], c_in[:], c_hi[:, b, :].bitcast(F32),
                                   ALU.subtract).then_inc(c_split, 1)

            def rstd(i):
                pool.wait_ge(var_done, i + 1)
                pool.tensor_tensor(mv[:, 1:2], mv[:, 1:2], half[:], ALU.pow).then_inc(rstd_done, 1)

            def batch(i, b, first):
                split_cT(i, b, first)
                mask_bias(i, b, first)
                split_c(i, b, first)

            for b in range(2):
                batch(0, b, True)
            with pool.Fori(1, NPAIR) as i:
                batch(i, 0, False)
                batch(i, 1, False)
                rstd(i - 1)
            rstd(NPAIR - 1)


def phase_c(nc, D):
    with ExitStack() as ctx:
        def sb(name, shape, dt=F32):
            return ctx.enter_context(nc.sbuf_tensor("c_" + name, shape, dt))

        def sem(name):
            return ctx.enter_context(nc.semaphore("c_" + name))

        def ps(name):
            return ctx.enter_context(nc.psum_tensor("c_" + name, [128, 512], F32))

        gate_bank = [ps(f"gate{j}") for j in range(2)]
        up_bank = [ps(f"up{j}") for j in range(2)]
        comb_bank = [ps(f"comb{j}") for j in range(2)]
        down_bank = [ps(f"down{j}") for j in range(2)]

        w_gate = sb("w_gate", [128, KC, IW])
        w_up = sb("w_up", [128, KC, IW])
        w_down = sb("w_down", [128, IC, F])
        w_route = sb("w_route", [128, KC, NR])
        owner = sb("owner", [NR, IW])
        ident = sb("ident", [128, 128])
        rank = sb("rank", [PAIR, TILES, EXPERTS])
        half = sb("half", [PAIR, 1])
        y2 = sb("y2", [PAIR, TILES, F])
        y2T = sb("y2T", [128, KC, BLK])
        logit = sb("logit", [PAIR, TILES, NR])
        ex = sb("ex", [PAIR, TILES, NR])
        best = sb("best", [PAIR, 2, TILES])
        rest = sb("rest", [PAIR, TILES, EXPERTS])
        pick = sb("pick", [PAIR, 2, TILES, EXPERTS])
        first_of = sb("first_of", [PAIR, TILES])
        combine = sb("combine", [PAIR, TILES, NR])
        total = sb("total", [PAIR, TILES])
        combT = sb("combT", [NR, BLK])
        act_g = sb("act_g", [128, 2, BLK])
        act_gu = sb("act_gu", [128, 2, BLK])
        h = sb("h", [128, 2, BLK])
        sumT = sb("sumT", [128, KC, BLK])
        z = sb("z", [PAIR, TILES, F])
        y = sb("y", [PAIR, TILES, F])
        stats = sb("stats", [PAIR, TILES, 6])
        mv = sb("mv", [PAIR, TILES, 2])

        loaded, y2_loaded, half_set = sem("loaded"), sem("y2_loaded"), sem("half_set")
        y2_turned, y2T_done, route_done = sem("y2_turned"), sem("y2T_done"), sem("route_done")
        route_chain, ex_done, combine_done = sem("route_chain"), sem("ex_done"), sem("combine_done")
        comb_turned, combT_done = sem("comb_turned"), sem("combT_done")
        gate_done, up_done, comb_done = sem("gate_done"), sem("up_done"), sem("comb_done")
        silu_done, gu_done, h_done, down_done = sem("silu_done"), sem("gu_done"), sem("h_done"), sem("down_done")
        sumT_done, sum_turned, z_done = sem("sumT_done"), sem("sum_turned"), sem("z_done")
        stat_chain, var_done, rstd_done = sem("stat_chain"), sem("var_done"), sem("rstd_done")
        y_done, y_stored = sem("y_done"), sem("y_stored")
        LOADS = 4 + 2 + 3 + 5
        LOGITS = 4
        CHAIN = LOGITS + 17

        def rows_of(c):
            return min(128, IW - 128 * c)

        block = ctx.enter_context(nc.Block())

        @block.sync
        def _(sp):
            def inc(ins):
                ins.then_inc(loaded, 16)
            moe = EXPERTS * I_MOE
            gu = D["gate_up"]
            for kc in range(KC):
                inc(sp.dma_start(w_gate[:, kc, 0:moe].rearrange("p (e n) -> p e n", e=EXPERTS), gu[:, kc, :, 0:I_MOE]))
                inc(sp.dma_start(w_up[:, kc, 0:moe].rearrange("p (e n) -> p e n", e=EXPERTS), gu[:, kc, :, I_MOE:]))
            inc(sp.dma_start(w_gate[:, :, moe:], D["sh_gate"]))
            inc(sp.dma_start(w_up[:, :, moe:], D["sh_up"]))
            mc, sc = moe // 128, I_SH // 128
            inc(sp.dma_start(w_down[:, 0:mc, :], D["down"].rearrange("(c p) n -> p c n", p=128)))
            inc(sp.dma_start(w_down[:, mc:mc + sc, :], D["sh_down"][0:sc * 128].rearrange("(c p) n -> p c n", p=128)))
            inc(sp.dma_start(w_down[0:I_SH - sc * 128, mc + sc, :], D["sh_down"][sc * 128:]))
            inc(sp.dma_start(w_route[:, :, 0:EXPERTS], D["route_w"]))
            inc(sp.dma_start(w_route[:, :, EXPERTS:NR], D["route_sh"], allow_slow_non_contiguous=True))
            inc(sp.dma_start(owner[:], D["owner"]))
            inc(sp.dma_start(ident[:], D["ident"]))
            inc(sp.dma_start(rank[:], D["rank"]))

            def block_io(i, first=False):
                if not first:
                    sp.wait_ge(z_done, TILES * i)
                sp.dma_start(y2[:], D["y2"][:, bass.ts(i, TILES), :]).then_inc(y2_loaded, 16)
                for t in range(TILES):
                    sp.wait_ge(y_done, TILES * i + t + 1)
                    sp.dma_start(D["out"][:, bass.ds(i * TILES + t, 1), :], y[:, t:t + 1]).then_inc(y_stored, 16)

            block_io(0, first=True)
            with sp.Fori(1, NBLK) as i:
                block_io(i)
            sp.wait_ge(y_stored, 16 * NPAIR)

        @block.tensor
        def _(pe):
            pe.wait_ge(loaded, 16 * LOADS)

            def block_pe(i, first=False):
                pe.wait_ge(y2_loaded, 16 * (i + 1))
                if not first:
                    pe.wait_ge(z_done, TILES * i)
                for kc in range(KC):
                    for t in range(TILES):
                        mm = pe.transpose(gate_bank[kc][:, t * PAIR:(t + 1) * PAIR], y2[:, t, kc * 128:(kc + 1) * 128],
                                          ident[0:PAIR, 0:PAIR])
                    mm.then_inc(y2_turned, 1)
                pe.wait_ge(y2T_done, KC * (i + 1))
                for t in range(TILES):
                    for kc in range(KC):
                        mm = pe.matmul(up_bank[0][0:PAIR, t * NR:(t + 1) * NR], y2T[:, kc, t * PAIR:(t + 1) * PAIR],
                                       w_route[:, kc, :], start=(kc == 0), stop=(kc == KC - 1))
                mm.then_inc(route_done, 1)
                pe.wait_ge(combine_done, 2 * (i + 1))
                for t in range(TILES):
                    mm = pe.transpose(up_bank[1][0:NR, t * PAIR:(t + 1) * PAIR], combine[:, t, :], ident[0:PAIR, 0:PAIR])
                mm.then_inc(comb_turned, 1)
                pe.wait_ge(combT_done, i + 1)

                def hidden(c):
                    m, k = rows_of(c), c % 2
                    cols = slice(128 * c, 128 * c + m)
                    if c >= 2:
                        pe.wait_ge(silu_done, IC * i + c - 1)
                    for kc in range(KC):
                        mm = pe.matmul(gate_bank[k][0:m, 0:BLK], w_gate[:, kc, cols], y2T[:, kc, :],
                                       start=(kc == 0), stop=(kc == KC - 1))
                    mm.then_inc(gate_done, 1)
                    if c >= 2:
                        pe.wait_ge(gu_done, IC * i + c - 1)
                    for kc in range(KC):
                        mm = pe.matmul(up_bank[k][0:m, 0:BLK], w_up[:, kc, cols], y2T[:, kc, :],
                                       start=(kc == 0), stop=(kc == KC - 1))
                    mm.then_inc(up_done, 1)
                    if c >= 2:
                        pe.wait_ge(h_done, IC * i + c - 1)
                    elif not first:
                        pe.wait_ge(h_done, IC * i)
                    pe.matmul(comb_bank[k][0:m, 0:BLK], owner[:, cols], combT[:], start=True, stop=True).then_inc(comb_done, 1)

                def down(c):
                    m = rows_of(c)
                    pe.wait_ge(h_done, IC * i + c + 1)
                    if c == 0 and not first:
                        pe.wait_ge(sumT_done, KC * i)
                    for f in range(KC):
                        mm = pe.matmul(down_bank[f][:, 0:BLK], w_down[0:m, c, f * 128:(f + 1) * 128], h[0:m, c % 2, :],
                                       start=(c == 0), stop=(c == IC - 1))
                    mm.then_inc(down_done, 1)

                for c in range(IC + 1):
                    if c < IC:
                        hidden(c)
                    if c >= 1:
                        down(c - 1)
                pe.wait_ge(sumT_done, KC * (i + 1))
                for t in range(TILES):
                    for f in range(KC):
                        mm = pe.transpose((gate_bank + up_bank)[t][0:PAIR, f * 128:(f + 1) * 128],
                                          sumT[:, f, t * PAIR:(t + 1) * PAIR], ident[:])
                    mm.then_inc(sum_turned, 1)

            block_pe(0, first=True)
            with pe.Fori(1, NBLK) as i:
                block_pe(i)

        @block.scalar
        def _(act):
            def block_act(i):
                for kc in range(KC):
                    act.wait_ge(y2_turned, KC * i + kc + 1)
                    act.copy(y2T[:, kc, :], gate_bank[kc][:, 0:BLK]).then_inc(y2T_done, 1)
                act.wait_ge(route_chain, CHAIN * i + LOGITS)
                act.activation(ex[:], logit[:], ACT.Exp).then_inc(ex_done, 1)
                act.wait_ge(comb_turned, i + 1)
                act.copy(combT[:], up_bank[1][0:NR, 0:BLK]).then_inc(combT_done, 1)
                for c in range(IC):
                    m = rows_of(c)
                    act.wait_ge(gate_done, IC * i + c + 1)
                    if c >= 2:
                        act.wait_ge(gu_done, IC * i + c - 1)
                    act.activation(act_g[0:m, c % 2, :], gate_bank[c % 2][0:m, 0:BLK], ACT.Silu).then_inc(silu_done, 1)
                for f in range(KC):
                    act.wait_ge(down_done, IC * (i + 1))
                    act.copy(sumT[:, f, :], down_bank[f][:, 0:BLK]).then_inc(sumT_done, 1)

            block_act(0)
            with act.Fori(1, NBLK) as i:
                block_act(i)

        @block.vector
        def _(dve):
            dve.memset(half[:], -0.5).then_inc(half_set, 1)
            dve.wait_ge(loaded, 16 * LOADS)

            def block_dve(i, first=False):
                steps = 0

                def link(ins):
                    nonlocal steps
                    steps += 1
                    ins.then_inc(route_chain, 1)
                    dve.wait_ge(route_chain, CHAIN * i + steps)

                def wide(ap):
                    return ap.unsqueeze(2).to_broadcast([PAIR, TILES, EXPERTS])

                logits, exps = logit[:, :, 0:EXPERTS], ex[:, :, 0:EXPERTS]
                dve.wait_ge(route_done, i + 1)
                link(dve.tensor_copy(logit[:], up_bank[0][0:PAIR, 0:TILES * NR].rearrange("p (t n) -> p t n", t=TILES)))
                link(dve.tensor_reduce(best[:, 0, :], logits, AX.X, ALU.max))
                link(dve.tensor_scalar(logit[:, :, EXPERTS:NR], logit[:, :, EXPERTS:NR], -1.0, None, ALU.mult))
                link(dve.tensor_tensor(logits, logits, wide(best[:, 0, :]), ALU.subtract))
                assert steps == LOGITS
                dve.wait_ge(ex_done, i + 1)
                for k in range(2):
                    src = exps if k == 0 else rest[:]
                    link(dve.tensor_reduce(best[:, k, :], src, AX.X, ALU.max))
                    link(dve.tensor_tensor(pick[:, k], src, wide(best[:, k, :]), ALU.is_equal))
                    link(dve.tensor_tensor(pick[:, k], pick[:, k], rank[:], ALU.mult))
                    link(dve.tensor_reduce(first_of[:], pick[:, k], AX.X, ALU.max))
                    link(dve.tensor_tensor(pick[:, k], rank[:], wide(first_of[:]), ALU.is_equal))
                    if k == 0:
                        link(dve.tensor_scalar(rest[:], pick[:, 0], -2.0, None, ALU.mult))
                        link(dve.tensor_tensor(rest[:], rest[:], exps, ALU.add))
                link(dve.tensor_tensor(pick[:, 0], pick[:, 0], pick[:, 1], ALU.add))
                link(dve.tensor_tensor(pick[:, 0], pick[:, 0], exps, ALU.mult))
                link(dve.tensor_reduce(total[:], pick[:, 0], AX.X, ALU.add))
                link(dve.reciprocal(total[:], total[:]))
                link(dve.tensor_scalar(ex[:, :, EXPERTS:NR], ex[:, :, EXPERTS:NR], 1.0, None, ALU.add))
                if not first:
                    dve.wait_ge(comb_turned, i)
                dve.reciprocal(combine[:, :, EXPERTS:NR], ex[:, :, EXPERTS:NR]).then_inc(combine_done, 1)
                dve.tensor_tensor(combine[:, :, 0:EXPERTS], pick[:, 0], wide(total[:]), ALU.mult).then_inc(combine_done, 1)
                assert steps == CHAIN

                for c in range(IC):
                    m, k, n = rows_of(c), c % 2, IC * i + c
                    dve.wait_ge(silu_done, n + 1)
                    dve.wait_ge(up_done, n + 1)
                    dve.tensor_tensor(act_gu[0:m, k, :], up_bank[k][0:m, 0:BLK], act_g[0:m, k, :], ALU.mult).then_inc(gu_done, 1)
                    dve.wait_ge(gu_done, n + 1)
                    dve.wait_ge(comb_done, n + 1)
                    if c >= 2:
                        dve.wait_ge(down_done, n - 1)
                    dve.tensor_tensor(h[0:m, k, :], comb_bank[k][0:m, 0:BLK], act_gu[0:m, k, :], ALU.mult).then_inc(h_done, 1)
                for t in range(TILES):
                    n = TILES * i + t
                    dve.wait_ge(sum_turned, n + 1)
                    dve.tensor_tensor(z[:, t, :], (gate_bank + up_bank)[t][0:PAIR, 0:F], y2[:, t, :], ALU.add).then_inc(z_done, 1)
                    dve.wait_ge(z_done, n + 1)
                    norm_stats(dve, z[:, t, :], stats[:, t, :], mv[:, t, :], stat_chain, 2 * n, (loaded, 16)).then_inc(var_done, 1)
                for t in range(TILES):
                    n = TILES * i + t
                    dve.wait_ge(rstd_done, n + 1)
                    if not first:
                        dve.wait_ge(y_stored, 16 * (n - TILES + 1))
                    dve.tensor_scalar(y[:, t, :], z[:, t, :], mv[:, t, 0:1], mv[:, t, 1:2],
                                      ALU.subtract, ALU.mult).then_inc(y_done, 1)

            block_dve(0, first=True)
            with dve.Fori(1, NBLK) as i:
                block_dve(i)

        @block.gpsimd
        def _(pool):
            pool.wait_ge(half_set, 1)

            def block_pool(i):
                for t in range(TILES):
                    pool.wait_ge(var_done, TILES * i + t + 1)
                    pool.tensor_tensor(mv[:, t, 1:2], mv[:, t, 1:2], half[:], ALU.pow).then_inc(rstd_done, 1)

            block_pool(0)
            with pool.Fori(1, NBLK) as i:
                block_pool(i)


def decoder_layer(nc, D):
    with ExitStack() as ctx:
        A_fold = ctx.enter_context(nc.sbuf_tensor("A_fold", [128, XH, F], F32))
        M_fold = ctx.enter_context(nc.sbuf_tensor("M_fold", [128, XH, F], F32))
        phase_a(nc, D, A_fold, M_fold)
        phase_b(nc, D, A_fold, M_fold)
    phase_c(nc, D)


def layouts(x, ctx_1024, mask_BxS2_bf1, L0_attn_Wq, L0_attn_bq, L0_attn_Wk, L0_attn_bk, L0_attn_Wv, L0_attn_bv,
            L0_attn_Wo, L0_attn_bo, L0_xattn_Wq, L0_xattn_Wk, L0_xattn_Wv, L0_xattn_Wo, L0_ffn_router_weight,
            L0_ffn_gate_up_proj, L0_ffn_down_proj, L0_ffn_sh_gate_w, L0_ffn_sh_up_w, L0_ffn_sh_down_w,
            L0_ffn_shared_gate_w):
    def rows(w):
        return w.reshape(KC, 128, -1).transpose(1, 0, 2)

    tokens = x.reshape(NPAIR, PAIR, F)
    moe = L0_ffn_gate_up_proj.transpose(2, 0, 1).reshape(KC, 128, EXPERTS, 2 * I_MOE)
    return {
        "x": tokens.transpose(1, 0, 2),
        "xT": rows(x.reshape(B * S, F).T),
        "ctx": ctx_1024.reshape(B, CK, CH * CD),
        "ctxT": ctx_1024.reshape(B, CK, CH, CD).transpose(0, 3, 2, 1).reshape(B, CD, CTX),
        "mask": mask_BxS2_bf1.view(np.uint8).reshape(B, CK, CH).transpose(0, 2, 1).reshape(B, CTX),
        "wq": rows(L0_attn_Wq), "wk": rows(L0_attn_Wk), "wv": rows(L0_attn_Wv), "wo": rows(L0_attn_Wo),
        "bq": L0_attn_bq.reshape(KC, 128).T, "bk": L0_attn_bk.reshape(KC, 128).T,
        "bv": L0_attn_bv, "bo": L0_attn_bo,
        "xwqT": L0_xattn_Wq.reshape(F, XH, 128).transpose(2, 1, 0),
        "xwkT": L0_xattn_Wk.reshape(CD, XKV, 128).transpose(2, 1, 0),
        "xwvT": L0_xattn_Wv.reshape(CD, XKV, 128).transpose(2, 1, 0),
        "xwo": L0_xattn_Wo.reshape(XH, 128, F).transpose(1, 0, 2),
        "gate_up": moe.transpose(1, 0, 2, 3),
        "sh_gate": rows(L0_ffn_sh_gate_w.T), "sh_up": rows(L0_ffn_sh_up_w.T),
        "down": L0_ffn_down_proj.transpose(0, 2, 1).reshape(EXPERTS * I_MOE, F),
        "sh_down": L0_ffn_sh_down_w.T,
        "route_w": rows(L0_ffn_router_weight.T), "route_sh": rows(L0_ffn_shared_gate_w.T),
    }


def constants():
    f = np.float32
    own_q = np.zeros((2, PAIR), f)
    own_q[0, :S] = own_q[1, S:] = 1
    other_k = np.zeros((2, SA_HEADS, PAIR), f)
    other_k[0, :, S:] = other_k[1, :, :S] = -BIG
    own_unit = np.zeros((2 * UNITS, UNITS, PAIR), f)
    owner = np.zeros((NR, IW), f)
    for n in range(IW):
        owner[min(n // I_MOE, EXPERTS), n] = 1
    for r in range(2 * UNITS):
        own_unit[r, r % UNITS] = 1
    rank = np.broadcast_to(np.arange(EXPERTS, 0, -1, dtype=f), (PAIR, TILES, EXPERTS))
    return {"ident": np.eye(128, dtype=f), "own_q": own_q, "other_k": other_k.reshape(2, -1),
            "own_unit": own_unit, "owner": owner, "rank": rank}


def kernel(**inputs):
    import concourse.bacc as bacc
    from concourse.bass_utils import run_bass_kernel_spmd

    nc = bacc.Bacc("TRN2", target_bir_lowering=False, num_devices=1)
    arrays, D = {}, {}
    for name, a in {**layouts(**{k: np.asarray(v) for k, v in inputs.items()}), **constants()}.items():
        a = np.ascontiguousarray(a)
        arrays["in_" + name] = a
        D[name] = nc.dram_tensor("in_" + name, a.shape, mybir.dt.from_np(a.dtype), kind="ExternalInput").ap()
    D["y1"] = nc.dram_tensor("y1_store", (PAIR, NPAIR, F), F32, kind="Internal").ap()
    D["y2"] = nc.dram_tensor("y2_store", (PAIR, NPAIR, F), F32, kind="Internal").ap()
    D["out"] = nc.dram_tensor("out", (PAIR, NPAIR, F), F32, kind="ExternalOutput").ap()
    decoder_layer(nc, D)
    r = run_bass_kernel_spmd(nc, [arrays], core_ids=[0])
    return r.results[0]["out"].transpose(1, 0, 2).reshape(B, S, F)
```

```python
from contextlib import ExitStack

import numpy as np

import concourse.bass as bass
from concourse import mybir

ALU = mybir.AluOpType
ACT = mybir.ActivationFunctionType
AX = mybir.AxisListType
F32 = mybir.dt.float32
F32R = mybir.dt.float32r
BF16 = mybir.dt.bfloat16
U8 = mybir.dt.uint8

B, S, F = 32, 56, 256
KC = F // 128
PAIR = 2 * S
NPAIR = B // 2
TILES = 4
BLK = TILES * PAIR
NBLK = NPAIR // TILES
SA_HEADS, SA_D = 4, 64
SA_SCALE = 1.0 / np.sqrt(F // 64)
CTX, CD = 1500, 128
XH, XKV = 16, 8
X_SCALE = 1.0 / np.sqrt(128.0)
CH = 12
CK = CTX // CH
FILLS = 3
FW = CTX // FILLS
ROWS = XH * S
UNITS = (4, 3)
SLOTS = 4
WIDE = UNITS[0] * 128
EXPERTS, I_MOE, I_SH = 8, 176, 704
NR = EXPERTS + 1
IW = EXPERTS * I_MOE + I_SH
IC = -(-IW // 128)
EPS = 1e-5
BIG = 1e30


def wait_apart(engine, held, *waits):
    for semaphore, count in waits[:-1]:
        engine.wait_ge(semaphore, count)
    semaphore, count = waits[-1]
    if not isinstance(count, int):
        with engine.register() as own:
            engine.reg_add(own, count - 1, 1)
            engine.wait_ge(*held)
            engine.wait_ge(semaphore, own)
    else:
        engine.wait_ge(semaphore, count)


def norm_stats(dve, z, stats, mv, chain, count, done):
    dve.bn_stats(out=stats, in_=z).then_inc(chain, 1)
    wait_apart(dve, done, (chain, count + 1))
    dve.bn_aggr(out=mv, in_=stats).then_inc(chain, 1)
    dve.wait_ge(chain, count + 2)
    return dve.tensor_scalar(mv[:, 1:2], mv[:, 1:2], EPS, None, ALU.add)


def phase_a(nc, D, A_hi, A_lo, M_fold):
    with ExitStack() as ctx:
        def sb(name, shape, dt=F32):
            return ctx.enter_context(nc.sbuf_tensor(name, shape, dt))

        def sem(name):
            return ctx.enter_context(nc.semaphore("a_" + name))

        bank = [ctx.enter_context(nc.psum_tensor(f"a_bank{j}", [128, 512], F32)) for j in range(8)]

        wqT = sb("a_wqT", [128, XH, F])
        wkT = sb("a_wkT", [128, XKV, CD])
        wvT = sb("a_wvT", [128, XKV, CD])
        wo = sb("a_wo", [128, XH, F])
        saw = sb("a_saw", [128, 4, KC, F])
        bqk = sb("a_bqk", [128, 2, KC])
        bv = sb("a_bv", [PAIR, F])
        bo = sb("a_bo", [PAIR, F])
        ident = sb("a_ident", [128, 128])
        own_q = sb("a_own_q", [2, PAIR])
        other_k = sb("a_other_k", [2, SA_HEADS * PAIR])
        xT = sb("a_xT", [128, KC, BLK])
        x = sb("a_x", [PAIR, TILES, F])
        xb = sb("a_xb", [PAIR, TILES, F])
        qT = sb("a_qT", [128, KC, BLK])
        kT = sb("a_kT", [128, 2, KC, BLK])
        v = sb("a_v", [PAIR, TILES, F])
        e = sb("a_e", [PAIR, TILES, SA_HEADS, PAIR])
        eT = sb("a_eT", [PAIR, TILES, SA_HEADS * PAIR])
        oT = sb("a_oT", [128, TILES, KC, PAIR])
        mx = sb("a_mx", [PAIR, TILES, SA_HEADS])
        shift = sb("a_shift", [PAIR, TILES, SA_HEADS])
        den = sb("a_den", [PAIR, TILES, SA_HEADS])
        rden = sb("a_rden", [PAIR, TILES, SA_HEADS])
        z = sb("a_z", [PAIR, TILES, F])
        y = sb("a_y", [PAIR, TILES, F])
        stats = sb("a_stats", [PAIR, TILES, 6])
        mv = sb("a_mv", [PAIR, TILES, 2])
        half = sb("a_half", [PAIR, 1])
        yT_hi = sb("a_yT_hi", [128, TILES, KC, PAIR], F32R)
        yT_lo = sb("a_yT_lo", [128, TILES, KC, PAIR], F32R)

        fold_loaded, loaded, x_loaded = sem("fold_loaded"), sem("loaded"), sem("x_loaded")
        folded, fold_taken, fold_rest = sem("folded"), sem("fold_taken"), sem("fold_rest")
        y_turned, yT_hi_done, yT_lo_done, yT_stored = sem("y_turned"), sem("yT_hi_done"), sem("yT_lo_done"), sem("yT_stored")
        half_set = sem("half_set")
        qk_done, qk_taken = sem("qk_done"), sem("qk_taken")
        v_done, v_taken = sem("v_done"), sem("v_taken")
        xb_done, s_done = sem("xb_done"), sem("s_done")
        max_done, shift_done, e_done = sem("max_done"), sem("shift_done"), sem("e_done")
        rden_done, e_normed = sem("rden_done"), sem("e_normed")
        eT_done, eT_taken = sem("eT_done"), sem("eT_taken")
        o_done, o_taken = sem("o_done"), sem("o_taken")
        p_done, z_done = sem("p_done"), sem("z_done")
        stat_chain, var_done, rstd_done = sem("stat_chain"), sem("var_done"), sem("rstd_done")
        y_done, y_stored = sem("y_done"), sem("y_stored")

        FOLDS = XH

        block = ctx.enter_context(nc.Block())

        @block.sync
        def _(sp):
            for dst, src in ((wqT, D["xwqT"]), (wkT, D["xwkT"]), (wvT, D["xwvT"]), (wo, D["xwo"])):
                sp.dma_start(dst[:], src).then_inc(fold_loaded, 16)
            for n, name in enumerate(("wq", "wk", "wv", "wo")):
                sp.dma_start(saw[:, n], D[name]).then_inc(loaded, 16)
            sp.dma_start(bqk[:, 0], D["bq"]).then_inc(loaded, 16)
            sp.dma_start(bqk[:, 1], D["bk"]).then_inc(loaded, 16)
            sp.dma_start(bv[:], D["bv"].partition_broadcast(PAIR)).then_inc(loaded, 16)
            sp.dma_start(bo[:], D["bo"].partition_broadcast(PAIR)).then_inc(loaded, 16)
            sp.dma_start(ident[:], D["ident"]).then_inc(loaded, 16)
            sp.dma_start(own_q[:], D["own_q"]).then_inc(loaded, 16)
            sp.dma_start(other_k[:], D["other_k"]).then_inc(loaded, 16)

            def block_io(i, first=False):
                if not first:
                    sp.wait_ge(v_done, 2 * i)
                    sp.wait_ge(xb_done, i)
                sp.dma_start(xT[:], D["xT"][:, :, bass.ts(i, BLK)]).then_inc(x_loaded, 16)
                sp.dma_start(x[:], D["x"][:, bass.ts(i, TILES), :]).then_inc(x_loaded, 16)
                for t in range(TILES):
                    sp.wait_ge(y_done, TILES * i + t + 1)
                    sp.dma_start(D["y1"][:, bass.ds(i * TILES + t, 1), :], y[:, t:t + 1]).then_inc(y_stored, 16)
                sp.wait_ge(yT_lo_done, TILES * (i + 1))
                sp.dma_start(D["y1T_hi"][:, bass.ts(i, TILES)], yT_hi[:].bitcast(F32)).then_inc(yT_stored, 16)
                sp.dma_start(D["y1T_lo"][:, bass.ts(i, TILES)], yT_lo[:].bitcast(F32)).then_inc(yT_stored, 16)

            block_io(0, first=True)
            with sp.Fori(1, NBLK) as i:
                block_io(i)
            sp.wait_ge(y_stored, 16 * NPAIR)
            sp.wait_ge(yT_stored, 32 * NBLK)

        @block.tensor
        def _(pe):
            pe.wait_ge(fold_loaded, 64)
            for n in range(FOLDS):
                if n >= 8:
                    pe.wait_ge(fold_rest, n - 7)
                for k in range(2):
                    h = 2 * (n % 8) + k
                    out = bank[n % 8][:, k * F:(k + 1) * F]
                    if n < 8:
                        for kc in range(KC):
                            mm = pe.matmul(out[:, kc * 128:(kc + 1) * 128], wqT[:, h, kc * 128:(kc + 1) * 128],
                                           wkT[:, h // 2, :], start=True, stop=True)
                    else:
                        mm = pe.matmul(out, wvT[:, h // 2, :], wo[:, h, :], start=True, stop=True)
                mm.then_inc(folded, 1)
            pe.wait_ge(loaded, 16 * 11)
            pe.wait_ge(fold_taken, FOLDS)
            pe.wait_ge(half_set, 3)

            def block_pe(i, first=False):
                pe.wait_ge(x_loaded, 32 * (i + 1))
                if not first:
                    pe.wait_ge(o_taken, 2 * TILES * i)
                for n in range(4):
                    for kc in range(KC):
                        mm = pe.matmul(bank[n][:, 0:BLK], saw[:, n // 2, kc, (n % 2) * 128:(n % 2 + 1) * 128],
                                       xT[:, kc, :], start=(kc == 0), stop=(kc == KC - 1))
                    mm.then_inc(qk_done, 1)
                if not first:
                    pe.wait_ge(yT_lo_done, TILES * i)
                for t in range(TILES):
                    for kc in range(KC):
                        mm = pe.matmul(bank[4 + t // 2][0:PAIR, (t % 2) * F:(t % 2 + 1) * F],
                                       xT[:, kc, t * PAIR:(t + 1) * PAIR], saw[:, 2, kc, :],
                                       start=(kc == 0), stop=(kc == KC - 1))
                    if t % 2:
                        mm.then_inc(v_done, 1)
                pe.wait_ge(qk_taken, 6 * (i + 1))
                for t in range(TILES):
                    sc = bank[t][0:PAIR, 0:SA_HEADS * PAIR]
                    for h in range(SA_HEADS):
                        mm = pe.matmul(sc[:, h * PAIR:(h + 1) * PAIR],
                                       qT[:, h // 2, t * PAIR:(t + 1) * PAIR],
                                       kT[:, h % 2, h // 2, t * PAIR:(t + 1) * PAIR],
                                       start=(h == 0), stop=False, skip_group_check=True)
                    pe.matmul(sc, own_q[:], other_k[:], start=False, stop=True, skip_group_check=True).then_inc(s_done, 1)
                pe.wait_ge(v_taken, 2 * (i + 1))
                for t in range(TILES):
                    pe.wait_ge(e_normed, TILES * i + t + 1)
                    for h in range(SA_HEADS):
                        mm = pe.transpose(bank[4 + t][0:PAIR, h * PAIR:(h + 1) * PAIR], e[:, t, h, :],
                                          ident[0:PAIR, 0:PAIR])
                    mm.then_inc(eT_done, 1)
                for t in range(TILES):
                    pe.wait_ge(eT_taken, TILES * i + t + 1)
                    for m in range(KC):
                        mm = pe.matmul(bank[t][:, m * 2 * PAIR:(m + 1) * 2 * PAIR], v[:, t, m * 128:(m + 1) * 128],
                                       eT[:, t, m * 2 * PAIR:(m + 1) * 2 * PAIR], start=True, stop=True)
                    mm.then_inc(o_done, 1)
                for t in range(TILES):
                    pe.wait_ge(o_taken, 2 * (TILES * i + t + 1))
                    for m in range(KC):
                        mm = pe.matmul(bank[4 + t][0:PAIR, 0:F], oT[:, t, m, :], saw[:, 3, m, :],
                                       start=(m == 0), stop=(m == KC - 1))
                    mm.then_inc(p_done, 1)
                for t in range(TILES):
                    pe.wait_ge(y_done, TILES * i + t + 1)
                    for kc in range(KC):
                        mm = pe.transpose(bank[4 + t][:, kc * PAIR:(kc + 1) * PAIR], y[:, t, kc * 128:(kc + 1) * 128],
                                          ident[0:PAIR, 0:PAIR])
                    mm.then_inc(y_turned, 1)

            block_pe(0, first=True)
            with pe.Fori(1, NBLK) as i:
                block_pe(i)

        @block.scalar
        def _(act):
            for n in range(FOLDS):
                act.wait_ge(folded, n + 1)
                dst = (A_hi if n < 8 else M_fold)[:, 2 * (n % 8):2 * (n % 8) + 2, :]
                act.copy(dst, bank[n % 8][:].rearrange("p (a n) -> p a n", a=2)).then_inc(fold_taken, 1)
            act.wait_ge(loaded, 16 * 11)

            def block_act(i, first=False):
                for m in range(KC):
                    act.wait_ge(qk_done, 4 * i + m + 1)
                    act.activation(qT[:, m, :], bank[m][:, 0:BLK], ACT.Identity,
                                   bias=bqk[:, 0, m:m + 1]).then_inc(qk_taken, 1)
                for m in range(KC):
                    act.wait_ge(qk_done, 4 * i + KC + m + 1)
                    for k in range(2):
                        own = slice(SA_D * k, SA_D * (k + 1))
                        act.activation(kT[own, k, m, :], bank[KC + m][own, 0:BLK], ACT.Identity,
                                       bias=bqk[own, 1, m:m + 1]).then_inc(qk_taken, 1)
                for t in range(TILES):
                    act.wait_ge(shift_done, TILES * i + t + 1)
                    for h in range(SA_HEADS):
                        act.activation(e[:, t, h, :], bank[t][0:PAIR, h * PAIR:(h + 1) * PAIR], ACT.Exp,
                                       bias=shift[:, t, h:h + 1], scale=float(SA_SCALE),
                                       accum_out=den[:, t, h:h + 1]).then_inc(e_done, 1)
                for t in range(TILES):
                    act.wait_ge(eT_done, TILES * i + t + 1)
                    act.copy(eT[:, t, :], bank[4 + t][0:PAIR, 0:SA_HEADS * PAIR]).then_inc(eT_taken, 1)
                for t in range(TILES):
                    act.wait_ge(y_turned, TILES * i + t + 1)
                    if not first:
                        act.wait_ge(yT_stored, 32 * i)
                    act.copy(yT_hi[:, t].rearrange("p k q -> p (k q)"), bank[4 + t][:, 0:KC * PAIR]).then_inc(yT_hi_done, 1)

            block_act(0, first=True)
            with act.Fori(1, NBLK) as i:
                block_act(i)

        @block.vector
        def _(dve):
            dve.memset(half[:], -0.5).then_inc(half_set, 1)
            dve.memset(kT[SA_D:, 0], 0.0).then_inc(half_set, 1)
            dve.memset(kT[:SA_D, 1], 0.0).then_inc(half_set, 1)
            for n in range(8):
                dve.wait_ge(fold_taken, n + 1)
                part = (slice(None), slice(2 * n, 2 * n + 2))
                dve.tensor_tensor(A_lo[part], bank[n][:].rearrange("p (a n) -> p a n", a=2),
                                  A_hi[part].bitcast(F32), ALU.subtract).then_inc(fold_rest, 1)
            dve.wait_ge(loaded, 16 * 11)

            def block_dve(i, first=False):
                for n in range(2):
                    dve.wait_ge(v_done, 2 * i + n + 1)
                    dve.tensor_tensor(v[:, 2 * n:2 * n + 2, :],
                                      bank[4 + n][0:PAIR, :].rearrange("p (t f) -> p t f", t=2),
                                      bv[:].unsqueeze(1).to_broadcast([PAIR, 2, F]), ALU.add).then_inc(v_taken, 1)
                for t in range(TILES):
                    dve.wait_ge(s_done, TILES * i + t + 1)
                    dve.tensor_reduce(mx[:, t, :], bank[t][0:PAIR, 0:SA_HEADS * PAIR].rearrange(
                        "p (h k) -> p h k", h=SA_HEADS), AX.X, ALU.max).then_inc(max_done, 1)
                    dve.wait_ge(max_done, TILES * i + t + 1)
                    dve.tensor_scalar(shift[:, t, :], mx[:, t, :], -float(SA_SCALE), None,
                                      ALU.mult).then_inc(shift_done, 1)
                for t in range(TILES):
                    dve.wait_ge(e_done, SA_HEADS * (TILES * i + t + 1))
                    dve.reciprocal(rden[:, t, :], den[:, t, :]).then_inc(rden_done, 1)
                    dve.wait_ge(rden_done, TILES * i + t + 1)
                    dve.tensor_tensor(e[:, t], e[:, t], rden[:, t, :].unsqueeze(2).to_broadcast(
                        [PAIR, SA_HEADS, PAIR]), ALU.mult).then_inc(e_normed, 1)
                for t in range(TILES):
                    dve.wait_ge(o_done, TILES * i + t + 1)
                    for k in range(2):
                        p0 = SA_D * k
                        dve.tensor_copy(oT[p0:p0 + SA_D, t], bank[t][p0:p0 + SA_D, 0:4 * PAIR].rearrange(
                            "p (m k q) -> p m k q", m=KC, k=2)[:, :, k, :]).then_inc(o_taken, 1)
                dve.wait_ge(xb_done, i + 1)
                for t in range(TILES):
                    n = TILES * i + t
                    dve.wait_ge(p_done, n + 1)
                    dve.tensor_tensor(z[:, t, :], bank[4 + t][0:PAIR, 0:F], xb[:, t, :], ALU.add).then_inc(z_done, 1)
                    dve.wait_ge(z_done, n + 1)
                    norm_stats(dve, z[:, t, :], stats[:, t, :], mv[:, t, :], stat_chain, 2 * n, (loaded, 16)).then_inc(var_done, 1)
                for t in range(TILES):
                    n = TILES * i + t
                    dve.wait_ge(rstd_done, n + 1)
                    if not first:
                        dve.wait_ge(y_stored, 16 * (n - TILES + 1))
                    dve.tensor_scalar(y[:, t, :], z[:, t, :], mv[:, t, 0:1], mv[:, t, 1:2],
                                      ALU.subtract, ALU.mult).then_inc(y_done, 1)
                for t in range(TILES):
                    dve.wait_ge(yT_hi_done, TILES * i + t + 1)
                    dve.tensor_tensor(yT_lo[:, t].rearrange("p k q -> p (k q)"), bank[4 + t][:, 0:KC * PAIR],
                                      yT_hi[:, t].rearrange("p k q -> p (k q)").bitcast(F32),
                                      ALU.subtract).then_inc(yT_lo_done, 1)

            block_dve(0, first=True)
            with dve.Fori(1, NBLK) as i:
                block_dve(i)

        @block.gpsimd
        def _(pool):
            pool.wait_ge(loaded, 16 * 11)
            pool.wait_ge(half_set, 1)

            def block_pool(i, first=False):
                pool.wait_ge(x_loaded, 32 * (i + 1))
                if not first:
                    pool.wait_ge(z_done, TILES * i)
                pool.tensor_tensor(xb[:], x[:], bo[:].unsqueeze(1).to_broadcast([PAIR, TILES, F]),
                                   ALU.add).then_inc(xb_done, 1)
                for t in range(TILES):
                    pool.wait_ge(var_done, TILES * i + t + 1)
                    pool.tensor_tensor(mv[:, t, 1:2], mv[:, t, 1:2], half[:], ALU.pow).then_inc(rstd_done, 1)

            block_pool(0, first=True)
            with pool.Fori(1, NBLK) as i:
                block_pool(i)


def phase_b(nc, D, A_hi, A_lo, M_fold):
    with ExitStack() as ctx:
        def sb(name, shape, dt=F32):
            return ctx.enter_context(nc.sbuf_tensor("b_" + name, shape, dt))

        def sem(name):
            return ctx.enter_context(nc.semaphore("b_" + name))

        def ps(name):
            return ctx.enter_context(nc.psum_tensor("b_" + name, [128, 512], F32))

        score_bank = [ps(f"score{j}") for j in range(FILLS)]
        turn_bank = [ps(f"turn{j}") for j in range(3)]
        out_bank = ps("out")
        misc_bank = ps("misc")

        ident = sb("ident", [128, 128])
        ones_r = sb("ones_r", [2 * UNITS[0], 128], F32R)
        own_unit = [sb(f"own_unit{k}", [2 * UNITS[k], UNITS[k], 128]) for k in range(2)]
        half = sb("half", [PAIR, 1])
        y1T_hi = sb("y1T_hi", [128, KC, PAIR], F32R)
        y1T_lo = sb("y1T_lo", [128, KC, PAIR], F32R)
        q_hi = sb("q_hi", [128, 2, XH, S], F32R)
        q_lo = sb("q_lo", [128, 2, XH, S], F32R)
        cT_in = sb("cT_in", [128, CTX])
        cT_hi = sb("cT_hi", [128, 2, CTX], F32R)
        cT_lo = sb("cT_lo", [128, 2, CTX], F32R)
        c_in = sb("c_in", [CK, CH * CD])
        c_hi = sb("c_hi", [CK, 2, CH * CD], F32R)
        c_lo = sb("c_lo", [CK, 2, CH * CD], F32R)
        mask_in = sb("mask_in", [128, CTX], U8)
        mask_add = sb("mask_add", [128, 2, CTX], BF16)
        p = [sb(f"p{k}", [128, UNITS[k], CTX]) for k in range(2)]
        top = sb("top", [128, 2, UNITS[0], FILLS])
        top3 = sb("top3", [128, FILLS])
        shift = sb("shift", [128, 2, UNITS[0]])
        den = sb("den", [128, 2, UNITS[0]])
        keep = sb("keep", [128, UNITS[0]])
        rden = sb("rden", [128, UNITS[0]])
        rden_parts = sb("rden_parts", [128, 2 * UNITS[0]])
        rden_r = sb("rden_r", [128, UNITS[0]], F32R)
        rden_rows = sb("rden_rows", [2 * UNITS[0], WIDE], F32R)
        pT_hi = sb("pT_hi", [CK, 3, WIDE], F32R)
        pT_lo = sb("pT_lo", [CK, 3, WIDE], F32R)
        out_sb = sb("out_sb", [128, WIDE])
        oT = sb("oT", [128, XH, 2, S])
        y1_res = sb("y1_res", [PAIR, F])
        z = sb("z", [PAIR, F])
        y2 = sb("y2", [PAIR, F])
        stats = sb("stats", [PAIR, 6])
        mv = sb("mv", [PAIR, 2])

        const_loaded, const_set = sem("const_loaded"), sem("const_set")
        y1T_loaded, cT_loaded, c_loaded, mask_loaded = sem("y1T_loaded"), sem("cT_loaded"), sem("c_loaded"), sem("mask_loaded")
        res_loaded, y2_stored = sem("res_loaded"), sem("y2_stored")
        q_done, q_hi_done, q_lo_done = sem("q_done"), sem("q_hi_done"), sem("q_lo_done")
        cT_split, c_split, mask_ready = sem("cT_split"), sem("c_split"), sem("mask_ready")
        fill_done, fill_taken = sem("fill_done"), sem("fill_taken")
        shift_done, exp_done = sem("shift_done"), sem("exp_done")
        turned, hi_done, lo_done, pv_done = sem("turned"), sem("hi_done"), sem("lo_done"), sem("pv_done")
        out_copied = sem("out_copied")
        rden_chain, rden_turned, rows_done, spread_done = sem("rden_chain"), sem("rden_turned"), sem("rows_done"), sem("spread_done")
        oT_done, proj_done = sem("oT_done"), sem("proj_done")
        z_done, stat_chain, var_done, rstd_done, y2_done = sem("z_done"), sem("stat_chain"), sem("var_done"), sem("rstd_done"), sem("y2_done")

        CONSTS = 3
        STEPS = SLOTS * CH
        TURN_LAG = CH + 3
        PV_LAG = TURN_LAG + 2
        RDEN = 6
        OT_OPS = 2
        QG = XH // 4
        AHEAD = 2

        def units(slot):
            return UNITS[slot % 2]

        unit0 = [sum(units(k) for k in range(slot)) for slot in range(SLOTS + 1)]
        PUNITS = unit0[SLOTS]
        PFILLS = FILLS * PUNITS

        def fills_at(n):
            slot, k = n // CH, n % CH
            count = FILLS * units(slot)
            return [(slot, m) for m in range(count) if m * CH // count == k]

        def slot_before(i, slot, k):
            return i + (slot - k) // SLOTS, (slot - k) % SLOTS

        def lagging(i, n, lag, first, last):
            if (first and n < lag) or (last and n - lag >= STEPS):
                return None
            return i + (n - lag) // STEPS, (n - lag) % STEPS

        def lagging_slot(i, n, k, first, last):
            slot = n // CH
            if (first and slot < k) or (last and slot - k >= SLOTS):
                return None
            return slot_before(i, slot, k)

        def four_heads(q, g):
            return q[:, :, 4 * g:4 * g + 4, :].rearrange("p b h q -> p h b q")

        def four_heads_bank(g):
            return score_bank[g % FILLS][:, 0:4 * PAIR].rearrange("p (h b q) -> p h b q", h=4, b=2)

        def run_pair(i, first, query_group, fill_step, lag_step):
            ahead = 0 if first else AHEAD
            for g in range(QG):
                query_group(g)
                if not first and g >= QG - AHEAD:
                    lag_step(g - (QG - AHEAD))
            for n in range(STEPS):
                fill_step(n)
                if n >= ahead:
                    lag_step(n)

        block = ctx.enter_context(nc.Block())

        @block.sync
        def _(sp):
            sp.dma_start(ident[:], D["ident"]).then_inc(const_loaded, 16)
            for k in range(2):
                sp.dma_start(own_unit[k][:], D[f"own_unit{k}"]).then_inc(const_loaded, 16)

            def load_y1T(i, first=False):
                if not first:
                    sp.wait_ge(q_done, QG * i)
                for dst, src in ((y1T_hi, D["y1T_hi"]), (y1T_lo, D["y1T_lo"])):
                    sp.dma_start(dst[:].bitcast(F32), src[:, bass.ds(i, 1)].rearrange("p a k q -> p (a k) q")).then_inc(y1T_loaded, 16)

            def load_batch(i, b, first=False):
                n = 2 * i + b
                if not (first and b == 0):
                    sp.wait_ge(cT_split, 2 * n)
                sp.dma_start(cT_in[:], D["ctxT"][bass.ds(n, 1)].rearrange("a d s -> (a d) s")).then_inc(cT_loaded, 16)
                if not (first and b == 0):
                    wait_apart(sp, (y1T_loaded, 16), (mask_ready, n))
                sp.dma_start(mask_in[:], D["mask"][bass.ds(n, 1)].rearrange("a s -> (a s)").partition_broadcast(
                    128)).then_inc(mask_loaded, 16)
                if not (first and b == 0):
                    sp.wait_ge(c_split, 2 * n)
                sp.dma_start(c_in[:], D["ctx"][bass.ds(n, 1)].rearrange("a p n -> (a p) n")).then_inc(c_loaded, 16)

            def residual(i):
                sp.dma_start(y1_res[:], D["y1"][:, bass.ds(i, 1), :].rearrange("p a f -> p (a f)")).then_inc(res_loaded, 16)

            def store(i):
                sp.wait_ge(y2_done, i + 1)
                sp.dma_start(D["y2"][:, bass.ds(i, 1), :].rearrange("p a f -> p (a f)"), y2[:]).then_inc(y2_stored, 16)

            load_y1T(0, first=True)
            load_batch(0, 0, first=True)
            load_batch(0, 1, first=True)
            residual(0)
            with sp.Fori(1, NPAIR) as i:
                load_y1T(i)
                load_batch(i, 0)
                load_batch(i, 1)
                store(i - 1)
                residual(i)
            store(NPAIR - 1)
            sp.wait_ge(y2_stored, 16 * NPAIR)

        @block.tensor
        def _(pe):
            pe.wait_ge(const_loaded, 16 * CONSTS)
            pe.wait_ge(const_set, 3)

            def queries(i, g, first):
                if g == 0:
                    pe.wait_ge(y1T_loaded, 32 * (i + 1))
                    if not first:
                        pe.wait_ge(fill_taken, PFILLS * i)
                if g >= FILLS:
                    pe.wait_ge(q_lo_done, QG * i + g - FILLS + 1)
                for k in range(4):
                    out = score_bank[g % FILLS][:, k * PAIR:(k + 1) * PAIR]
                    terms = [(A, y, kc) for kc in range(KC) for A, y in ((A_hi, y1T_hi), (A_hi, y1T_lo), (A_lo, y1T_hi))]
                    for n, (A, y, kc) in enumerate(terms):
                        mm = pe.matmul(out, A[:, 4 * g + k, kc * 128:(kc + 1) * 128], y[:, kc, :],
                                       start=(n == 0), stop=(n == len(terms) - 1))
                mm.then_inc(q_done, 1)

            def fill(i, slot, m):
                u, j, b = m // FILLS, m % FILLS, slot // 2
                n = FILLS * unit0[slot] + m
                if m == 0 and slot % 2 == 0:
                    pe.wait_ge(cT_split, 2 * (2 * i + b + 1))
                if n == 0:
                    pe.wait_ge(q_lo_done, QG * (i + 1))
                if n >= FILLS:
                    pe.wait_ge(fill_taken, PFILLS * i + n - FILLS + 1)
                out = score_bank[j][:, 0:FW]
                keys = slice(j * FW, (j + 1) * FW)
                r0 = WIDE * (slot % 2) + 128 * u
                hi = q_hi[:, b].rearrange("p h q -> p (h q)")[:, r0:r0 + 128]
                lo = q_lo[:, b].rearrange("p h q -> p (h q)")[:, r0:r0 + 128]
                pe.matmul(out, hi, cT_hi[:, b, keys], start=True, stop=False)
                pe.matmul(out, hi, cT_lo[:, b, keys], start=False, stop=False)
                pe.matmul(out, lo, cT_hi[:, b, keys], start=False, stop=True).then_inc(fill_done, 1)

            def turn(i, n, first):
                slot, c = n // CH, n % CH
                if c == 0:
                    pe.wait_ge(exp_done, PUNITS * i + unit0[slot + 1])
                if not (first and n < 3):
                    pe.wait_ge(lo_done, STEPS * i + n - 2)
                for u in range(units(slot)):
                    mm = pe.transpose(turn_bank[n % 3][0:CK, u * 128:(u + 1) * 128],
                                      p[slot % 2][:, u, c * CK:(c + 1) * CK], ident[:])
                mm.then_inc(turned, 1)

            def weigh(i, n, first):
                slot, c = n // CH, n % CH
                b, w = slot // 2, 128 * units(slot)
                if c == 0:
                    if not (first and slot == 0):
                        pe.wait_ge(out_copied, SLOTS * i + slot)
                    pe.wait_ge(c_split, 2 * (2 * i + b + 1))
                pe.wait_ge(lo_done, STEPS * i + n + 1)
                out = out_bank[:, 0:w]
                hi, lo = c_hi[:, b, c * CD:(c + 1) * CD], c_lo[:, b, c * CD:(c + 1) * CD]
                pe.matmul(out, hi, pT_hi[:, n % 3, 0:w], start=(c == 0), stop=False)
                pe.matmul(out, hi, pT_lo[:, n % 3, 0:w], start=False, stop=False)
                pe.matmul(out, lo, pT_hi[:, n % 3, 0:w], start=False, stop=(c == CH - 1)).then_inc(pv_done, 1)

            def turn_rden(i, slot, first):
                s = SLOTS * i + slot
                if not (first and slot == 0):
                    pe.wait_ge(oT_done, OT_OPS * s)
                if slot == 0 and not first:
                    pe.wait_ge(z_done, i)
                pe.wait_ge(rden_chain, RDEN * (s + 1))
                pe.transpose(misc_bank[0:2 * units(slot), 0:128], rden_parts[:, 0:2 * units(slot)],
                             ident[:]).then_inc(rden_turned, 1)

            def spread_rden(i, slot):
                u = units(slot)
                pe.wait_ge(rows_done, SLOTS * i + slot + 1)
                pe.matmul(misc_bank[:, 0:128 * u], ones_r[0:2 * u, :], rden_rows[0:2 * u, 0:128 * u],
                          start=True, stop=True).then_inc(spread_done, 1)

            def project(i):
                pe.wait_ge(oT_done, OT_OPS * SLOTS * (i + 1))
                for h in range(XH):
                    mm = pe.matmul(misc_bank[0:PAIR, 0:F], oT[:, h].rearrange("p b q -> p (b q)"), M_fold[:, h, :],
                                   start=(h == 0), stop=(h == XH - 1))
                mm.then_inc(proj_done, 1)

            def lag_step(i, n, first, last=False):
                if at := lagging(i, n, TURN_LAG, first, last):
                    turn(*at, first)
                if at := lagging(i, n, PV_LAG, first, last):
                    weigh(*at, first)
                if n % CH == 7 and (at := lagging_slot(i, n, 1, first, last)):
                    turn_rden(*at, first)
                if n % CH == 4 and (at := lagging_slot(i, n, 2, first, last)):
                    spread_rden(*at)
                if n == CH + 6 and not first:
                    project(i - 1)

            def pair_pe(i, first=False):
                run_pair(i, first, lambda g: queries(i, g, first),
                         lambda n: [fill(i, *f) for f in fills_at(n)], lambda n: lag_step(i, n, first))

            pair_pe(0, first=True)
            with pe.Fori(1, NPAIR) as i:
                pair_pe(i)
            for n in range(STEPS, STEPS + PV_LAG):
                lag_step(NPAIR - 1, n, False, last=True)
            project(NPAIR - 1)

        @block.scalar
        def _(act):
            def q_round(i, g):
                act.wait_ge(q_done, QG * i + g + 1)
                act.copy(four_heads(q_hi, g), four_heads_bank(g)).then_inc(q_hi_done, 1)

            def p_round(i, n, first):
                g, w = STEPS * i + n, 128 * units(n // CH)
                act.wait_ge(turned, g + 1)
                if not (first and n < 3):
                    act.wait_ge(pv_done, g - 2)
                act.copy(pT_hi[:, n % 3, 0:w], turn_bank[n % 3][0:CK, 0:w]).then_inc(hi_done, 1)

            def exps(i, slot, u):
                act.wait_ge(shift_done, PUNITS * i + unit0[slot] + u + 1)
                row = p[slot % 2][:, u, :]
                act.activation(row, row, ACT.Exp, bias=shift[:, slot % 2, u:u + 1], scale=float(X_SCALE),
                               accum_out=den[:, slot % 2, u:u + 1]).then_inc(exp_done, 1)

            def out_copy(i, slot, first):
                w = 128 * units(slot)
                if not (first and slot == 0):
                    act.wait_ge(oT_done, OT_OPS * (SLOTS * i + slot))
                act.wait_ge(pv_done, CH * (SLOTS * i + slot + 1))
                act.copy(out_sb[:, 0:w], out_bank[:, 0:w]).then_inc(out_copied, 1)

            def fill_step(i, n):
                for slot, m in fills_at(n):
                    if m % FILLS == FILLS - 1:
                        exps(i, slot, m // FILLS)

            def lag_step(i, n, first, last=False):
                if at := lagging(i, n, TURN_LAG, first, last):
                    p_round(*at, first)
                if n % CH == 4 and (at := lagging_slot(i, n, 2, first, last)):
                    out_copy(*at, first)

            def pair_act(i, first=False):
                ahead = 0 if first else AHEAD
                run_pair(i, first, lambda g: q_round(i, g), lambda n: n < ahead and fill_step(i, n),
                         lambda n: (lag_step(i, n, first), n >= ahead and fill_step(i, n)))

            pair_act(0, first=True)
            with act.Fori(1, NPAIR) as i:
                pair_act(i)
            for n in range(STEPS, STEPS + PV_LAG):
                lag_step(NPAIR - 1, n, False, last=True)

        @block.vector
        def _(dve):
            dve.memset(half[:], -0.5).then_inc(const_set, 1)
            dve.memset(out_sb[0:2 * UNITS[0], 0:128], 1.0).then_inc(const_set, 1)
            dve.wait_ge(const_set, 2)
            dve.tensor_copy(ones_r[:], out_sb[0:2 * UNITS[0], 0:128]).then_inc(const_set, 1)
            dve.wait_ge(const_loaded, 16 * CONSTS)

            def q_rest(i, g):
                dve.wait_ge(q_hi_done, QG * i + g + 1)
                dve.tensor_tensor(four_heads(q_lo, g), four_heads_bank(g), four_heads(q_hi, g).bitcast(F32),
                                  ALU.subtract).then_inc(q_lo_done, 1)

            def scores(i, slot, m, first):
                u, j, b = m // FILLS, m % FILLS, slot // 2
                waits = [(fill_done, PFILLS * i + FILLS * unit0[slot] + m + 1)]
                if m == 0 and slot % 2 == 0:
                    waits.append((mask_ready, 2 * i + b + 1))
                if u == 0 and not (first and slot < 2):
                    waits.append((turned, CH * (SLOTS * i + slot - 2) + (j + 1) * (CH // FILLS)))
                wait_apart(dve, (const_loaded, 16 * CONSTS), *waits)
                keys = slice(j * FW, (j + 1) * FW)
                dve.tensor_tensor_reduce(out=p[slot % 2][:, u, keys], in0=score_bank[j][:, 0:FW],
                                         in1=mask_add[:, b, keys], scale=1.0, scalar=-3.0e38,
                                         op0=ALU.add, op1=ALU.max,
                                         accum_out=top[:, slot % 2, u, j:j + 1]).then_inc(fill_taken, 1)

            def shifts(i, slot, u):
                dve.wait_ge(fill_taken, PFILLS * i + FILLS * (unit0[slot] + u + 1))
                dve.tensor_scalar(top3[:], top[:, slot % 2, u, :], -float(X_SCALE), None, ALU.mult, ALU.min,
                                  accum_out=shift[:, slot % 2, u:u + 1]).then_inc(shift_done, 1)

            def p_rest(i, n):
                w = 128 * units(n // CH)
                dve.wait_ge(hi_done, STEPS * i + n + 1)
                dve.tensor_tensor(pT_lo[:, n % 3, 0:w], turn_bank[n % 3][0:CK, 0:w],
                                  pT_hi[:, n % 3, 0:w].bitcast(F32), ALU.subtract).then_inc(lo_done, 1)

            def reciprocals(i, slot):
                s, par, u = SLOTS * i + slot, slot % 2, units(slot)
                dve.wait_ge(exp_done, PUNITS * i + unit0[slot + 1])
                dve.tensor_scalar(keep[:, 0:u], shift[:, par, 0:u], float(X_SCALE * BIG / 2), None,
                                  ALU.is_lt).then_inc(rden_chain, 1)
                dve.reciprocal(rden[:, 0:u], den[:, par, 0:u]).then_inc(rden_chain, 1)
                dve.wait_ge(rden_chain, RDEN * s + 2)
                dve.tensor_tensor(rden[:, 0:u], rden[:, 0:u], keep[:, 0:u], ALU.mult).then_inc(rden_chain, 1)
                dve.wait_ge(rden_chain, RDEN * s + 3)
                dve.tensor_copy(rden_r[:, 0:u], rden[:, 0:u]).then_inc(rden_chain, 1)
                dve.wait_ge(rden_chain, RDEN * s + 4)
                dve.tensor_copy(rden_parts[:, 0:u], rden_r[:, 0:u].bitcast(F32)).then_inc(rden_chain, 1)
                dve.tensor_tensor(rden_parts[:, u:2 * u], rden[:, 0:u], rden_r[:, 0:u].bitcast(F32),
                                  ALU.subtract).then_inc(rden_chain, 1)

            def rows(i, slot):
                u = units(slot)
                dve.wait_ge(rden_turned, SLOTS * i + slot + 1)
                dve.tensor_tensor(rden_rows[0:2 * u, 0:128 * u].rearrange("r (u q) -> r u q", u=u),
                                  misc_bank[0:2 * u, 0:128].unsqueeze(1).to_broadcast([2 * u, u, 128]),
                                  own_unit[slot % 2][:], ALU.mult).then_inc(rows_done, 1)

            def scale_out(i, slot, first):
                s, b = SLOTS * i + slot, slot // 2
                shared, cut = WIDE // S, WIDE % S
                dve.wait_ge(out_copied, s + 1)
                dve.wait_ge(spread_done, s + 1)
                if slot == 0 and not first:
                    dve.wait_ge(proj_done, i)
                if slot % 2 == 0:
                    whole, r0 = range(0, shared), 0
                    part, q0 = slice(shared * S, WIDE), 0
                else:
                    whole, r0 = range(shared + 1, XH), S - cut
                    part, q0 = slice(0, S - cut), cut
                cols = slice(r0, r0 + S * len(whole))
                dve.tensor_tensor(oT[:, whole[0]:whole[-1] + 1, b, :],
                                  misc_bank[:, cols].rearrange("p (h q) -> p h q", q=S),
                                  out_sb[:, cols].rearrange("p (h q) -> p h q", q=S), ALU.mult).then_inc(oT_done, 1)
                dve.tensor_tensor(oT[:, shared, b, q0:q0 + part.stop - part.start], misc_bank[:, part], out_sb[:, part],
                                  ALU.mult).then_inc(oT_done, 1)

            def norm(i):
                dve.wait_ge(proj_done, i + 1)
                dve.wait_ge(res_loaded, 16 * (i + 1))
                dve.tensor_tensor(z[:], misc_bank[0:PAIR, 0:F], y1_res[:], ALU.add).then_inc(z_done, 1)
                dve.wait_ge(z_done, i + 1)
                norm_stats(dve, z[:], stats[:], mv[:], stat_chain, 2 * i, (const_loaded, 32)).then_inc(var_done, 1)

            def norm_out(i, first=False):
                dve.wait_ge(rstd_done, i + 1)
                if not first:
                    dve.wait_ge(y2_stored, 16 * i)
                dve.tensor_scalar(y2[:], z[:], mv[:, 0:1], mv[:, 1:2], ALU.subtract, ALU.mult).then_inc(y2_done, 1)

            def fill_step(i, n, first):
                for slot, m in fills_at(n):
                    scores(i, slot, m, first)
                    if m % FILLS == FILLS - 1:
                        shifts(i, slot, m // FILLS)

            def lag_step(i, n, first, last=False):
                if at := lagging(i, n, TURN_LAG, first, last):
                    p_rest(*at)
                if n % CH == 5 and (at := lagging_slot(i, n, 2, first, last)):
                    scale_out(*at, first)
                if n % CH == 5 and (at := lagging_slot(i, n, 1, first, last)):
                    reciprocals(*at)
                if n % CH == 8 and (at := lagging_slot(i, n, 1, first, last)):
                    rows(*at)
                if n == CH + 6 and not first:
                    norm(i - 1)
                if n == CH + 9 and not first:
                    norm_out(i - 1)

            def pair_dve(i, first=False):
                run_pair(i, first, lambda g: q_rest(i, g), lambda n: fill_step(i, n, first), lambda n: lag_step(i, n, first))

            pair_dve(0, first=True)
            with dve.Fori(1, NPAIR) as i:
                pair_dve(i)
            for n in range(STEPS, STEPS + PV_LAG + 1):
                lag_step(NPAIR - 1, n, False, last=True)
            norm(NPAIR - 1)
            norm_out(NPAIR - 1)

        @block.gpsimd
        def _(pool):
            pool.wait_ge(const_set, 1)

            def split(hi, lo, src, loaded, done, free, count, i, b, first):
                n = 2 * i + b
                waits = [(loaded, 16 * (n + 1))]
                if not first:
                    waits.append((free, count))
                wait_apart(pool, (const_set, 1), *waits)
                pool.tensor_scalar(hi[:, b, :], src[:], 1.0, 0.0, ALU.mult, ALU.add).then_inc(done, 1)
                pool.wait_ge(done, 2 * n + 1)
                pool.tensor_tensor(lo[:, b, :], src[:], hi[:, b, :].bitcast(F32), ALU.subtract).then_inc(done, 1)

            def mask_bias(i, b, first):
                n = 2 * i + b
                waits = [(mask_loaded, 16 * (n + 1))]
                if not first:
                    waits.append((fill_taken, PFILLS * (i - 1) + FILLS * unit0[2 * b + 2]))
                wait_apart(pool, (const_set, 1), *waits)
                pool.tensor_scalar(mask_add[:, b, :], mask_in[:], BIG, -BIG, ALU.mult, ALU.add).then_inc(mask_ready, 1)

            def rstd(i):
                pool.wait_ge(var_done, i + 1)
                pool.tensor_tensor(mv[:, 1:2], mv[:, 1:2], half[:], ALU.pow).then_inc(rstd_done, 1)

            def batch(i, b, first):
                split(cT_hi, cT_lo, cT_in, cT_loaded, cT_split, fill_done, PFILLS * (i - 1) + FILLS * unit0[2 * b + 2],
                      i, b, first)
                mask_bias(i, b, first)
                split(c_hi, c_lo, c_in, c_loaded, c_split, pv_done, 2 * CH * (2 * i + b - 1), i, b, first)

            for b in range(2):
                batch(0, b, True)
            with pool.Fori(1, NPAIR) as i:
                batch(i, 0, False)
                batch(i, 1, False)
                rstd(i - 1)
            rstd(NPAIR - 1)


def phase_c(nc, D):
    with ExitStack() as ctx:
        def sb(name, shape, dt=F32):
            return ctx.enter_context(nc.sbuf_tensor("c_" + name, shape, dt))

        def sem(name):
            return ctx.enter_context(nc.semaphore("c_" + name))

        def ps(name):
            return ctx.enter_context(nc.psum_tensor("c_" + name, [128, 512], F32))

        gate_bank = [ps(f"gate{j}") for j in range(2)]
        up_bank = [ps(f"up{j}") for j in range(2)]
        down_bank = [ps(f"down{j}") for j in range(2)]
        comb_bank, misc_bank = ps("comb"), ps("misc")

        W_IN, W_SLOTS = 2 * KC, 4
        w_in = sb("w_in", [128, W_SLOTS, W_IN + 2, 128])
        w_hi = sb("w_hi", [128, IC, W_IN + 2, 128], F32R)
        w_lo = sb("w_lo", [128, IC, W_IN + 2, 128], F32R)
        w_route = sb("w_route", [128, KC, NR])
        owner_in = sb("owner_in", [2 * NR, IW])
        owner = sb("owner", [2 * NR, IW], F32R)
        ident = sb("ident", [128, 128])
        rank = sb("rank", [PAIR, TILES, EXPERTS])
        half = sb("half", [PAIR, 1])
        y2 = sb("y2", [PAIR, TILES, F])
        y2_res = sb("y2_res", [PAIR, TILES, F])
        y2T = sb("y2T", [128, KC, BLK])
        y2T_hi = sb("y2T_hi", [128, KC, BLK], F32R)
        y2T_lo = sb("y2T_lo", [128, KC, BLK], F32R)
        logit = sb("logit", [PAIR, TILES, NR])
        ex = sb("ex", [PAIR, TILES, NR])
        best = sb("best", [PAIR, 2, TILES])
        rest = sb("rest", [PAIR, TILES, EXPERTS])
        pick = sb("pick", [PAIR, 2, TILES, EXPERTS])
        first_of = sb("first_of", [PAIR, TILES])
        total = sb("total", [PAIR, TILES])
        combine = sb("combine", [PAIR, TILES, NR])
        combine_r = sb("combine_r", [PAIR, TILES, NR], F32R)
        combine_parts = sb("combine_parts", [PAIR, TILES, 2 * NR])
        combT = sb("combT", [2 * NR, BLK], F32R)
        act_g = sb("act_g", [128, 2, BLK])
        act_gu = sb("act_gu", [128, 2, BLK])
        h = sb("h", [128, 2, BLK])
        H_DEEP = 3
        h_hi = sb("h_hi", [128, H_DEEP, BLK], F32R)
        h_lo = sb("h_lo", [128, H_DEEP, BLK], F32R)
        z = sb("z", [PAIR, TILES, F])
        y = sb("y", [PAIR, TILES, F])
        stats = sb("stats", [PAIR, TILES, 6])
        mv = sb("mv", [PAIR, TILES, 2])

        loaded, y2_loaded, res_loaded, half_set = sem("loaded"), sem("y2_loaded"), sem("res_loaded"), sem("half_set")
        owner_loaded, owner_set = sem("owner_loaded"), sem("owner_set")
        w_loaded = [sem(f"w_loaded{k}") for k in range(W_SLOTS)]
        w_hi_done, w_split = sem("w_hi_done"), sem("w_split")
        y2_turned, y2T_done, route_done = sem("y2_turned"), sem("y2T_done"), sem("route_done")
        y2T_hi_done, y2T_lo_done = sem("y2T_hi_done"), sem("y2T_lo_done")
        route_chain, ex_done, combine_done = sem("route_chain"), sem("ex_done"), sem("combine_done")
        comb_turned, combT_done = sem("comb_turned"), sem("combT_done")
        gate_done, up_done, comb_done = sem("gate_done"), sem("up_done"), sem("comb_done")
        silu_done, gu_done, h_done = sem("silu_done"), sem("gu_done"), sem("h_done")
        h_hi_done, h_lo_done, down_done, z_done = sem("h_hi_done"), sem("h_lo_done"), sem("down_done"), sem("z_done")
        stat_chain, var_done, rstd_done = sem("stat_chain"), sem("var_done"), sem("rstd_done")
        y_done, y_stored = sem("y_done"), sem("y_stored")
        LOADS = 4
        LOGITS = 4
        CHAIN = LOGITS + 21
        TURN_AT, ROUTE_AT, LOGITS_AT, EXP_AT, PICK_AT, WEIGHTS_AT = (5, 6), 8, 9, 10, (11, 12), 13

        def rows_of(c):
            return min(128, IW - 128 * c)

        def last_use(i, c, deep, first):
            if c >= deep:
                return IC * i + c - deep + 1
            if first:
                return None
            return IC * (i - 1) + max(k for k in range(IC) if k % deep == c) + 1

        def w_parts(c):
            m = rows_of(c)
            if m == 128:
                return [(slice(0, 128), slice(0, W_IN + 2), slice(0, 128))]
            return [(slice(0, 128), slice(0, W_IN), slice(0, m)), (slice(0, m), slice(W_IN, W_IN + 2), slice(0, 128))]

        W_PARTS = [sum(len(w_parts(k)) for k in range(c + 1)) for c in range(IC)]

        def every_block(engine, body):
            body(0, True, False)
            with engine.Fori(1, NBLK - 1) as i:
                body(i, False, False)
            body(NBLK - 1, False, True)

        block = ctx.enter_context(nc.Block())

        @block.sync
        def _(sp):
            sp.dma_start(y2[:], D["y2"][:, 0:TILES, :]).then_inc(y2_loaded, 16)
            sp.dma_start(ident[:], D["ident"]).then_inc(loaded, 16)
            sp.dma_start(w_route[:, :, 0:EXPERTS], D["route_w"]).then_inc(loaded, 16)
            sp.dma_start(w_route[:, :, EXPERTS:NR], D["route_sh"], allow_slow_non_contiguous=True).then_inc(loaded, 16)
            sp.dma_start(rank[:], D["rank"]).then_inc(loaded, 16)

            def load_next(i, first, last):
                if not last:
                    sp.wait_ge(y2_turned, KC * (i + 1))
                    sp.dma_start(y2[:], D["y2"][:, bass.ts(i + 1, TILES), :]).then_inc(y2_loaded, 16)
                if not first:
                    sp.wait_ge(z_done, TILES * i)
                sp.dma_start(y2_res[:], D["y2"][:, bass.ts(i, TILES), :]).then_inc(res_loaded, 16)

            for c in range(IC):
                m = rows_of(c)
                if c >= W_SLOTS:
                    sp.wait_ge(w_split, W_PARTS[c - W_SLOTS])
                sp.dma_start(w_in[:, c % W_SLOTS, 0:W_IN, 0:m], D["hidden"][:, :, 128 * c:128 * c + m]).then_inc(w_loaded[c % W_SLOTS], 16)
                sp.dma_start(w_in[0:m, c % W_SLOTS, W_IN:, :].rearrange("p a n -> p (a n)"),
                             D["down"][128 * c:128 * c + m]).then_inc(w_loaded[c % W_SLOTS], 16)
                if c == 2:
                    load_next(0, True, False)
                if c == 0:
                    sp.dma_start(owner_in[:], D["owner"]).then_inc(owner_loaded, 16)

            def block_io(i, first, last):
                if not first:
                    load_next(i, first, last)
                for t in range(TILES):
                    sp.wait_ge(y_done, TILES * i + t + 1)
                    sp.dma_start(D["out"][:, bass.ds(i * TILES + t, 1), :], y[:, t:t + 1]).then_inc(y_stored, 16)

            every_block(sp, block_io)
            sp.wait_ge(y_stored, 16 * NPAIR)

        @block.tensor
        def _(pe):
            pe.wait_ge(loaded, 16 * LOADS)

            def turn_y2(i, kc, first=False):
                if kc == 0:
                    pe.wait_ge(y2_loaded, 16 * (i + 1))
                    if not first:
                        pe.wait_ge(combT_done, i)
                else:
                    pe.wait_ge(y2T_done, KC * i + kc)
                for t in range(TILES):
                    mm = pe.transpose(misc_bank[:, t * PAIR:(t + 1) * PAIR], y2[:, t, kc * 128:(kc + 1) * 128],
                                      ident[0:PAIR, 0:PAIR])
                mm.then_inc(y2_turned, 1)

            def route(i):
                pe.wait_ge(y2T_done, KC * (i + 1))
                for t in range(TILES):
                    for kc in range(KC):
                        mm = pe.matmul(misc_bank[0:PAIR, t * NR:(t + 1) * NR], y2T[:, kc, t * PAIR:(t + 1) * PAIR],
                                       w_route[:, kc, :], start=(kc == 0), stop=(kc == KC - 1))
                mm.then_inc(route_done, 1)

            def turn_combine(i):
                pe.wait_ge(combine_done, i + 1)
                for t in range(TILES):
                    mm = pe.transpose(misc_bank[0:2 * NR, t * PAIR:(t + 1) * PAIR], combine_parts[:, t, :],
                                      ident[0:PAIR, 0:PAIR])
                mm.then_inc(comb_turned, 1)

            def hidden(i, c, first):
                m = rows_of(c)
                if first:
                    pe.wait_ge(w_split, W_PARTS[c])
                for j, (bank, free, done) in enumerate(((gate_bank[c % 2], silu_done, gate_done),
                                                        (up_bank[c % 2], gu_done, up_done))):
                    if (used := last_use(i, c, 2, first)) is not None:
                        pe.wait_ge(free, used)
                    for kc in range(KC):
                        if c == 0 and j == 0:
                            pe.wait_ge(y2T_lo_done, KC * i + kc + 1)
                        w = KC * j + kc
                        terms = ((w_hi, y2T_hi), (w_lo, y2T_hi), (w_hi, y2T_lo))
                        for n, (a, b) in enumerate(terms):
                            mm = pe.matmul(bank[0:m, 0:BLK], a[:, c, w, 0:m], b[:, kc, :],
                                           start=(kc == 0 and n == 0), stop=(kc == KC - 1 and n == len(terms) - 1))
                    mm.then_inc(done, 1)

            def spread_combine(i, c, first):
                m = rows_of(c)
                if c == 0:
                    pe.wait_ge(owner_set, 1)
                    pe.wait_ge(combT_done, i + 1)
                if not (first and c == 0):
                    pe.wait_ge(h_done, IC * i + c)
                pe.matmul(comb_bank[0:m, 0:BLK], owner[:, 128 * c:128 * c + m], combT[:], start=True,
                          stop=True).then_inc(comb_done, 1)

            def down(i, c, first):
                m = rows_of(c)
                if c == 0 and not first:
                    pe.wait_ge(z_done, TILES * i)
                pe.wait_ge(h_lo_done, IC * i + c + 1)
                for t in range(TILES):
                    terms = ((h_hi, w_hi), (h_hi, w_lo), (h_lo, w_hi))
                    for n, (a, b) in enumerate(terms):
                        mm = pe.matmul(down_bank[t // 2][0:PAIR, (t % 2) * F:(t % 2 + 1) * F],
                                       a[0:m, c % H_DEEP, t * PAIR:(t + 1) * PAIR], b[0:m, c, W_IN:, :],
                                       start=(c == 0 and t % 2 == 0 and n == 0),
                                       stop=(c == IC - 1 and t % 2 == 1 and n == len(terms) - 1), skip_group_check=True)
                mm.then_inc(down_done, 1)

            def block_pe(i, first, last):
                if not first:
                    turn_combine(i)
                for s in range(IC + 2):
                    if (2 if first else 1) <= s <= IC:
                        spread_combine(i, s - 1, first)
                    if s < IC:
                        hidden(i, s, first)
                    if first and s == 1:
                        turn_combine(i)
                        spread_combine(i, 0, first)
                    if s >= 2:
                        down(i, s - 2, first)
                    if not last:
                        if s in TURN_AT:
                            turn_y2(i + 1, TURN_AT.index(s))
                        if s == ROUTE_AT:
                            route(i + 1)

            for kc in range(KC):
                turn_y2(0, kc, first=True)
            route(0)
            every_block(pe, block_pe)

        @block.scalar
        def _(act):
            def copy_y2T(i, kc, first=False):
                if kc == 0 and not first:
                    act.wait_ge(y2T_lo_done, KC * i)
                act.wait_ge(y2_turned, KC * i + kc + 1)
                act.copy(y2T[:, kc, :], misc_bank[:, 0:BLK]).then_inc(y2T_done, 1)

            def round_y2T(i, first=False):
                act.wait_ge(y2T_done, KC * (i + 1))
                if not first:
                    act.wait_ge(up_done, IC * i)
                for kc in range(KC):
                    act.copy(y2T_hi[:, kc, :], y2T[:, kc, :]).then_inc(y2T_hi_done, 1)

            def router_exp(i):
                act.wait_ge(route_chain, CHAIN * i + LOGITS)
                act.activation(ex[:], logit[:], ACT.Exp).then_inc(ex_done, 1)

            def copy_combT(i):
                act.wait_ge(comb_turned, i + 1)
                act.copy(combT[:], misc_bank[0:2 * NR, 0:BLK]).then_inc(combT_done, 1)

            def silu(i, c, first):
                m = rows_of(c)
                if (used := last_use(i, c, 2, first)) is not None:
                    act.wait_ge(gu_done, used)
                act.wait_ge(gate_done, IC * i + c + 1)
                act.activation(act_g[0:m, c % 2, :], gate_bank[c % 2][0:m, 0:BLK], ACT.Silu).then_inc(silu_done, 1)

            def round_h(i, c, first):
                m = rows_of(c)
                if (used := last_use(i, c, H_DEEP, first)) is not None:
                    act.wait_ge(down_done, used)
                act.wait_ge(h_done, IC * i + c + 1)
                act.copy(h_hi[0:m, c % H_DEEP, :], h[0:m, c % 2, :]).then_inc(h_hi_done, 1)

            def block_act(i, first, last):
                if not first:
                    copy_combT(i)
                for s in range(IC + 1):
                    if s < IC:
                        silu(i, s, first)
                    if first and s == 1:
                        copy_combT(i)
                    if s == IC and not last:
                        round_y2T(i + 1)
                    if s >= 1:
                        round_h(i, s - 1, first)
                    if not last:
                        if s in TURN_AT:
                            copy_y2T(i + 1, TURN_AT.index(s))
                        if s == EXP_AT:
                            router_exp(i + 1)

            for kc in range(KC):
                copy_y2T(0, kc, first=True)
            round_y2T(0, first=True)
            router_exp(0)
            act.wait_ge(owner_loaded, 16)
            act.copy(owner[:], owner_in[:]).then_inc(owner_set, 1)
            every_block(act, block_act)

        @block.vector
        def _(dve):
            dve.memset(half[:], -0.5).then_inc(half_set, 1)
            dve.wait_ge(loaded, 16 * LOADS)

            def wide(ap):
                return ap.unsqueeze(2).to_broadcast([PAIR, TILES, EXPERTS])

            logits, exps = logit[:, :, 0:EXPERTS], ex[:, :, 0:EXPERTS]

            def chain(i, done):
                def link(ins):
                    nonlocal done
                    done += 1
                    ins.then_inc(route_chain, 1)
                    dve.wait_ge(route_chain, CHAIN * i + done)
                return link

            def shifted_logits(i):
                link = chain(i, 0)
                dve.wait_ge(route_done, i + 1)
                link(dve.tensor_copy(logit[:], misc_bank[0:PAIR, 0:TILES * NR].rearrange("p (t n) -> p t n", t=TILES)))
                link(dve.tensor_reduce(best[:, 0, :], logits, AX.X, ALU.max))
                link(dve.tensor_scalar(logit[:, :, EXPERTS:NR], logit[:, :, EXPERTS:NR], -1.0, None, ALU.mult))
                link(dve.tensor_tensor(logits, logits, wide(best[:, 0, :]), ALU.subtract))

            def pick_largest(i, k):
                link = chain(i, LOGITS + 7 * k)
                if k == 0:
                    dve.wait_ge(ex_done, i + 1)
                src = exps if k == 0 else rest[:]
                link(dve.tensor_reduce(best[:, k, :], src, AX.X, ALU.max))
                link(dve.tensor_tensor(pick[:, k], src, wide(best[:, k, :]), ALU.is_equal))
                link(dve.tensor_tensor(pick[:, k], pick[:, k], rank[:], ALU.mult))
                link(dve.tensor_reduce(first_of[:], pick[:, k], AX.X, ALU.max))
                link(dve.tensor_tensor(pick[:, k], rank[:], wide(first_of[:]), ALU.is_equal))
                if k == 0:
                    link(dve.tensor_scalar(rest[:], pick[:, 0], -2.0, None, ALU.mult))
                    link(dve.tensor_tensor(rest[:], rest[:], exps, ALU.add))

            def combine_weights(i, first=False):
                link = chain(i, LOGITS + 12)
                link(dve.tensor_tensor(pick[:, 0], pick[:, 0], pick[:, 1], ALU.add))
                link(dve.tensor_tensor(pick[:, 0], pick[:, 0], exps, ALU.mult))
                link(dve.tensor_reduce(total[:], pick[:, 0], AX.X, ALU.add))
                link(dve.reciprocal(total[:], total[:]))
                link(dve.tensor_scalar(ex[:, :, EXPERTS:NR], ex[:, :, EXPERTS:NR], 1.0, None, ALU.add))
                link(dve.reciprocal(combine[:, :, EXPERTS:NR], ex[:, :, EXPERTS:NR]))
                link(dve.tensor_tensor(combine[:, :, 0:EXPERTS], pick[:, 0], wide(total[:]), ALU.mult))
                link(dve.tensor_copy(combine_r[:], combine[:]))
                if not first:
                    dve.wait_ge(comb_turned, i)
                link(dve.tensor_copy(combine_parts[:, :, 0:NR], combine_r[:].bitcast(F32)))
                dve.tensor_tensor(combine_parts[:, :, NR:], combine[:], combine_r[:].bitcast(F32),
                                  ALU.subtract).then_inc(combine_done, 1)

            def gated(i, c):
                m, k = rows_of(c), c % 2
                dve.wait_ge(silu_done, IC * i + c + 1)
                dve.wait_ge(up_done, IC * i + c + 1)
                dve.tensor_tensor(act_gu[0:m, k, :], up_bank[k][0:m, 0:BLK], act_g[0:m, k, :], ALU.mult).then_inc(gu_done, 1)

            def weighed(i, c):
                m, k = rows_of(c), c % 2
                dve.wait_ge(gu_done, IC * i + c + 1)
                dve.wait_ge(comb_done, IC * i + c + 1)
                dve.tensor_tensor(h[0:m, k, :], comb_bank[0:m, 0:BLK], act_gu[0:m, k, :], ALU.mult).then_inc(h_done, 1)

            def h_rest(i, c):
                m = rows_of(c)
                dve.wait_ge(h_hi_done, IC * i + c + 1)
                dve.tensor_tensor(h_lo[0:m, c % H_DEEP, :], h[0:m, c % 2, :], h_hi[0:m, c % H_DEEP, :].bitcast(F32),
                                  ALU.subtract).then_inc(h_lo_done, 1)

            def norm(i, first):
                dve.wait_ge(down_done, IC * (i + 1))
                dve.wait_ge(res_loaded, 16 * (i + 1))
                for t in range(TILES):
                    dve.tensor_tensor(z[:, t, :], down_bank[t // 2][0:PAIR, (t % 2) * F:(t % 2 + 1) * F], y2_res[:, t, :],
                                      ALU.add).then_inc(z_done, 1)
                for t in range(TILES):
                    n = TILES * i + t
                    dve.wait_ge(z_done, n + 1)
                    norm_stats(dve, z[:, t, :], stats[:, t, :], mv[:, t, :], stat_chain, 2 * n, (loaded, 16)).then_inc(var_done, 1)
                for t in range(TILES):
                    n = TILES * i + t
                    dve.wait_ge(rstd_done, n + 1)
                    if not first:
                        dve.wait_ge(y_stored, 16 * (n - TILES + 1))
                    dve.tensor_scalar(y[:, t, :], z[:, t, :], mv[:, t, 0:1], mv[:, t, 1:2],
                                      ALU.subtract, ALU.mult).then_inc(y_done, 1)

            def block_dve(i, first, last):
                for s in range(IC + 2):
                    if s >= 2:
                        h_rest(i, s - 2)
                    if (2 if first else 1) <= s <= IC:
                        weighed(i, s - 1)
                    if s < IC:
                        gated(i, s)
                    if first and s == 1:
                        weighed(i, 0)
                    if not last:
                        if s == LOGITS_AT:
                            shifted_logits(i + 1)
                        if s in PICK_AT:
                            pick_largest(i + 1, PICK_AT.index(s))
                        if s == WEIGHTS_AT:
                            combine_weights(i + 1)
                norm(i, first)

            shifted_logits(0)
            for k in range(2):
                pick_largest(0, k)
            combine_weights(0, first=True)
            every_block(dve, block_dve)

        @block.gpsimd
        def _(pool):
            pool.wait_ge(half_set, 1)

            def y2T_rest(i):
                for kc in range(KC):
                    pool.wait_ge(y2T_hi_done, KC * i + kc + 1)
                    pool.tensor_tensor(y2T_lo[:, kc, :], y2T[:, kc, :], y2T_hi[:, kc, :].bitcast(F32),
                                       ALU.subtract).then_inc(y2T_lo_done, 1)

            def split_weights(c):
                pool.wait_ge(w_loaded[c % W_SLOTS], 32 * (c // W_SLOTS + 1))
                parts = w_parts(c)
                for n, (rows, blocks, cols) in enumerate(parts):
                    src, hi, lo = w_in[rows, c % W_SLOTS, blocks, cols], w_hi[rows, c, blocks, cols], w_lo[rows, c, blocks, cols]
                    pool.tensor_scalar(hi, src, 1.0, 0.0, ALU.mult, ALU.add).then_inc(w_hi_done, 1)
                    pool.wait_ge(w_hi_done, W_PARTS[c] - len(parts) + n + 1)
                    pool.tensor_tensor(lo, src, hi.bitcast(F32), ALU.subtract).then_inc(w_split, 1)

            def block_pool(i, first, last):
                if not last:
                    y2T_rest(i + 1)
                for t in range(TILES):
                    pool.wait_ge(var_done, TILES * i + t + 1)
                    pool.tensor_tensor(mv[:, t, 1:2], mv[:, t, 1:2], half[:], ALU.pow).then_inc(rstd_done, 1)

            y2T_rest(0)
            for c in range(IC):
                split_weights(c)
            every_block(pool, block_pool)


def decoder_layer(nc, D):
    with ExitStack() as ctx:
        A_hi = ctx.enter_context(nc.sbuf_tensor("A_hi", [128, XH, F], F32R))
        A_lo = ctx.enter_context(nc.sbuf_tensor("A_lo", [128, XH, F], F32R))
        M_fold = ctx.enter_context(nc.sbuf_tensor("M_fold", [128, XH, F], F32))
        phase_a(nc, D, A_hi, A_lo, M_fold)
        phase_b(nc, D, A_hi, A_lo, M_fold)
    phase_c(nc, D)


def layouts(x, ctx_1024, mask_BxS2_bf1, L0_attn_Wq, L0_attn_bq, L0_attn_Wk, L0_attn_bk, L0_attn_Wv, L0_attn_bv,
            L0_attn_Wo, L0_attn_bo, L0_xattn_Wq, L0_xattn_Wk, L0_xattn_Wv, L0_xattn_Wo, L0_ffn_router_weight,
            L0_ffn_gate_up_proj, L0_ffn_down_proj, L0_ffn_sh_gate_w, L0_ffn_sh_up_w, L0_ffn_sh_down_w,
            L0_ffn_shared_gate_w):
    def rows(w):
        return w.reshape(KC, 128, -1).transpose(1, 0, 2)

    tokens = x.reshape(NPAIR, PAIR, F)
    moe = L0_ffn_gate_up_proj.reshape(EXPERTS, 2, I_MOE, F)
    gate = np.concatenate([moe[:, 0].reshape(-1, F), L0_ffn_sh_gate_w])
    up = np.concatenate([moe[:, 1].reshape(-1, F), L0_ffn_sh_up_w])
    return {
        "x": tokens.transpose(1, 0, 2),
        "xT": rows(x.reshape(B * S, F).T),
        "ctx": ctx_1024.reshape(B, CK, CH * CD),
        "ctxT": ctx_1024.reshape(B, CK, CH, CD).transpose(0, 3, 2, 1).reshape(B, CD, CTX),
        "mask": mask_BxS2_bf1.view(np.uint8).reshape(B, CK, CH).transpose(0, 2, 1).reshape(B, CTX),
        "wq": rows(L0_attn_Wq), "wk": rows(L0_attn_Wk), "wv": rows(L0_attn_Wv), "wo": rows(L0_attn_Wo),
        "bq": L0_attn_bq.reshape(KC, 128).T, "bk": L0_attn_bk.reshape(KC, 128).T,
        "bv": L0_attn_bv, "bo": L0_attn_bo,
        "xwqT": L0_xattn_Wq.reshape(F, XH, 128).transpose(2, 1, 0),
        "xwkT": L0_xattn_Wk.reshape(CD, XKV, 128).transpose(2, 1, 0),
        "xwvT": L0_xattn_Wv.reshape(CD, XKV, 128).transpose(2, 1, 0),
        "xwo": L0_xattn_Wo.reshape(XH, 128, F).transpose(1, 0, 2),
        "hidden": np.concatenate([rows(gate.T), rows(up.T)], axis=1),
        "down": np.concatenate([L0_ffn_down_proj.transpose(0, 2, 1).reshape(-1, F), L0_ffn_sh_down_w.T]),
        "route_w": rows(L0_ffn_router_weight.T), "route_sh": rows(L0_ffn_shared_gate_w.T),
    }


def constants():
    f = np.float32
    own_q = np.zeros((2, PAIR), f)
    own_q[0, :S] = own_q[1, S:] = 1
    other_k = np.zeros((2, SA_HEADS, PAIR), f)
    other_k[0, :, S:] = other_k[1, :, :S] = -BIG
    owner = np.zeros((2, NR, IW), f)
    for n in range(IW):
        owner[:, min(n // I_MOE, EXPERTS), n] = 1
    own_unit = {}
    for k, units in enumerate(UNITS):
        own_unit[f"own_unit{k}"] = np.zeros((2 * units, units, 128), f)
        for r in range(2 * units):
            own_unit[f"own_unit{k}"][r, r % units] = 1
    rank = np.broadcast_to(np.arange(EXPERTS, 0, -1, dtype=f), (PAIR, TILES, EXPERTS))
    return {"ident": np.eye(128, dtype=f), "own_q": own_q, "other_k": other_k.reshape(2, -1),
            **own_unit, "owner": owner.reshape(2 * NR, IW), "rank": rank}


def kernel(**inputs):
    import concourse.bacc as bacc
    from concourse.bass_utils import run_bass_kernel_spmd

    nc = bacc.Bacc("TRN2", target_bir_lowering=False, num_devices=1)
    arrays, D = {}, {}
    for name, a in {**layouts(**{k: np.asarray(v) for k, v in inputs.items()}), **constants()}.items():
        a = np.ascontiguousarray(a)
        arrays["in_" + name] = a
        D[name] = nc.dram_tensor("in_" + name, a.shape, mybir.dt.from_np(a.dtype), kind="ExternalInput").ap()
    D["y1"] = nc.dram_tensor("y1_store", (PAIR, NPAIR, F), F32, kind="Internal").ap()
    for name in ("y1T_hi", "y1T_lo"):
        D[name] = nc.dram_tensor(name + "_store", (128, NPAIR, KC, PAIR), F32, kind="Internal").ap()
    D["y2"] = nc.dram_tensor("y2_store", (PAIR, NPAIR, F), F32, kind="Internal").ap()
    D["out"] = nc.dram_tensor("out", (PAIR, NPAIR, F), F32, kind="ExternalOutput").ap()
    decoder_layer(nc, D)
    r = run_bass_kernel_spmd(nc, [arrays], core_ids=[0])
    return r.results[0]["out"].transpose(1, 0, 2).reshape(B, S, F)
```

```python
from contextlib import ExitStack

import numpy as np

import concourse.bass as bass
from concourse import mybir

ALU = mybir.AluOpType
ACT = mybir.ActivationFunctionType
AX = mybir.AxisListType
F32 = mybir.dt.float32
F32R = mybir.dt.float32r
BF16 = mybir.dt.bfloat16
U8 = mybir.dt.uint8

B, S, F = 32, 56, 256
KC = F // 128
PAIR = 2 * S
NPAIR = B // 2
TILES = 4
BLK = TILES * PAIR
NBLK = NPAIR // TILES
SA_HEADS, SA_D = 4, 64
SA_SCALE = 1.0 / np.sqrt(F // 64)
CTX, CD = 1500, 128
XH, XKV = 16, 8
X_SCALE = 1.0 / np.sqrt(128.0)
CH = 12
CK = CTX // CH
FILLS = 3
FW = CTX // FILLS
ROWS = XH * S
UNITS = (4, 3)
SLOTS = 4
WIDE = UNITS[0] * 128
EXPERTS, I_MOE, I_SH = 8, 176, 704
NR = EXPERTS + 1
IW = EXPERTS * I_MOE + I_SH
IC = -(-IW // 128)
EPS = 1e-5
BIG = 1e30


def wait_apart(engine, held, *waits):
    for semaphore, count in waits[:-1]:
        engine.wait_ge(semaphore, count)
    semaphore, count = waits[-1]
    if not isinstance(count, int):
        with engine.register() as own:
            engine.reg_add(own, count - 1, 1)
            engine.wait_ge(*held)
            engine.wait_ge(semaphore, own)
    else:
        engine.wait_ge(semaphore, count)


def norm_stats(dve, z, stats, mv, chain, count, done):
    dve.bn_stats(out=stats, in_=z).then_inc(chain, 1)
    wait_apart(dve, done, (chain, count + 1))
    dve.bn_aggr(out=mv, in_=stats).then_inc(chain, 1)
    dve.wait_ge(chain, count + 2)
    return dve.tensor_scalar(mv[:, 1:2], mv[:, 1:2], EPS, None, ALU.add)


def phase_a(nc, D, M_hi, M_lo):
    with ExitStack() as ctx:
        def sb(name, shape, dt=F32):
            return ctx.enter_context(nc.sbuf_tensor(name, shape, dt))

        def sem(name):
            return ctx.enter_context(nc.semaphore("a_" + name))

        bank = [ctx.enter_context(nc.psum_tensor(f"a_bank{j}", [128, 512], F32)) for j in range(8)]

        A_hi = sb("A_hi", [128, XH, F], F32R)
        A_lo = sb("A_lo", [128, XH, F], F32R)
        wqT = sb("a_wqT", [128, XH, F])
        wkT = sb("a_wkT", [128, XKV, CD])
        wvT = sb("a_wvT", [128, XKV, CD])
        wo = sb("a_wo", [128, XH, F])
        saw = sb("a_saw", [128, 4, KC, F])
        bqk = sb("a_bqk", [128, 2, KC])
        bv = sb("a_bv", [PAIR, F])
        bo = sb("a_bo", [PAIR, F])
        ident = sb("a_ident", [128, 128])
        own_q = sb("a_own_q", [2, PAIR])
        other_k = sb("a_other_k", [2, SA_HEADS * PAIR])
        xT = sb("a_xT", [128, KC, BLK])
        x = sb("a_x", [PAIR, TILES, F])
        xb = sb("a_xb", [PAIR, TILES, F])
        qT = sb("a_qT", [128, KC, BLK])
        kT = sb("a_kT", [128, 2, KC, BLK])
        v = sb("a_v", [PAIR, TILES, F])
        e = sb("a_e", [PAIR, TILES, SA_HEADS, PAIR])
        eT = sb("a_eT", [PAIR, TILES, SA_HEADS * PAIR])
        oT = sb("a_oT", [128, TILES, KC, PAIR])
        mx = sb("a_mx", [PAIR, TILES, SA_HEADS])
        shift = sb("a_shift", [PAIR, TILES, SA_HEADS])
        den = sb("a_den", [PAIR, TILES, SA_HEADS])
        rden = sb("a_rden", [PAIR, TILES, SA_HEADS])
        z = sb("a_z", [PAIR, TILES, F])
        y = sb("a_y", [PAIR, TILES, F])
        stats = sb("a_stats", [PAIR, TILES, 6])
        mv = sb("a_mv", [PAIR, TILES, 2])
        half = sb("a_half", [PAIR, 1])
        yT_hi = sb("a_yT_hi", [128, KC, BLK], F32R)
        yT_lo = sb("a_yT_lo", [128, KC, BLK], F32R)
        q_stage = sb("a_q_stage", [128, 2 * TILES, XH, S])

        A_loaded, M_loaded, loaded, x_loaded = sem("A_loaded"), sem("M_loaded"), sem("loaded"), sem("x_loaded")
        folded, fold_taken, fold_rest = sem("folded"), sem("fold_taken"), sem("fold_rest")
        y_turned, yT_hi_done, yT_lo_done = sem("y_turned"), sem("yT_hi_done"), sem("yT_lo_done")
        q_done = sem("q_done")
        q_taken = [sem("q_taken_even"), sem("q_taken_odd")]
        q_stored = [sem(f"q_stored{k}") for k in range(4)]
        half_set = sem("half_set")
        qk_done, qk_taken = sem("qk_done"), sem("qk_taken")
        v_done, v_taken = sem("v_done"), sem("v_taken")
        xb_done, s_done = sem("xb_done"), sem("s_done")
        max_done, shift_done, e_done = sem("max_done"), sem("shift_done"), sem("e_done")
        rden_done, e_normed = sem("rden_done"), sem("e_normed")
        eT_done, eT_taken = sem("eT_done"), sem("eT_taken")
        o_done, o_taken = sem("o_done"), sem("o_taken")
        p_done, z_done = sem("p_done"), sem("z_done")
        stat_chain, var_done, rstd_done = sem("stat_chain"), sem("var_done"), sem("rstd_done")
        y_done, y_stored = sem("y_done"), sem("y_stored")

        FOLDS = XH
        QBANK = 6
        QH = XH // 2
        PARTS = len(q_stored)
        PH = XH // PARTS

        def every_block(engine, body):
            body(0, 0)
            body(1, 1)
            with engine.Fori(2, NBLK) as i:
                body(i, 2)

        def turned(k):
            return bank[4 + k][:].rearrange("p (kc q) -> p kc q", kc=KC)[:, :, 0:2 * PAIR]

        def two_tiles(yT, k):
            return yT[:, :, k * 2 * PAIR:(k + 1) * 2 * PAIR]

        def take_head(engine, copy, j, h, past):
            if past >= 2 and h % PH < 2:
                engine.wait_ge(q_stored[h // PH], 16 * j)
            engine.wait_ge(q_done, XH * j + h + 1)
            copy(q_stage[:, :, h, :], bank[QBANK + h % 2][:, 0:BLK].rearrange("p (b q) -> p b q", q=S)).then_inc(
                q_taken[h % 2], 1)

        block = ctx.enter_context(nc.Block())

        @block.sync
        def _(sp):
            for dst, src, loads in ((wkT, D["xwkT"], A_loaded), (wqT, D["xwqT"], A_loaded), (wvT, D["xwvT"], M_loaded),
                                    (wo, D["xwo"], M_loaded)):
                sp.dma_start(dst[:], src).then_inc(loads, 16)
            sp.dma_start(xT[:], D["xT"][:, :, 0:BLK]).then_inc(x_loaded, 16)
            sp.dma_start(x[:], D["x"][:, 0:TILES, :]).then_inc(x_loaded, 16)
            for n, name in enumerate(("wq", "wk", "wv", "wo")):
                sp.dma_start(saw[:, n], D[name]).then_inc(loaded, 16)
            sp.dma_start(bqk[:, 0], D["bq"]).then_inc(loaded, 16)
            sp.dma_start(bqk[:, 1], D["bk"]).then_inc(loaded, 16)
            sp.dma_start(bv[:], D["bv"].partition_broadcast(PAIR)).then_inc(loaded, 16)
            sp.dma_start(bo[:], D["bo"].partition_broadcast(PAIR)).then_inc(loaded, 16)
            sp.dma_start(ident[:], D["ident"]).then_inc(loaded, 16)
            sp.dma_start(own_q[:], D["own_q"]).then_inc(loaded, 16)
            sp.dma_start(other_k[:], D["other_k"]).then_inc(loaded, 16)

            def load(i):
                sp.wait_ge(v_done, 2 * i)
                sp.wait_ge(xb_done, i)
                sp.dma_start(xT[:], D["xT"][:, :, bass.ts(i, BLK)]).then_inc(x_loaded, 16)
                sp.dma_start(x[:], D["x"][:, bass.ts(i, TILES), :]).then_inc(x_loaded, 16)

            def store_y(i):
                for t in range(TILES):
                    sp.wait_ge(y_done, TILES * i + t + 1)
                    sp.dma_start(D["y1"][:, bass.ds(i * TILES + t, 1), :], y[:, t:t + 1]).then_inc(y_stored, 16)

            def store_q(j, parts):
                for part in parts:
                    for k in range(2):
                        sp.wait_ge(q_taken[k], QH * j + PH // 2 * (part + 1))
                    sp.dma_start(D["q"][:, bass.ds(2 * TILES * j, 2 * TILES), part * PH * S:(part + 1) * PH * S],
                                 q_stage[:, :, part * PH:(part + 1) * PH, :].rearrange("p b h q -> p b (h q)")).then_inc(
                                     q_stored[part], 16)

            load(1)
            store_y(0)
            with sp.Fori(1, NBLK - 1) as i:
                store_q(i - 1, range(0, PARTS // 2))
                load(i + 1)
                store_q(i - 1, range(PARTS // 2, PARTS))
                store_y(i)
            store_q(NBLK - 2, range(PARTS))
            store_y(NBLK - 1)
            store_q(NBLK - 1, range(PARTS))
            sp.wait_ge(y_stored, 16 * NPAIR)
            for part in range(PARTS):
                sp.wait_ge(q_stored[part], 16 * NBLK)

        @block.tensor
        def _(pe):
            pe.wait_ge(A_loaded, 32)
            for n in range(FOLDS):
                if n == 8:
                    pe.wait_ge(M_loaded, 32)
                if n >= 8:
                    pe.wait_ge(fold_rest, n - 7)
                for k in range(2):
                    h = 2 * (n % 8) + k
                    out = bank[n % 8][:, k * F:(k + 1) * F]
                    if n < 8:
                        for kc in range(KC):
                            mm = pe.matmul(out[:, kc * 128:(kc + 1) * 128], wqT[:, h, kc * 128:(kc + 1) * 128],
                                           wkT[:, h // 2, :], start=True, stop=True)
                    else:
                        mm = pe.matmul(out, wvT[:, h // 2, :], wo[:, h, :], start=True, stop=True)
                mm.then_inc(folded, 1)
            pe.wait_ge(loaded, 16 * 11)
            pe.wait_ge(fold_rest, FOLDS)
            pe.wait_ge(half_set, 3)

            def queries(j, heads, past):
                for h in heads:
                    if h >= 2 or past >= 2:
                        pe.wait_ge(q_taken[h % 2], QH * j + h // 2)
                    terms = [(A, y, kc) for kc in range(KC) for A, y in ((A_hi, yT_hi), (A_hi, yT_lo), (A_lo, yT_hi))]
                    for n, (A, y, kc) in enumerate(terms):
                        mm = pe.matmul(bank[QBANK + h % 2][:, 0:BLK], A[:, h, kc * 128:(kc + 1) * 128],
                                       y[:, kc, :], start=(n == 0), stop=(n == len(terms) - 1))
                    mm.then_inc(q_done, 1)

            def block_pe(i, past):
                def fill_in(*heads):
                    if past:
                        queries(i - 1, heads, past)

                pe.wait_ge(x_loaded, 32 * (i + 1))
                if past:
                    pe.wait_ge(o_taken, 2 * TILES * i)
                for n in range(4):
                    for kc in range(KC):
                        mm = pe.matmul(bank[n][:, 0:BLK], saw[:, n // 2, kc, (n % 2) * 128:(n % 2 + 1) * 128],
                                       xT[:, kc, :], start=(kc == 0), stop=(kc == KC - 1))
                    mm.then_inc(qk_done, 1)
                if past:
                    pe.wait_ge(yT_lo_done, 2 * i)
                for t in range(TILES):
                    for kc in range(KC):
                        mm = pe.matmul(bank[4 + t // 2][0:PAIR, (t % 2) * F:(t % 2 + 1) * F],
                                       xT[:, kc, t * PAIR:(t + 1) * PAIR], saw[:, 2, kc, :],
                                       start=(kc == 0), stop=(kc == KC - 1))
                    if t % 2:
                        mm.then_inc(v_done, 1)
                fill_in(0)
                pe.wait_ge(qk_taken, 6 * (i + 1))
                for t in range(TILES):
                    sc = bank[t][0:PAIR, 0:SA_HEADS * PAIR]
                    for h in range(SA_HEADS):
                        mm = pe.matmul(sc[:, h * PAIR:(h + 1) * PAIR],
                                       qT[:, h // 2, t * PAIR:(t + 1) * PAIR],
                                       kT[:, h % 2, h // 2, t * PAIR:(t + 1) * PAIR],
                                       start=(h == 0), stop=False, skip_group_check=True)
                    pe.matmul(sc, own_q[:], other_k[:], start=False, stop=True, skip_group_check=True).then_inc(s_done, 1)
                fill_in(1, 2, 3)
                pe.wait_ge(v_taken, 2 * (i + 1))
                for t in range(TILES):
                    pe.wait_ge(e_normed, TILES * i + t + 1)
                    if t >= 2:
                        pe.wait_ge(eT_taken, TILES * i + t - 1)
                    for h in range(SA_HEADS):
                        mm = pe.transpose(bank[4 + t % 2][0:PAIR, h * PAIR:(h + 1) * PAIR], e[:, t, h, :],
                                          ident[0:PAIR, 0:PAIR])
                    mm.then_inc(eT_done, 1)
                    fill_in(4 + t)
                for t in range(TILES):
                    pe.wait_ge(eT_taken, TILES * i + t + 1)
                    for m in range(KC):
                        mm = pe.matmul(bank[t][:, m * 2 * PAIR:(m + 1) * 2 * PAIR], v[:, t, m * 128:(m + 1) * 128],
                                       eT[:, t, m * 2 * PAIR:(m + 1) * 2 * PAIR], start=True, stop=True)
                    mm.then_inc(o_done, 1)
                fill_in(8, 9)
                for t in range(TILES):
                    pe.wait_ge(o_taken, 2 * (TILES * i + t + 1))
                    for m in range(KC):
                        mm = pe.matmul(bank[4 + t // 2][0:PAIR, (t % 2) * F:(t % 2 + 1) * F], oT[:, t, m, :], saw[:, 3, m, :],
                                       start=(m == 0), stop=(m == KC - 1))
                    if t % 2:
                        mm.then_inc(p_done, 1)
                fill_in(10, 11, 12, 13, 14, 15)
                for t in range(TILES):
                    pe.wait_ge(y_done, TILES * i + t + 1)
                    for kc in range(KC):
                        mm = pe.transpose(turned(t // 2)[:, kc, (t % 2) * PAIR:(t % 2 + 1) * PAIR], y[:, t, kc * 128:(kc + 1) * 128],
                                          ident[0:PAIR, 0:PAIR])
                    if t % 2:
                        mm.then_inc(y_turned, 1)

            every_block(pe, block_pe)
            pe.wait_ge(yT_lo_done, 2 * NBLK)
            queries(NBLK - 1, range(XH), 2)

        @block.scalar
        def _(act):
            for n in range(FOLDS):
                act.wait_ge(folded, n + 1)
                dst = (A_hi if n < 8 else M_hi)[:, 2 * (n % 8):2 * (n % 8) + 2, :]
                act.copy(dst, bank[n % 8][:].rearrange("p (a n) -> p a n", a=2)).then_inc(fold_taken, 1)
            act.wait_ge(loaded, 16 * 11)

            def block_act(i, past):
                def take(*heads):
                    if past:
                        for h in heads:
                            take_head(act, act.copy, i - 1, h, past)

                for m in range(KC):
                    act.wait_ge(qk_done, 4 * i + m + 1)
                    act.activation(qT[:, m, :], bank[m][:, 0:BLK], ACT.Identity,
                                   bias=bqk[:, 0, m:m + 1]).then_inc(qk_taken, 1)
                for m in range(KC):
                    act.wait_ge(qk_done, 4 * i + KC + m + 1)
                    for k in range(2):
                        own = slice(SA_D * k, SA_D * (k + 1))
                        act.activation(kT[own, k, m, :], bank[KC + m][own, 0:BLK], ACT.Identity,
                                       bias=bqk[own, 1, m:m + 1]).then_inc(qk_taken, 1)
                take(0)
                for t in range(TILES):
                    act.wait_ge(shift_done, TILES * i + t + 1)
                    for h in range(SA_HEADS):
                        act.activation(e[:, t, h, :], bank[t][0:PAIR, h * PAIR:(h + 1) * PAIR], ACT.Exp,
                                       bias=shift[:, t, h:h + 1], scale=float(SA_SCALE),
                                       accum_out=den[:, t, h:h + 1]).then_inc(e_done, 1)
                    if t == 1:
                        take(2)
                for t in range(TILES):
                    act.wait_ge(eT_done, TILES * i + t + 1)
                    act.copy(eT[:, t, :], bank[4 + t % 2][0:PAIR, 0:SA_HEADS * PAIR]).then_inc(eT_taken, 1)
                    if t % 2 == 0:
                        take(4 + t)
                take(8, 10, 12, 14)
                for k in range(2):
                    act.wait_ge(y_turned, 2 * i + k + 1)
                    act.copy(two_tiles(yT_hi, k), turned(k)).then_inc(yT_hi_done, 1)

            every_block(act, block_act)
            for h in range(0, XH, 2):
                take_head(act, act.copy, NBLK - 1, h, 2)

        @block.vector
        def _(dve):
            dve.memset(half[:], -0.5).then_inc(half_set, 1)
            dve.memset(kT[SA_D:, 0], 0.0).then_inc(half_set, 1)
            dve.memset(kT[:SA_D, 1], 0.0).then_inc(half_set, 1)
            for n in range(FOLDS):
                dve.wait_ge(fold_taken, n + 1)
                hi, lo = (A_hi, A_lo) if n < 8 else (M_hi, M_lo)
                part = (slice(None), slice(2 * (n % 8), 2 * (n % 8) + 2))
                dve.tensor_tensor(lo[part], bank[n % 8][:].rearrange("p (a n) -> p a n", a=2),
                                  hi[part].bitcast(F32), ALU.subtract).then_inc(fold_rest, 1)
            dve.wait_ge(loaded, 16 * 11)

            def block_dve(i, past):
                def take(*heads):
                    if past:
                        for h in heads:
                            take_head(dve, dve.tensor_copy, i - 1, h, past)

                for n in range(2):
                    dve.wait_ge(v_done, 2 * i + n + 1)
                    dve.tensor_tensor(v[:, 2 * n:2 * n + 2, :],
                                      bank[4 + n][0:PAIR, :].rearrange("p (t f) -> p t f", t=2),
                                      bv[:].unsqueeze(1).to_broadcast([PAIR, 2, F]), ALU.add).then_inc(v_taken, 1)
                for t in range(TILES):
                    dve.wait_ge(s_done, TILES * i + t + 1)
                    dve.tensor_reduce(mx[:, t, :], bank[t][0:PAIR, 0:SA_HEADS * PAIR].rearrange(
                        "p (h k) -> p h k", h=SA_HEADS), AX.X, ALU.max).then_inc(max_done, 1)
                    dve.wait_ge(max_done, TILES * i + t + 1)
                    dve.tensor_scalar(shift[:, t, :], mx[:, t, :], -float(SA_SCALE), None,
                                      ALU.mult).then_inc(shift_done, 1)
                take(1)
                for t in range(TILES):
                    dve.wait_ge(e_done, SA_HEADS * (TILES * i + t + 1))
                    dve.reciprocal(rden[:, t, :], den[:, t, :]).then_inc(rden_done, 1)
                    dve.wait_ge(rden_done, TILES * i + t + 1)
                    dve.tensor_tensor(e[:, t], e[:, t], rden[:, t, :].unsqueeze(2).to_broadcast(
                        [PAIR, SA_HEADS, PAIR]), ALU.mult).then_inc(e_normed, 1)
                    if t == 1:
                        take(3)
                take(5, 7)
                for t in range(TILES):
                    dve.wait_ge(o_done, TILES * i + t + 1)
                    for k in range(2):
                        p0 = SA_D * k
                        dve.tensor_copy(oT[p0:p0 + SA_D, t], bank[t][p0:p0 + SA_D, 0:4 * PAIR].rearrange(
                            "p (m k q) -> p m k q", m=KC, k=2)[:, :, k, :]).then_inc(o_taken, 1)
                take(9)
                dve.wait_ge(xb_done, i + 1)
                for t in range(TILES):
                    n = TILES * i + t
                    if t % 2 == 0:
                        dve.wait_ge(p_done, 2 * i + t // 2 + 1)
                    dve.tensor_tensor(z[:, t, :], bank[4 + t // 2][0:PAIR, (t % 2) * F:(t % 2 + 1) * F], xb[:, t, :], ALU.add).then_inc(z_done, 1)
                    dve.wait_ge(z_done, n + 1)
                    norm_stats(dve, z[:, t, :], stats[:, t, :], mv[:, t, :], stat_chain, 2 * n, (loaded, 16)).then_inc(var_done, 1)
                take(11)
                for t in range(TILES):
                    n = TILES * i + t
                    dve.wait_ge(rstd_done, n + 1)
                    if past and t == 0:
                        dve.wait_ge(y_stored, 16 * TILES * i)
                    dve.tensor_scalar(y[:, t, :], z[:, t, :], mv[:, t, 0:1], mv[:, t, 1:2],
                                      ALU.subtract, ALU.mult).then_inc(y_done, 1)
                take(13, 15)
                for k in range(2):
                    dve.wait_ge(yT_hi_done, 2 * i + k + 1)
                    dve.tensor_tensor(two_tiles(yT_lo, k), turned(k), two_tiles(yT_hi, k).bitcast(F32),
                                      ALU.subtract).then_inc(yT_lo_done, 1)

            every_block(dve, block_dve)
            for h in range(1, XH, 2):
                take_head(dve, dve.tensor_copy, NBLK - 1, h, 2)

        @block.gpsimd
        def _(pool):
            pool.wait_ge(loaded, 16 * 11)
            pool.wait_ge(half_set, 1)

            def block_pool(i, past):
                pool.wait_ge(x_loaded, 32 * (i + 1))
                if past:
                    pool.wait_ge(z_done, TILES * i)
                pool.tensor_tensor(xb[:], x[:], bo[:].unsqueeze(1).to_broadcast([PAIR, TILES, F]),
                                   ALU.add).then_inc(xb_done, 1)
                for t in range(TILES):
                    pool.wait_ge(var_done, TILES * i + t + 1)
                    pool.tensor_tensor(mv[:, t, 1:2], mv[:, t, 1:2], half[:], ALU.pow).then_inc(rstd_done, 1)

            every_block(pool, block_pool)


def phase_b(nc, D, M_hi, M_lo):
    with ExitStack() as ctx:
        def sb(name, shape, dt=F32):
            return ctx.enter_context(nc.sbuf_tensor("b_" + name, shape, dt))

        def sem(name):
            return ctx.enter_context(nc.semaphore("b_" + name))

        def ps(name):
            return ctx.enter_context(nc.psum_tensor("b_" + name, [128, 512], F32))

        score_bank = [ps(f"score{j}") for j in range(FILLS)]
        turn_bank = [ps(f"turn{j}") for j in range(3)]
        out_bank = ps("out")
        misc_bank = ps("misc")

        ident = sb("ident", [128, 128])
        ones_r = sb("ones_r", [2 * UNITS[0], 128], F32R)
        own_unit = [sb(f"own_unit{k}", [2 * UNITS[k], UNITS[k], 128]) for k in range(2)]
        half = sb("half", [PAIR, 1])
        q_in = sb("q_in", [128, ROWS])
        q_hi = sb("q_hi", [128, 2, ROWS], F32R)
        q_lo = sb("q_lo", [128, 2, ROWS], F32R)
        cT_in = sb("cT_in", [128, CTX])
        cT_hi = sb("cT_hi", [128, 2, CTX], F32R)
        cT_lo = sb("cT_lo", [128, 2, CTX], F32R)
        c_in = sb("c_in", [CK, CH * CD])
        c_hi = sb("c_hi", [CK, 2, CH * CD], F32R)
        c_lo = sb("c_lo", [CK, 2, CH * CD], F32R)
        mask_in = sb("mask_in", [128, CTX], U8)
        mask_add = sb("mask_add", [128, 2, CTX], BF16)
        p = [sb(f"p{k}", [128, UNITS[k], CTX]) for k in range(2)]
        top = sb("top", [128, 2, UNITS[0], FILLS])
        top3 = sb("top3", [128, FILLS])
        shift = sb("shift", [128, 2, UNITS[0]])
        den = sb("den", [128, 2, UNITS[0]])
        keep = sb("keep", [128, UNITS[0]])
        rden = sb("rden", [128, UNITS[0]])
        rden_parts = sb("rden_parts", [128, 2 * UNITS[0]])
        rden_r = sb("rden_r", [128, UNITS[0]], F32R)
        rden_rows = sb("rden_rows", [2 * UNITS[0], WIDE], F32R)
        pT_hi = sb("pT_hi", [CK, 3, WIDE], F32R)
        pT_lo = sb("pT_lo", [CK, 3, WIDE], F32R)
        out_sb = sb("out_sb", [128, WIDE])
        oT = sb("oT", [128, XH, 2, S])
        oT_hi = sb("oT_hi", [128, XH, 2, S], F32R)
        oT_lo = sb("oT_lo", [128, XH, 2, S], F32R)
        y1_res = sb("y1_res", [PAIR, F])
        z = sb("z", [PAIR, F])
        y2 = sb("y2", [PAIR, F])
        stats = sb("stats", [PAIR, 6])
        mv = sb("mv", [PAIR, 2])

        const_loaded, const_set = sem("const_loaded"), sem("const_set")
        q_loaded, cT_loaded, c_loaded, mask_loaded = sem("q_loaded"), sem("cT_loaded"), sem("c_loaded"), sem("mask_loaded")
        res_loaded, y2_stored = sem("res_loaded"), sem("y2_stored")
        q_split, cT_split, c_split, mask_ready = sem("q_split"), sem("cT_split"), sem("c_split"), sem("mask_ready")
        fill_done, fill_taken = sem("fill_done"), sem("fill_taken")
        shift_done, exp_done = sem("shift_done"), sem("exp_done")
        turned, hi_done, lo_done, pv_done = sem("turned"), sem("hi_done"), sem("lo_done"), sem("pv_done")
        out_copied = sem("out_copied")
        rden_chain, rden_turned, rows_done, spread_done = sem("rden_chain"), sem("rden_turned"), sem("rows_done"), sem("spread_done")
        oT_done, oT_hi_done, oT_lo_done, proj_done = sem("oT_done"), sem("oT_hi_done"), sem("oT_lo_done"), sem("proj_done")
        z_done, stat_chain, var_done, rstd_done, y2_done = sem("z_done"), sem("stat_chain"), sem("var_done"), sem("rstd_done"), sem("y2_done")

        CONSTS = 3
        STEPS = SLOTS * CH
        TURN_LAG = CH + 3
        PV_LAG = TURN_LAG + 2
        RDEN_AT, TURN_RDEN_AT = 6, 11
        ROWS_AT, SPREAD_AT, COPY_AT, SCALE_AT, ROUND_AT, REST_AT = 1, 4, 5, 5, 6, 7
        PROJECT_AT, NORM_OUT_AT = CH + 9, 2 * CH + 1
        RDEN = 6
        OT_OPS = 2
        TAIL = PV_LAG + 3

        def units(slot):
            return UNITS[slot % 2]

        unit0 = [sum(units(k) for k in range(slot)) for slot in range(SLOTS + 1)]
        PUNITS = unit0[SLOTS]
        PFILLS = FILLS * PUNITS

        def fills_at(n):
            slot, k = n // CH, n % CH
            count = FILLS * units(slot)
            return [(slot, m) for m in range(count) if m * CH // count == k]

        def slot_before(i, slot, k):
            return i + (slot - k) // SLOTS, (slot - k) % SLOTS

        def lagging(i, n, lag, first, last):
            if (first and n < lag) or (last and n - lag >= STEPS):
                return None
            return i + (n - lag) // STEPS, (n - lag) % STEPS

        def lagging_slot(i, n, k, first, last):
            slot = n // CH
            if (first and slot < k) or (last and slot - k >= SLOTS):
                return None
            return slot_before(i, slot, k)

        block = ctx.enter_context(nc.Block())

        @block.sync
        def _(sp):
            sp.dma_start(ident[:], D["ident"]).then_inc(const_loaded, 16)
            for k in range(2):
                sp.dma_start(own_unit[k][:], D[f"own_unit{k}"]).then_inc(const_loaded, 16)

            def load_q(i, b, first=False):
                if not first:
                    sp.wait_ge(q_split, 2 * (2 * i + b))
                sp.dma_start(q_in[:], D["q"][:, bass.ds(2 * i + b, 1)].rearrange("p a n -> p (a n)")).then_inc(q_loaded, 16)

            def load_batch(i, b, first=False):
                n = 2 * i + b
                if not (first and b == 0):
                    sp.wait_ge(cT_split, 2 * n)
                sp.dma_start(cT_in[:], D["ctxT"][bass.ds(n, 1)].rearrange("a d s -> (a d) s")).then_inc(cT_loaded, 16)
                if not (first and b == 0):
                    wait_apart(sp, (const_loaded, 16), (mask_ready, n))
                sp.dma_start(mask_in[:], D["mask"][bass.ds(n, 1)].rearrange("a s -> (a s)").partition_broadcast(
                    128)).then_inc(mask_loaded, 16)
                if not (first and b == 0):
                    sp.wait_ge(c_split, 2 * n)
                sp.dma_start(c_in[:], D["ctx"][bass.ds(n, 1)].rearrange("a p n -> (a p) n")).then_inc(c_loaded, 16)

            def residual(i):
                sp.dma_start(y1_res[:], D["y1"][:, bass.ds(i, 1), :].rearrange("p a f -> p (a f)")).then_inc(res_loaded, 16)

            def store(i):
                sp.wait_ge(y2_done, i + 1)
                sp.dma_start(D["y2"][:, bass.ds(i, 1), :].rearrange("p a f -> p (a f)"), y2[:]).then_inc(y2_stored, 16)

            load_q(0, 0, first=True)
            load_batch(0, 0, first=True)
            load_q(0, 1)
            load_batch(0, 1, first=True)
            residual(0)
            with sp.Fori(1, NPAIR) as i:
                for b in range(2):
                    load_q(i, b)
                    load_batch(i, b)
                store(i - 1)
                residual(i)
            store(NPAIR - 1)
            sp.wait_ge(y2_stored, 16 * NPAIR)

        @block.tensor
        def _(pe):
            pe.wait_ge(const_loaded, 16 * CONSTS)
            pe.wait_ge(const_set, 3)

            def fill(i, slot, m, first):
                u, j, b = m // FILLS, m % FILLS, slot // 2
                n = FILLS * unit0[slot] + m
                if m == 0 and slot % 2 == 0:
                    pe.wait_ge(q_split, 2 * (2 * i + b + 1))
                    pe.wait_ge(cT_split, 2 * (2 * i + b + 1))
                if not (first and n < FILLS):
                    pe.wait_ge(fill_taken, PFILLS * i + n - FILLS + 1)
                out = score_bank[j][:, 0:FW]
                keys = slice(j * FW, (j + 1) * FW)
                rows = slice(WIDE * (slot % 2) + 128 * u, WIDE * (slot % 2) + 128 * (u + 1))
                pe.matmul(out, q_hi[:, b, rows], cT_hi[:, b, keys], start=True, stop=False)
                pe.matmul(out, q_hi[:, b, rows], cT_lo[:, b, keys], start=False, stop=False)
                pe.matmul(out, q_lo[:, b, rows], cT_hi[:, b, keys], start=False, stop=True).then_inc(fill_done, 1)

            def turn(i, n, first):
                slot, c = n // CH, n % CH
                if c == 0:
                    pe.wait_ge(exp_done, PUNITS * i + unit0[slot + 1])
                if not (first and n < 3):
                    pe.wait_ge(lo_done, STEPS * i + n - 2)
                for u in range(units(slot)):
                    mm = pe.transpose(turn_bank[n % 3][0:CK, u * 128:(u + 1) * 128],
                                      p[slot % 2][:, u, c * CK:(c + 1) * CK], ident[:])
                mm.then_inc(turned, 1)

            def weigh(i, n, first):
                slot, c = n // CH, n % CH
                b, w = slot // 2, 128 * units(slot)
                if c == 0:
                    if not (first and slot == 0):
                        pe.wait_ge(out_copied, SLOTS * i + slot)
                    pe.wait_ge(c_split, 2 * (2 * i + b + 1))
                pe.wait_ge(lo_done, STEPS * i + n + 1)
                out = out_bank[:, 0:w]
                hi, lo = c_hi[:, b, c * CD:(c + 1) * CD], c_lo[:, b, c * CD:(c + 1) * CD]
                pe.matmul(out, hi, pT_hi[:, n % 3, 0:w], start=(c == 0), stop=False)
                pe.matmul(out, hi, pT_lo[:, n % 3, 0:w], start=False, stop=False)
                pe.matmul(out, lo, pT_hi[:, n % 3, 0:w], start=False, stop=(c == CH - 1)).then_inc(pv_done, 1)

            def turn_rden(i, slot, first):
                s = SLOTS * i + slot
                if not (first and slot == 0):
                    pe.wait_ge(oT_done, OT_OPS * s)
                if slot == 0 and not first:
                    pe.wait_ge(z_done, i)
                pe.wait_ge(rden_chain, RDEN * (s + 1))
                pe.transpose(misc_bank[0:2 * units(slot), 0:128], rden_parts[:, 0:2 * units(slot)],
                             ident[:]).then_inc(rden_turned, 1)

            def spread_rden(i, slot):
                u = units(slot)
                pe.wait_ge(rows_done, SLOTS * i + slot + 1)
                pe.matmul(misc_bank[:, 0:128 * u], ones_r[0:2 * u, :], rden_rows[0:2 * u, 0:128 * u],
                          start=True, stop=True).then_inc(spread_done, 1)

            def project(i):
                pe.wait_ge(oT_lo_done, 2 * (i + 1))
                for h in range(XH):
                    terms = ((oT_hi, M_hi), (oT_hi, M_lo), (oT_lo, M_hi))
                    for n, (o, M) in enumerate(terms):
                        mm = pe.matmul(misc_bank[0:PAIR, 0:F], o[:, h].rearrange("p b q -> p (b q)"), M[:, h, :],
                                       start=(h == 0 and n == 0), stop=(h == XH - 1 and n == len(terms) - 1))
                mm.then_inc(proj_done, 1)

            def lag_step(i, n, first, last=False):
                if at := lagging(i, n, TURN_LAG, first, last):
                    turn(*at, first)
                if at := lagging(i, n, PV_LAG, first, last):
                    weigh(*at, first)
                if n % CH == TURN_RDEN_AT and (at := lagging_slot(i, n, 1, first, last)):
                    turn_rden(*at, first)
                if n % CH == SPREAD_AT and (at := lagging_slot(i, n, 2, first, last)):
                    spread_rden(*at)
                if n == PROJECT_AT and not first:
                    project(i - 1)

            def pair_pe(i, first=False):
                for n in range(STEPS):
                    for slot, m in fills_at(n):
                        fill(i, slot, m, first)
                    lag_step(i, n, first)

            pair_pe(0, first=True)
            with pe.Fori(1, NPAIR) as i:
                pair_pe(i)
            for n in range(STEPS, STEPS + TAIL):
                lag_step(NPAIR - 1, n, False, last=True)
            project(NPAIR - 1)

        @block.scalar
        def _(act):
            def p_round(i, n, first):
                g, w = STEPS * i + n, 128 * units(n // CH)
                act.wait_ge(turned, g + 1)
                if not (first and n < 3):
                    act.wait_ge(pv_done, g - 2)
                act.copy(pT_hi[:, n % 3, 0:w], turn_bank[n % 3][0:CK, 0:w]).then_inc(hi_done, 1)

            def exps(i, slot, u):
                act.wait_ge(shift_done, PUNITS * i + unit0[slot] + u + 1)
                row = p[slot % 2][:, u, :]
                act.activation(row, row, ACT.Exp, bias=shift[:, slot % 2, u:u + 1], scale=float(X_SCALE),
                               accum_out=den[:, slot % 2, u:u + 1]).then_inc(exp_done, 1)

            def out_copy(i, slot, first):
                w = 128 * units(slot)
                if not (first and slot == 0):
                    act.wait_ge(oT_done, OT_OPS * (SLOTS * i + slot))
                act.wait_ge(pv_done, CH * (SLOTS * i + slot + 1))
                act.copy(out_sb[:, 0:w], out_bank[:, 0:w]).then_inc(out_copied, 1)

            def oT_round(i, slot):
                b = slot // 2
                act.wait_ge(oT_done, OT_OPS * (SLOTS * i + slot + 1))
                act.copy(oT_hi[:, :, b, :], oT[:, :, b, :]).then_inc(oT_hi_done, 1)

            def exp_step(i, n, first, last=False):
                if at := lagging(i, n, 1, first, last):
                    for slot, m in fills_at(at[1]):
                        if m % FILLS == FILLS - 1:
                            exps(at[0], slot, m // FILLS)

            def lag_step(i, n, first, last=False):
                if n % CH == COPY_AT and (at := lagging_slot(i, n, 2, first, last)):
                    out_copy(*at, first)
                if at := lagging(i, n, TURN_LAG, first, last):
                    p_round(*at, first)
                if n % CH == ROUND_AT and (at := lagging_slot(i, n, 2, first, last)) and at[1] % 2:
                    oT_round(*at)

            def pair_act(i, first=False):
                for n in range(STEPS):
                    lag_step(i, n, first)
                    exp_step(i, n, first)

            pair_act(0, first=True)
            with act.Fori(1, NPAIR) as i:
                pair_act(i)
            for n in range(STEPS, STEPS + TAIL):
                lag_step(NPAIR - 1, n, False, last=True)
                exp_step(NPAIR - 1, n, False, last=True)

        @block.vector
        def _(dve):
            dve.memset(half[:], -0.5).then_inc(const_set, 1)
            dve.memset(out_sb[0:2 * UNITS[0], 0:128], 1.0).then_inc(const_set, 1)
            dve.wait_ge(const_set, 2)
            dve.tensor_copy(ones_r[:], out_sb[0:2 * UNITS[0], 0:128]).then_inc(const_set, 1)
            dve.wait_ge(const_loaded, 16 * CONSTS)

            def scores(i, slot, m, first):
                u, j, b = m // FILLS, m % FILLS, slot // 2
                waits = [(fill_done, PFILLS * i + FILLS * unit0[slot] + m + 1)]
                if m == 0 and slot % 2 == 0:
                    waits.append((mask_ready, 2 * i + b + 1))
                if u == 0 and not (first and slot < 2):
                    waits.append((turned, CH * (SLOTS * i + slot - 2) + (j + 1) * (CH // FILLS)))
                wait_apart(dve, (const_loaded, 16 * CONSTS), *waits)
                keys = slice(j * FW, (j + 1) * FW)
                dve.tensor_tensor_reduce(out=p[slot % 2][:, u, keys], in0=score_bank[j][:, 0:FW],
                                         in1=mask_add[:, b, keys], scale=1.0, scalar=-3.0e38,
                                         op0=ALU.add, op1=ALU.max,
                                         accum_out=top[:, slot % 2, u, j:j + 1]).then_inc(fill_taken, 1)

            def shifts(i, slot, u):
                dve.wait_ge(fill_taken, PFILLS * i + FILLS * (unit0[slot] + u + 1))
                dve.tensor_scalar(top3[:], top[:, slot % 2, u, :], -float(X_SCALE), None, ALU.mult, ALU.min,
                                  accum_out=shift[:, slot % 2, u:u + 1]).then_inc(shift_done, 1)

            def p_rest(i, n):
                w = 128 * units(n // CH)
                dve.wait_ge(hi_done, STEPS * i + n + 1)
                dve.tensor_tensor(pT_lo[:, n % 3, 0:w], turn_bank[n % 3][0:CK, 0:w],
                                  pT_hi[:, n % 3, 0:w].bitcast(F32), ALU.subtract).then_inc(lo_done, 1)

            def reciprocals(i, slot):
                s, par, u = SLOTS * i + slot, slot % 2, units(slot)
                dve.wait_ge(exp_done, PUNITS * i + unit0[slot + 1])
                dve.tensor_scalar(keep[:, 0:u], shift[:, par, 0:u], float(X_SCALE * BIG / 2), None,
                                  ALU.is_lt).then_inc(rden_chain, 1)
                dve.reciprocal(rden[:, 0:u], den[:, par, 0:u]).then_inc(rden_chain, 1)
                dve.wait_ge(rden_chain, RDEN * s + 2)
                dve.tensor_tensor(rden[:, 0:u], rden[:, 0:u], keep[:, 0:u], ALU.mult).then_inc(rden_chain, 1)
                dve.wait_ge(rden_chain, RDEN * s + 3)
                dve.tensor_copy(rden_r[:, 0:u], rden[:, 0:u]).then_inc(rden_chain, 1)
                dve.wait_ge(rden_chain, RDEN * s + 4)
                dve.tensor_copy(rden_parts[:, 0:u], rden_r[:, 0:u].bitcast(F32)).then_inc(rden_chain, 1)
                dve.tensor_tensor(rden_parts[:, u:2 * u], rden[:, 0:u], rden_r[:, 0:u].bitcast(F32),
                                  ALU.subtract).then_inc(rden_chain, 1)

            def rows(i, slot):
                u = units(slot)
                dve.wait_ge(rden_turned, SLOTS * i + slot + 1)
                dve.tensor_tensor(rden_rows[0:2 * u, 0:128 * u].rearrange("r (u q) -> r u q", u=u),
                                  misc_bank[0:2 * u, 0:128].unsqueeze(1).to_broadcast([2 * u, u, 128]),
                                  own_unit[slot % 2][:], ALU.mult).then_inc(rows_done, 1)

            def scale_out(i, slot, first):
                s, b = SLOTS * i + slot, slot // 2
                shared, cut = WIDE // S, WIDE % S
                dve.wait_ge(out_copied, s + 1)
                dve.wait_ge(spread_done, s + 1)
                if slot == 0 and not first:
                    dve.wait_ge(proj_done, i)
                if slot % 2 == 0:
                    whole, r0 = range(0, shared), 0
                    part, q0 = slice(shared * S, WIDE), 0
                else:
                    whole, r0 = range(shared + 1, XH), S - cut
                    part, q0 = slice(0, S - cut), cut
                cols = slice(r0, r0 + S * len(whole))
                dve.tensor_tensor(oT[:, whole[0]:whole[-1] + 1, b, :],
                                  misc_bank[:, cols].rearrange("p (h q) -> p h q", q=S),
                                  out_sb[:, cols].rearrange("p (h q) -> p h q", q=S), ALU.mult).then_inc(oT_done, 1)
                dve.tensor_tensor(oT[:, shared, b, q0:q0 + part.stop - part.start], misc_bank[:, part], out_sb[:, part],
                                  ALU.mult).then_inc(oT_done, 1)

            def oT_rest(i, slot):
                b = slot // 2
                dve.wait_ge(oT_hi_done, 2 * i + b + 1)
                dve.tensor_tensor(oT_lo[:, :, b, :], oT[:, :, b, :], oT_hi[:, :, b, :].bitcast(F32),
                                  ALU.subtract).then_inc(oT_lo_done, 1)

            def norm(i):
                dve.wait_ge(proj_done, i + 1)
                dve.wait_ge(res_loaded, 16 * (i + 1))
                dve.tensor_tensor(z[:], misc_bank[0:PAIR, 0:F], y1_res[:], ALU.add).then_inc(z_done, 1)
                dve.wait_ge(z_done, i + 1)
                norm_stats(dve, z[:], stats[:], mv[:], stat_chain, 2 * i, (const_loaded, 32)).then_inc(var_done, 1)

            def norm_out(i, first=False):
                dve.wait_ge(rstd_done, i + 1)
                if not first:
                    dve.wait_ge(y2_stored, 16 * i)
                dve.tensor_scalar(y2[:], z[:], mv[:, 0:1], mv[:, 1:2], ALU.subtract, ALU.mult).then_inc(y2_done, 1)

            def fill_step(i, n, first):
                for slot, m in fills_at(n):
                    scores(i, slot, m, first)
                    if m % FILLS == FILLS - 1:
                        shifts(i, slot, m // FILLS)

            def lag_step(i, n, first, last=False):
                if at := lagging(i, n, TURN_LAG, first, last):
                    p_rest(*at)
                if n % CH == SCALE_AT and (at := lagging_slot(i, n, 2, first, last)):
                    scale_out(*at, first)
                if n % CH == RDEN_AT and (at := lagging_slot(i, n, 1, first, last)):
                    reciprocals(*at)
                if n % CH == REST_AT and (at := lagging_slot(i, n, 2, first, last)) and at[1] % 2:
                    oT_rest(*at)
                if n % CH == ROWS_AT and (at := lagging_slot(i, n, 2, first, last)):
                    rows(*at)
                if n == PROJECT_AT and not first:
                    norm(i - 1)
                if n == NORM_OUT_AT and not first:
                    norm_out(i - 1)

            def pair_dve(i, first=False):
                for n in range(STEPS):
                    fill_step(i, n, first)
                    lag_step(i, n, first)

            pair_dve(0, first=True)
            with dve.Fori(1, NPAIR) as i:
                pair_dve(i)
            for n in range(STEPS, STEPS + TAIL):
                lag_step(NPAIR - 1, n, False, last=True)
            norm(NPAIR - 1)
            norm_out(NPAIR - 1)

        @block.gpsimd
        def _(pool):
            pool.wait_ge(const_set, 1)

            def split(hi, lo, src, loaded, loads, done, free, count, i, b, first):
                n = 2 * i + b
                waits = [(loaded, 16 * loads)]
                if not first:
                    waits.append((free, count))
                wait_apart(pool, (const_set, 1), *waits)
                pool.tensor_scalar(hi[:, b, :], src, 1.0, 0.0, ALU.mult, ALU.add).then_inc(done, 1)
                pool.wait_ge(done, 2 * n + 1)
                pool.tensor_tensor(lo[:, b, :], src, hi[:, b, :].bitcast(F32), ALU.subtract).then_inc(done, 1)

            def mask_bias(i, b, first):
                n = 2 * i + b
                waits = [(mask_loaded, 16 * (n + 1))]
                if not first:
                    waits.append((fill_taken, PFILLS * (i - 1) + FILLS * unit0[2 * b + 2]))
                wait_apart(pool, (const_set, 1), *waits)
                pool.tensor_scalar(mask_add[:, b, :], mask_in[:], BIG, -BIG, ALU.mult, ALU.add).then_inc(mask_ready, 1)

            def rstd(i):
                pool.wait_ge(var_done, i + 1)
                pool.tensor_tensor(mv[:, 1:2], mv[:, 1:2], half[:], ALU.pow).then_inc(rstd_done, 1)

            def batch(i, b, first):
                n = 2 * i + b
                filled = PFILLS * (i - 1) + FILLS * unit0[2 * b + 2]
                split(q_hi, q_lo, q_in[:], q_loaded, n + 1, q_split, fill_done, filled, i, b, first)
                split(cT_hi, cT_lo, cT_in[:], cT_loaded, n + 1, cT_split, fill_done, filled, i, b, first)
                mask_bias(i, b, first)
                split(c_hi, c_lo, c_in[:], c_loaded, n + 1, c_split, pv_done, 2 * CH * (n - 1), i, b, first)

            for b in range(2):
                batch(0, b, True)
            with pool.Fori(1, NPAIR) as i:
                batch(i, 0, False)
                batch(i, 1, False)
                rstd(i - 1)
            rstd(NPAIR - 1)


def phase_c(nc, D):
    with ExitStack() as ctx:
        def sb(name, shape, dt=F32):
            return ctx.enter_context(nc.sbuf_tensor("c_" + name, shape, dt))

        def sem(name):
            return ctx.enter_context(nc.semaphore("c_" + name))

        def ps(name):
            return ctx.enter_context(nc.psum_tensor("c_" + name, [128, 512], F32))

        gate_bank = [ps(f"gate{j}") for j in range(2)]
        up_bank = [ps(f"up{j}") for j in range(2)]
        down_bank = [ps(f"down{j}") for j in range(2)]
        comb_bank, misc_bank = ps("comb"), ps("misc")

        W_IN, W_SLOTS = 2 * KC, 4
        w_in = sb("w_in", [128, W_SLOTS, W_IN + 2, 128])
        w_hi = sb("w_hi", [128, IC, W_IN + 2, 128], F32R)
        w_lo = sb("w_lo", [128, IC, W_IN + 2, 128], F32R)
        w_route = sb("w_route", [128, KC, NR])
        owner_in = sb("owner_in", [2 * NR, IW])
        owner = sb("owner", [2 * NR, IW], F32R)
        ident = sb("ident", [128, 128])
        rank = sb("rank", [PAIR, TILES, EXPERTS])
        half = sb("half", [PAIR, 1])
        y2 = sb("y2", [PAIR, TILES, F])
        y2_res = sb("y2_res", [PAIR, TILES, F])
        y2T = sb("y2T", [128, KC, BLK])
        y2T_hi = sb("y2T_hi", [128, KC, BLK], F32R)
        y2T_lo = sb("y2T_lo", [128, KC, BLK], F32R)
        logit = sb("logit", [PAIR, TILES, NR])
        ex = sb("ex", [PAIR, TILES, NR])
        best = sb("best", [PAIR, 2, TILES])
        rest = sb("rest", [PAIR, TILES, EXPERTS])
        pick = sb("pick", [PAIR, 2, TILES, EXPERTS])
        first_of = sb("first_of", [PAIR, TILES])
        total = sb("total", [PAIR, TILES])
        combine = sb("combine", [PAIR, TILES, NR])
        combine_r = sb("combine_r", [PAIR, TILES, NR], F32R)
        combine_parts = sb("combine_parts", [PAIR, TILES, 2 * NR])
        combT = sb("combT", [2 * NR, BLK], F32R)
        act_g = sb("act_g", [128, 2, BLK])
        act_gu = sb("act_gu", [128, 2, BLK])
        h = sb("h", [128, 2, BLK])
        H_DEEP = 3
        h_hi = sb("h_hi", [128, H_DEEP, BLK], F32R)
        h_lo = sb("h_lo", [128, H_DEEP, BLK], F32R)
        z = sb("z", [PAIR, TILES, F])
        y = sb("y", [PAIR, TILES, F])
        stats = sb("stats", [PAIR, TILES, 6])
        mv = sb("mv", [PAIR, TILES, 2])

        loaded, y2_loaded, res_loaded, half_set = sem("loaded"), sem("y2_loaded"), sem("res_loaded"), sem("half_set")
        owner_loaded, owner_set = sem("owner_loaded"), sem("owner_set")
        w_loaded = [sem(f"w_loaded{k}") for k in range(W_SLOTS)]
        w_hi_done, w_split = sem("w_hi_done"), sem("w_split")
        y2_turned, y2T_done, route_done = sem("y2_turned"), sem("y2T_done"), sem("route_done")
        y2T_hi_done, y2T_lo_done = sem("y2T_hi_done"), sem("y2T_lo_done")
        route_chain, ex_done, combine_done = sem("route_chain"), sem("ex_done"), sem("combine_done")
        comb_turned, combT_done = sem("comb_turned"), sem("combT_done")
        gate_done, up_done, comb_done = sem("gate_done"), sem("up_done"), sem("comb_done")
        silu_done, gu_done, h_done = sem("silu_done"), sem("gu_done"), sem("h_done")
        h_hi_done, h_lo_done, down_done, z_done = sem("h_hi_done"), sem("h_lo_done"), sem("down_done"), sem("z_done")
        stat_chain, var_done, rstd_done = sem("stat_chain"), sem("var_done"), sem("rstd_done")
        y_done, y_stored = sem("y_done"), sem("y_stored")
        LOADS = 4
        LOGITS = 4
        CHAIN = LOGITS + 21
        TURN_AT, ROUTE_AT, LOGITS_AT, EXP_AT, PICK_AT, WEIGHTS_AT = (5, 6), 8, 9, 10, (11, 12), 13

        def rows_of(c):
            return min(128, IW - 128 * c)

        def last_use(i, c, deep, first):
            if c >= deep:
                return IC * i + c - deep + 1
            if first:
                return None
            return IC * (i - 1) + max(k for k in range(IC) if k % deep == c) + 1

        def w_parts(c):
            m = rows_of(c)
            if m == 128:
                return [(slice(0, 128), slice(0, W_IN + 2), slice(0, 128))]
            return [(slice(0, 128), slice(0, W_IN), slice(0, m)), (slice(0, m), slice(W_IN, W_IN + 2), slice(0, 128))]

        W_PARTS = [sum(len(w_parts(k)) for k in range(c + 1)) for c in range(IC)]

        def every_block(engine, body):
            body(0, True, False)
            with engine.Fori(1, NBLK - 1) as i:
                body(i, False, False)
            body(NBLK - 1, False, True)

        block = ctx.enter_context(nc.Block())

        @block.sync
        def _(sp):
            sp.dma_start(y2[:], D["y2"][:, 0:TILES, :]).then_inc(y2_loaded, 16)
            sp.dma_start(ident[:], D["ident"]).then_inc(loaded, 16)
            sp.dma_start(w_route[:, :, 0:EXPERTS], D["route_w"]).then_inc(loaded, 16)
            sp.dma_start(w_route[:, :, EXPERTS:NR], D["route_sh"], allow_slow_non_contiguous=True).then_inc(loaded, 16)
            sp.dma_start(rank[:], D["rank"]).then_inc(loaded, 16)

            def load_next(i, first, last):
                if not last:
                    sp.wait_ge(y2_turned, KC * (i + 1))
                    sp.dma_start(y2[:], D["y2"][:, bass.ts(i + 1, TILES), :]).then_inc(y2_loaded, 16)
                if not first:
                    sp.wait_ge(z_done, TILES * i)
                sp.dma_start(y2_res[:], D["y2"][:, bass.ts(i, TILES), :]).then_inc(res_loaded, 16)

            for c in range(IC):
                m = rows_of(c)
                if c >= W_SLOTS:
                    sp.wait_ge(w_split, W_PARTS[c - W_SLOTS])
                sp.dma_start(w_in[:, c % W_SLOTS, 0:W_IN, 0:m], D["hidden"][:, :, 128 * c:128 * c + m]).then_inc(w_loaded[c % W_SLOTS], 16)
                sp.dma_start(w_in[0:m, c % W_SLOTS, W_IN:, :].rearrange("p a n -> p (a n)"),
                             D["down"][128 * c:128 * c + m]).then_inc(w_loaded[c % W_SLOTS], 16)
                if c == 2:
                    load_next(0, True, False)
                if c == 0:
                    sp.dma_start(owner_in[:], D["owner"]).then_inc(owner_loaded, 16)

            def block_io(i, first, last):
                if not first:
                    load_next(i, first, last)
                for t in range(TILES):
                    sp.wait_ge(y_done, TILES * i + t + 1)
                    sp.dma_start(D["out"][:, bass.ds(i * TILES + t, 1), :], y[:, t:t + 1]).then_inc(y_stored, 16)

            every_block(sp, block_io)
            sp.wait_ge(y_stored, 16 * NPAIR)

        @block.tensor
        def _(pe):
            pe.wait_ge(loaded, 16 * LOADS)

            def turn_y2(i, kc, first=False):
                if kc == 0:
                    pe.wait_ge(y2_loaded, 16 * (i + 1))
                    if not first:
                        pe.wait_ge(combT_done, i)
                else:
                    pe.wait_ge(y2T_done, KC * i + kc)
                for t in range(TILES):
                    mm = pe.transpose(misc_bank[:, t * PAIR:(t + 1) * PAIR], y2[:, t, kc * 128:(kc + 1) * 128],
                                      ident[0:PAIR, 0:PAIR])
                mm.then_inc(y2_turned, 1)

            def route(i):
                pe.wait_ge(y2T_done, KC * (i + 1))
                for t in range(TILES):
                    for kc in range(KC):
                        mm = pe.matmul(misc_bank[0:PAIR, t * NR:(t + 1) * NR], y2T[:, kc, t * PAIR:(t + 1) * PAIR],
                                       w_route[:, kc, :], start=(kc == 0), stop=(kc == KC - 1))
                mm.then_inc(route_done, 1)

            def turn_combine(i):
                pe.wait_ge(combine_done, i + 1)
                for t in range(TILES):
                    mm = pe.transpose(misc_bank[0:2 * NR, t * PAIR:(t + 1) * PAIR], combine_parts[:, t, :],
                                      ident[0:PAIR, 0:PAIR])
                mm.then_inc(comb_turned, 1)

            def hidden(i, c, first):
                m = rows_of(c)
                if first:
                    pe.wait_ge(w_split, W_PARTS[c])
                for j, (bank, free, done) in enumerate(((gate_bank[c % 2], silu_done, gate_done),
                                                        (up_bank[c % 2], gu_done, up_done))):
                    if (used := last_use(i, c, 2, first)) is not None:
                        pe.wait_ge(free, used)
                    for kc in range(KC):
                        if c == 0 and j == 0:
                            pe.wait_ge(y2T_lo_done, KC * i + kc + 1)
                        w = KC * j + kc
                        terms = ((w_hi, y2T_hi), (w_lo, y2T_hi), (w_hi, y2T_lo))
                        for n, (a, b) in enumerate(terms):
                            mm = pe.matmul(bank[0:m, 0:BLK], a[:, c, w, 0:m], b[:, kc, :],
                                           start=(kc == 0 and n == 0), stop=(kc == KC - 1 and n == len(terms) - 1))
                    mm.then_inc(done, 1)

            def spread_combine(i, c, first):
                m = rows_of(c)
                if c == 0:
                    pe.wait_ge(owner_set, 1)
                    pe.wait_ge(combT_done, i + 1)
                if not (first and c == 0):
                    pe.wait_ge(h_done, IC * i + c)
                pe.matmul(comb_bank[0:m, 0:BLK], owner[:, 128 * c:128 * c + m], combT[:], start=True,
                          stop=True).then_inc(comb_done, 1)

            def down(i, c, first):
                m = rows_of(c)
                if c == 0 and not first:
                    pe.wait_ge(z_done, TILES * i)
                pe.wait_ge(h_lo_done, IC * i + c + 1)
                for t in range(TILES):
                    terms = ((h_hi, w_hi), (h_hi, w_lo), (h_lo, w_hi))
                    for n, (a, b) in enumerate(terms):
                        mm = pe.matmul(down_bank[t // 2][0:PAIR, (t % 2) * F:(t % 2 + 1) * F],
                                       a[0:m, c % H_DEEP, t * PAIR:(t + 1) * PAIR], b[0:m, c, W_IN:, :],
                                       start=(c == 0 and t % 2 == 0 and n == 0),
                                       stop=(c == IC - 1 and t % 2 == 1 and n == len(terms) - 1), skip_group_check=True)
                mm.then_inc(down_done, 1)

            def block_pe(i, first, last):
                if not first:
                    turn_combine(i)
                for s in range(IC + 2):
                    if (2 if first else 1) <= s <= IC:
                        spread_combine(i, s - 1, first)
                    if s < IC:
                        hidden(i, s, first)
                    if first and s == 1:
                        turn_combine(i)
                        spread_combine(i, 0, first)
                    if s >= 2:
                        down(i, s - 2, first)
                    if not last:
                        if s in TURN_AT:
                            turn_y2(i + 1, TURN_AT.index(s))
                        if s == ROUTE_AT:
                            route(i + 1)

            for kc in range(KC):
                turn_y2(0, kc, first=True)
            route(0)
            every_block(pe, block_pe)

        @block.scalar
        def _(act):
            def copy_y2T(i, kc, first=False):
                if kc == 0 and not first:
                    act.wait_ge(y2T_lo_done, KC * i)
                act.wait_ge(y2_turned, KC * i + kc + 1)
                act.copy(y2T[:, kc, :], misc_bank[:, 0:BLK]).then_inc(y2T_done, 1)

            def round_y2T(i, first=False):
                act.wait_ge(y2T_done, KC * (i + 1))
                if not first:
                    act.wait_ge(up_done, IC * i)
                for kc in range(KC):
                    act.copy(y2T_hi[:, kc, :], y2T[:, kc, :]).then_inc(y2T_hi_done, 1)

            def router_exp(i):
                act.wait_ge(route_chain, CHAIN * i + LOGITS)
                act.activation(ex[:], logit[:], ACT.Exp).then_inc(ex_done, 1)

            def copy_combT(i):
                act.wait_ge(comb_turned, i + 1)
                act.copy(combT[:], misc_bank[0:2 * NR, 0:BLK]).then_inc(combT_done, 1)

            def silu(i, c, first):
                m = rows_of(c)
                if (used := last_use(i, c, 2, first)) is not None:
                    act.wait_ge(gu_done, used)
                act.wait_ge(gate_done, IC * i + c + 1)
                act.activation(act_g[0:m, c % 2, :], gate_bank[c % 2][0:m, 0:BLK], ACT.Silu).then_inc(silu_done, 1)

            def round_h(i, c, first):
                m = rows_of(c)
                if (used := last_use(i, c, H_DEEP, first)) is not None:
                    act.wait_ge(down_done, used)
                act.wait_ge(h_done, IC * i + c + 1)
                act.copy(h_hi[0:m, c % H_DEEP, :], h[0:m, c % 2, :]).then_inc(h_hi_done, 1)

            def block_act(i, first, last):
                if not first:
                    copy_combT(i)
                for s in range(IC + 1):
                    if s < IC:
                        silu(i, s, first)
                    if first and s == 1:
                        copy_combT(i)
                    if s == IC and not last:
                        round_y2T(i + 1)
                    if s >= 1:
                        round_h(i, s - 1, first)
                    if not last:
                        if s in TURN_AT:
                            copy_y2T(i + 1, TURN_AT.index(s))
                        if s == EXP_AT:
                            router_exp(i + 1)

            for kc in range(KC):
                copy_y2T(0, kc, first=True)
            round_y2T(0, first=True)
            router_exp(0)
            act.wait_ge(owner_loaded, 16)
            act.copy(owner[:], owner_in[:]).then_inc(owner_set, 1)
            every_block(act, block_act)

        @block.vector
        def _(dve):
            dve.memset(half[:], -0.5).then_inc(half_set, 1)
            dve.wait_ge(loaded, 16 * LOADS)

            def wide(ap):
                return ap.unsqueeze(2).to_broadcast([PAIR, TILES, EXPERTS])

            logits, exps = logit[:, :, 0:EXPERTS], ex[:, :, 0:EXPERTS]

            def chain(i, done):
                def link(ins):
                    nonlocal done
                    done += 1
                    ins.then_inc(route_chain, 1)
                    dve.wait_ge(route_chain, CHAIN * i + done)
                return link

            def shifted_logits(i):
                link = chain(i, 0)
                dve.wait_ge(route_done, i + 1)
                link(dve.tensor_copy(logit[:], misc_bank[0:PAIR, 0:TILES * NR].rearrange("p (t n) -> p t n", t=TILES)))
                link(dve.tensor_reduce(best[:, 0, :], logits, AX.X, ALU.max))
                link(dve.tensor_scalar(logit[:, :, EXPERTS:NR], logit[:, :, EXPERTS:NR], -1.0, None, ALU.mult))
                link(dve.tensor_tensor(logits, logits, wide(best[:, 0, :]), ALU.subtract))

            def pick_largest(i, k):
                link = chain(i, LOGITS + 7 * k)
                if k == 0:
                    dve.wait_ge(ex_done, i + 1)
                src = exps if k == 0 else rest[:]
                link(dve.tensor_reduce(best[:, k, :], src, AX.X, ALU.max))
                link(dve.tensor_tensor(pick[:, k], src, wide(best[:, k, :]), ALU.is_equal))
                link(dve.tensor_tensor(pick[:, k], pick[:, k], rank[:], ALU.mult))
                link(dve.tensor_reduce(first_of[:], pick[:, k], AX.X, ALU.max))
                link(dve.tensor_tensor(pick[:, k], rank[:], wide(first_of[:]), ALU.is_equal))
                if k == 0:
                    link(dve.tensor_scalar(rest[:], pick[:, 0], -2.0, None, ALU.mult))
                    link(dve.tensor_tensor(rest[:], rest[:], exps, ALU.add))

            def combine_weights(i, first=False):
                link = chain(i, LOGITS + 12)
                link(dve.tensor_tensor(pick[:, 0], pick[:, 0], pick[:, 1], ALU.add))
                link(dve.tensor_tensor(pick[:, 0], pick[:, 0], exps, ALU.mult))
                link(dve.tensor_reduce(total[:], pick[:, 0], AX.X, ALU.add))
                link(dve.reciprocal(total[:], total[:]))
                link(dve.tensor_scalar(ex[:, :, EXPERTS:NR], ex[:, :, EXPERTS:NR], 1.0, None, ALU.add))
                link(dve.reciprocal(combine[:, :, EXPERTS:NR], ex[:, :, EXPERTS:NR]))
                link(dve.tensor_tensor(combine[:, :, 0:EXPERTS], pick[:, 0], wide(total[:]), ALU.mult))
                link(dve.tensor_copy(combine_r[:], combine[:]))
                if not first:
                    dve.wait_ge(comb_turned, i)
                link(dve.tensor_copy(combine_parts[:, :, 0:NR], combine_r[:].bitcast(F32)))
                dve.tensor_tensor(combine_parts[:, :, NR:], combine[:], combine_r[:].bitcast(F32),
                                  ALU.subtract).then_inc(combine_done, 1)

            def gated(i, c):
                m, k = rows_of(c), c % 2
                dve.wait_ge(silu_done, IC * i + c + 1)
                dve.wait_ge(up_done, IC * i + c + 1)
                dve.tensor_tensor(act_gu[0:m, k, :], up_bank[k][0:m, 0:BLK], act_g[0:m, k, :], ALU.mult).then_inc(gu_done, 1)

            def weighed(i, c):
                m, k = rows_of(c), c % 2
                dve.wait_ge(gu_done, IC * i + c + 1)
                dve.wait_ge(comb_done, IC * i + c + 1)
                dve.tensor_tensor(h[0:m, k, :], comb_bank[0:m, 0:BLK], act_gu[0:m, k, :], ALU.mult).then_inc(h_done, 1)

            def h_rest(i, c):
                m = rows_of(c)
                dve.wait_ge(h_hi_done, IC * i + c + 1)
                dve.tensor_tensor(h_lo[0:m, c % H_DEEP, :], h[0:m, c % 2, :], h_hi[0:m, c % H_DEEP, :].bitcast(F32),
                                  ALU.subtract).then_inc(h_lo_done, 1)

            def norm(i, first):
                dve.wait_ge(down_done, IC * (i + 1))
                dve.wait_ge(res_loaded, 16 * (i + 1))
                for t in range(TILES):
                    dve.tensor_tensor(z[:, t, :], down_bank[t // 2][0:PAIR, (t % 2) * F:(t % 2 + 1) * F], y2_res[:, t, :],
                                      ALU.add).then_inc(z_done, 1)
                for t in range(TILES):
                    n = TILES * i + t
                    dve.wait_ge(z_done, n + 1)
                    norm_stats(dve, z[:, t, :], stats[:, t, :], mv[:, t, :], stat_chain, 2 * n, (loaded, 16)).then_inc(var_done, 1)
                for t in range(TILES):
                    n = TILES * i + t
                    dve.wait_ge(rstd_done, n + 1)
                    if not first:
                        dve.wait_ge(y_stored, 16 * (n - TILES + 1))
                    dve.tensor_scalar(y[:, t, :], z[:, t, :], mv[:, t, 0:1], mv[:, t, 1:2],
                                      ALU.subtract, ALU.mult).then_inc(y_done, 1)

            def block_dve(i, first, last):
                for s in range(IC + 2):
                    if s >= 2:
                        h_rest(i, s - 2)
                    if (2 if first else 1) <= s <= IC:
                        weighed(i, s - 1)
                    if s < IC:
                        gated(i, s)
                    if first and s == 1:
                        weighed(i, 0)
                    if not last:
                        if s == LOGITS_AT:
                            shifted_logits(i + 1)
                        if s in PICK_AT:
                            pick_largest(i + 1, PICK_AT.index(s))
                        if s == WEIGHTS_AT:
                            combine_weights(i + 1)
                norm(i, first)

            shifted_logits(0)
            for k in range(2):
                pick_largest(0, k)
            combine_weights(0, first=True)
            every_block(dve, block_dve)

        @block.gpsimd
        def _(pool):
            pool.wait_ge(half_set, 1)

            def y2T_rest(i):
                for kc in range(KC):
                    pool.wait_ge(y2T_hi_done, KC * i + kc + 1)
                    pool.tensor_tensor(y2T_lo[:, kc, :], y2T[:, kc, :], y2T_hi[:, kc, :].bitcast(F32),
                                       ALU.subtract).then_inc(y2T_lo_done, 1)

            def split_weights(c):
                pool.wait_ge(w_loaded[c % W_SLOTS], 32 * (c // W_SLOTS + 1))
                parts = w_parts(c)
                for n, (rows, blocks, cols) in enumerate(parts):
                    src, hi, lo = w_in[rows, c % W_SLOTS, blocks, cols], w_hi[rows, c, blocks, cols], w_lo[rows, c, blocks, cols]
                    pool.tensor_scalar(hi, src, 1.0, 0.0, ALU.mult, ALU.add).then_inc(w_hi_done, 1)
                    pool.wait_ge(w_hi_done, W_PARTS[c] - len(parts) + n + 1)
                    pool.tensor_tensor(lo, src, hi.bitcast(F32), ALU.subtract).then_inc(w_split, 1)

            def block_pool(i, first, last):
                if not last:
                    y2T_rest(i + 1)
                for t in range(TILES):
                    pool.wait_ge(var_done, TILES * i + t + 1)
                    pool.tensor_tensor(mv[:, t, 1:2], mv[:, t, 1:2], half[:], ALU.pow).then_inc(rstd_done, 1)

            y2T_rest(0)
            for c in range(IC):
                split_weights(c)
            every_block(pool, block_pool)


def decoder_layer(nc, D):
    with ExitStack() as ctx:
        M_hi = ctx.enter_context(nc.sbuf_tensor("M_hi", [128, XH, F], F32R))
        M_lo = ctx.enter_context(nc.sbuf_tensor("M_lo", [128, XH, F], F32R))
        phase_a(nc, D, M_hi, M_lo)
        phase_b(nc, D, M_hi, M_lo)
    phase_c(nc, D)


def layouts(x, ctx_1024, mask_BxS2_bf1, L0_attn_Wq, L0_attn_bq, L0_attn_Wk, L0_attn_bk, L0_attn_Wv, L0_attn_bv,
            L0_attn_Wo, L0_attn_bo, L0_xattn_Wq, L0_xattn_Wk, L0_xattn_Wv, L0_xattn_Wo, L0_ffn_router_weight,
            L0_ffn_gate_up_proj, L0_ffn_down_proj, L0_ffn_sh_gate_w, L0_ffn_sh_up_w, L0_ffn_sh_down_w,
            L0_ffn_shared_gate_w):
    def rows(w):
        return w.reshape(KC, 128, -1).transpose(1, 0, 2)

    tokens = x.reshape(NPAIR, PAIR, F)
    moe = L0_ffn_gate_up_proj.reshape(EXPERTS, 2, I_MOE, F)
    gate = np.concatenate([moe[:, 0].reshape(-1, F), L0_ffn_sh_gate_w])
    up = np.concatenate([moe[:, 1].reshape(-1, F), L0_ffn_sh_up_w])
    return {
        "x": tokens.transpose(1, 0, 2),
        "xT": rows(x.reshape(B * S, F).T),
        "ctx": ctx_1024.reshape(B, CK, CH * CD),
        "ctxT": ctx_1024.reshape(B, CK, CH, CD).transpose(0, 3, 2, 1).reshape(B, CD, CTX),
        "mask": mask_BxS2_bf1.view(np.uint8).reshape(B, CK, CH).transpose(0, 2, 1).reshape(B, CTX),
        "wq": rows(L0_attn_Wq), "wk": rows(L0_attn_Wk), "wv": rows(L0_attn_Wv), "wo": rows(L0_attn_Wo),
        "bq": L0_attn_bq.reshape(KC, 128).T, "bk": L0_attn_bk.reshape(KC, 128).T,
        "bv": L0_attn_bv, "bo": L0_attn_bo,
        "xwqT": L0_xattn_Wq.reshape(F, XH, 128).transpose(2, 1, 0),
        "xwkT": L0_xattn_Wk.reshape(CD, XKV, 128).transpose(2, 1, 0),
        "xwvT": L0_xattn_Wv.reshape(CD, XKV, 128).transpose(2, 1, 0),
        "xwo": L0_xattn_Wo.reshape(XH, 128, F).transpose(1, 0, 2),
        "hidden": np.concatenate([rows(gate.T), rows(up.T)], axis=1),
        "down": np.concatenate([L0_ffn_down_proj.transpose(0, 2, 1).reshape(-1, F), L0_ffn_sh_down_w.T]),
        "route_w": rows(L0_ffn_router_weight.T), "route_sh": rows(L0_ffn_shared_gate_w.T),
    }


def constants():
    f = np.float32
    own_q = np.zeros((2, PAIR), f)
    own_q[0, :S] = own_q[1, S:] = 1
    other_k = np.zeros((2, SA_HEADS, PAIR), f)
    other_k[0, :, S:] = other_k[1, :, :S] = -BIG
    owner = np.zeros((2, NR, IW), f)
    for n in range(IW):
        owner[:, min(n // I_MOE, EXPERTS), n] = 1
    own_unit = {}
    for k, units in enumerate(UNITS):
        own_unit[f"own_unit{k}"] = np.zeros((2 * units, units, 128), f)
        for r in range(2 * units):
            own_unit[f"own_unit{k}"][r, r % units] = 1
    rank = np.broadcast_to(np.arange(EXPERTS, 0, -1, dtype=f), (PAIR, TILES, EXPERTS))
    return {"ident": np.eye(128, dtype=f), "own_q": own_q, "other_k": other_k.reshape(2, -1),
            **own_unit, "owner": owner.reshape(2 * NR, IW), "rank": rank}


def kernel(**inputs):
    import concourse.bacc as bacc
    from concourse.bass_utils import run_bass_kernel_spmd

    nc = bacc.Bacc("TRN2", target_bir_lowering=False, num_devices=1)
    arrays, D = {}, {}
    for name, a in {**layouts(**{k: np.asarray(v) for k, v in inputs.items()}), **constants()}.items():
        a = np.ascontiguousarray(a)
        arrays["in_" + name] = a
        D[name] = nc.dram_tensor("in_" + name, a.shape, mybir.dt.from_np(a.dtype), kind="ExternalInput").ap()
    D["y1"] = nc.dram_tensor("y1_store", (PAIR, NPAIR, F), F32, kind="Internal").ap()
    D["q"] = nc.dram_tensor("q_store", (128, B, ROWS), F32, kind="Internal").ap()
    D["y2"] = nc.dram_tensor("y2_store", (PAIR, NPAIR, F), F32, kind="Internal").ap()
    D["out"] = nc.dram_tensor("out", (PAIR, NPAIR, F), F32, kind="ExternalOutput").ap()
    decoder_layer(nc, D)
    r = run_bass_kernel_spmd(nc, [arrays], core_ids=[0])
    return r.results[0]["out"].transpose(1, 0, 2).reshape(B, S, F)
```
